# Optimizing a Trainium2 kernel written in Bass

```python
import numpy as np
import jax
import jax.numpy as jnp

def _softmax(x, axis=-1):
    return jax.nn.softmax(x, axis=axis)

def _gelu(x):
    return jax.nn.gelu(x, approximate=True)

def _silu(x):
    return jax.nn.silu(x)

def _sigmoid(x):
    return jax.nn.sigmoid(x)

def _layernorm(x, axis=-1, eps=1e-05):
    m = jnp.mean(x, axis=axis, keepdims=True)
    v = jnp.var(x, axis=axis, keepdims=True)
    return (x - m) / jnp.sqrt(v + eps)

def _scatter_add(tgt, idx, src, axis=0):
    return tgt.at[idx].add(src)

def _segment_sum(src, seg, n):
    return jax.ops.segment_sum(src, seg, n)
kernel_name = 'mk_gnn_resnorm_d4_gnn_r32_6e6a53'

def setup_inputs(seed: int=0):
    np.random.seed(seed)
    _w = jnp.asarray

    def _rec_inputs():
        import jax
        import jax.numpy as jnp
        _gk = jax.random.key(seed)
        x = -0.0009044 + 1 * jax.random.normal(jax.random.fold_in(_gk, 1), (3125, 16), jnp.float32)
        _s = jax.random.randint(jax.random.fold_in(_gk, 2), (50000,), 0, 3125, jnp.int32)
        _d = jax.random.randint(jax.random.fold_in(_gk, 3), (50000,), 0, 3125, jnp.int32)
        _loop = jnp.arange(3125, dtype=jnp.int32)
        src = jnp.concatenate([_s, _d, _loop])
        dst = jnp.concatenate([_d, _s, _loop])
        _o = jnp.argsort(dst, stable=True)
        src = src[_o]
        dst = dst[_o]
        edge_attr_16 = 0.000189758 + 1.00013 * jax.random.normal(jax.random.fold_in(_gk, 13), (103125, 16), jnp.float32)
        edge_attr_8 = -5.3897e-05 + 0.999841 * jax.random.normal(jax.random.fold_in(_gk, 14), (103125, 8), jnp.float32)
        edge_type_230 = jax.random.randint(jax.random.fold_in(_gk, 16), (103125,), 0, 230, jnp.int32)
        edge_type_8 = jax.random.randint(jax.random.fold_in(_gk, 17), (103125,), 0, 8, jnp.int32)
        node_vec1 = -0.00472126 + 0.997171 * jax.random.normal(jax.random.fold_in(_gk, 18), (3125, 1), jnp.float32)
        return (x, src, dst, edge_attr_16, edge_attr_8, edge_type_230, edge_type_8, node_vec1)
    x, src, dst, edge_attr_16, edge_attr_8, edge_type_230, edge_type_8, node_vec1 = _rec_inputs()

    def _L0_gnn_setup():
        import jax, jax.numpy as jnp
        import numpy as np
        N_NODES = 3125
        N_EDGES = 100000
        D_FEAT = 16
        key = jax.random.key(seed)
        k1, k2, k3 = jax.random.split(key, 3)
        x = jax.random.normal(k1, (N_NODES, D_FEAT), dtype=jnp.float32)
        edge_index = jax.random.randint(k2, (2, N_EDGES), 0, N_NODES, dtype=jnp.int64)
        edge_attr = jax.random.normal(k3, (N_EDGES, D_FEAT), dtype=jnp.float32)
        return {'x': x, 'edge_index': edge_index, 'edge_attr': edge_attr}
    _L0_gnn_all = _L0_gnn_setup()
    _L0_gnn_in = {k: v for k, v in _L0_gnn_all.items() if k in ()}
    del _L0_gnn_all

    def _L1_gnn_setup():
        import jax, jax.numpy as jnp
        import numpy as np
        N_NODES = 3125
        N_EDGES = 100000
        NUM_REL = 8

        def _rgcn_layer(x, src, dst, edge_type, W, root, bias):
            out = x @ root + bias
            x_src = x[src]
            for r in range(W.shape[0]):
                mask = (edge_type == r).astype(x.dtype)
                s = jax.ops.segment_sum(x_src * mask[:, None], dst, num_segments=x.shape[0])
                cnt = jax.ops.segment_sum(mask, dst, num_segments=x.shape[0])
                agg = s / jnp.clip(cnt, 1.0)[:, None]
                out = out + agg @ W[r]
            return out
        key = jax.random.key(seed)
        ks = jax.random.split(key, 9)
        x = jax.random.normal(ks[0], (N_NODES, 16), dtype=jnp.float32)
        edge_index = jax.random.randint(ks[1], (2, N_EDGES), 0, N_NODES, dtype=jnp.int32)
        edge_type = jax.random.randint(ks[2], (N_EDGES,), 0, NUM_REL, dtype=jnp.int32)
        s1 = 1.0 / np.sqrt(16.0)
        s2 = 1.0 / np.sqrt(32.0)
        W1 = jax.random.normal(ks[3], (NUM_REL, 16, 32), dtype=jnp.float32) * s1
        root1 = jax.random.normal(ks[4], (16, 32), dtype=jnp.float32) * s1
        b1 = jnp.zeros((32,), dtype=jnp.float32)
        W2 = jax.random.normal(ks[5], (NUM_REL, 32, 16), dtype=jnp.float32) * s2
        root2 = jax.random.normal(ks[6], (32, 16), dtype=jnp.float32) * s2
        b2 = jnp.zeros((16,), dtype=jnp.float32)
        return {'x': x, 'edge_index': edge_index, 'edge_type': edge_type, 'W1': W1, 'root1': root1, 'b1': b1, 'W2': W2, 'root2': root2, 'b2': b2}
    _L1_gnn_all = _L1_gnn_setup()
    _L1_gnn_in = {k: v for k, v in _L1_gnn_all.items() if k in ('W1', 'root1', 'b1', 'W2', 'root2', 'b2')}
    del _L1_gnn_all

    def _L2_gnn_setup():
        import jax, jax.numpy as jnp
        import numpy as np
        C = 0.01
        EPS = 1e-06
        MIN_NORM = 1e-10
        BALL_EPS = 1e-05

        def _norm(x):
            return jnp.sqrt(jnp.clip(jnp.sum(x * x, axis=-1, keepdims=True), MIN_NORM))

        def log_map_zero(x, c):
            sc = jnp.sqrt(c)
            n = _norm(x)
            return jnp.arctanh(jnp.clip(sc * n, -1.0 + BALL_EPS, 1.0 - BALL_EPS)) * x / (sc * n)

        def exp_map_zero(v, c):
            sc = jnp.sqrt(c)
            n = _norm(v)
            return jnp.tanh(sc * n) * v / (sc * n)

        def project_to_ball(x, c):
            n = _norm(x)
            maxn = (1.0 - BALL_EPS) / jnp.sqrt(c)
            return jnp.where(n > maxn, x * (maxn / n), x)

        def mobius_add(x, y, c):
            x2 = jnp.sum(x * x, axis=-1, keepdims=True)
            y2 = jnp.sum(y * y, axis=-1, keepdims=True)
            xy = jnp.sum(x * y, axis=-1, keepdims=True)
            num = (1.0 + 2.0 * c * xy + c * y2) * x + (1.0 - c * x2) * y
            den = 1.0 + 2.0 * c * xy + c * c * x2 * y2
            return num / jnp.clip(den, MIN_NORM)
        N, E, R, D = (50000, 12500, 230, 16)
        key = jax.random.key(seed)
        ks = jax.random.split(key, 8)
        h_hyper = project_to_ball(0.1 * jax.random.normal(ks[0], (N, D), dtype=jnp.float32), C)
        node_norm = jax.random.uniform(ks[1], (N, 1), dtype=jnp.float32)
        xav = float(np.sqrt(2.0 / (D + D)))
        rel_weight = xav * jax.random.normal(ks[2], (R, D, D), dtype=jnp.float32)
        loop_weight = xav * jax.random.normal(ks[3], (D, D), dtype=jnp.float32)
        rel_emb = 0.1 * jax.random.normal(ks[4], (R, D), dtype=jnp.float32)
        src = jax.random.randint(ks[5], (E,), 0, N, dtype=jnp.int32)
        dst = jax.random.randint(ks[6], (E,), 0, N, dtype=jnp.int32)
        etype = jax.random.randint(ks[7], (E,), 0, R, dtype=jnp.int32)
        return {'h_hyper': h_hyper, 'node_norm': node_norm, 'rel_weight': rel_weight, 'loop_weight': loop_weight, 'rel_emb': rel_emb, 'src': src, 'dst': dst, 'etype': etype}
    _L2_gnn_all = _L2_gnn_setup()
    _L2_gnn_in = {k: v for k, v in _L2_gnn_all.items() if k in ('rel_weight', 'loop_weight', 'rel_emb')}
    del _L2_gnn_all

    def _L3_gnn_setup():
        import jax, jax.numpy as jnp
        import numpy as np
        N_NODES = 3125
        N_EDGES = 100000
        D_NODE = 16
        D_EDGE = 8
        D_HIDDEN = 16
        key = jax.random.key(seed)
        ks = jax.random.split(key, 8)
        node_features = jax.random.normal(ks[0], (N_NODES, D_NODE), dtype=jnp.float32)
        edge_attr_e3nn = jax.random.normal(ks[1], (N_EDGES, D_EDGE), dtype=jnp.float32)
        node_attr_scalar_raw = jax.random.normal(ks[2], (N_NODES, 1), dtype=jnp.float32)
        W_msg_tp = jax.random.normal(ks[3], (D_NODE, D_EDGE, D_HIDDEN), dtype=jnp.float32)
        W_msg_lin = jax.random.normal(ks[4], (D_HIDDEN, D_HIDDEN), dtype=jnp.float32)
        W_upd_tp = jax.random.normal(ks[5], (D_NODE, D_HIDDEN, D_HIDDEN), dtype=jnp.float32)
        W_upd_lin = jax.random.normal(ks[6], (D_HIDDEN, D_NODE), dtype=jnp.float32)
        edge_index = jax.random.randint(ks[7], (2, N_EDGES), 0, N_NODES, dtype=jnp.int64)
        return {'node_features': node_features, 'edge_attr_e3nn': edge_attr_e3nn, 'node_attr_scalar_raw': node_attr_scalar_raw, 'W_msg_tp': W_msg_tp, 'W_msg_lin': W_msg_lin, 'W_upd_tp': W_upd_tp, 'W_upd_lin': W_upd_lin, 'edge_index': edge_index}
    _L3_gnn_all = _L3_gnn_setup()
    _L3_gnn_in = {k: v for k, v in _L3_gnn_all.items() if k in ('W_msg_tp', 'W_msg_lin', 'W_upd_tp', 'W_upd_lin')}
    del _L3_gnn_all
    return {'x': x, 'src': src, 'dst': dst, 'edge_attr_16': edge_attr_16, 'edge_attr_8': edge_attr_8, 'edge_type_230': edge_type_230, 'edge_type_8': edge_type_8, 'node_vec1': node_vec1, 'L1_gnn_W1': _L1_gnn_in['W1'], 'L1_gnn_root1': _L1_gnn_in['root1'], 'L1_gnn_b1': _L1_gnn_in['b1'], 'L1_gnn_W2': _L1_gnn_in['W2'], 'L1_gnn_root2': _L1_gnn_in['root2'], 'L1_gnn_b2': _L1_gnn_in['b2'], 'L2_gnn_rel_weight': _L2_gnn_in['rel_weight'], 'L2_gnn_loop_weight': _L2_gnn_in['loop_weight'], 'L2_gnn_rel_emb': _L2_gnn_in['rel_emb'], 'L3_gnn_W_msg_tp': _L3_gnn_in['W_msg_tp'], 'L3_gnn_W_msg_lin': _L3_gnn_in['W_msg_lin'], 'L3_gnn_W_upd_tp': _L3_gnn_in['W_upd_tp'], 'L3_gnn_W_upd_lin': _L3_gnn_in['W_upd_lin']}

def reference(x, src, dst, edge_attr_16, edge_attr_8, edge_type_230, edge_type_8, node_vec1, L1_gnn_W1, L1_gnn_root1, L1_gnn_b1, L1_gnn_W2, L1_gnn_root2, L1_gnn_b2, L2_gnn_rel_weight, L2_gnn_loop_weight, L2_gnn_rel_emb, L3_gnn_W_msg_tp, L3_gnn_W_msg_lin, L3_gnn_W_upd_tp, L3_gnn_W_upd_lin):
    import jax
    import jax.numpy as jnp

    def _L0_gnn_ref(x, edge_index, edge_attr):
        import jax, jax.numpy as jnp
        import numpy as np
        N_NODES = 3125
        N_EDGES = 100000
        D_FEAT = 16
        nb_node = x.shape[0]
        dst = edge_index[1]
        sums = jax.ops.segment_sum(edge_attr, dst, num_segments=nb_node)
        counts = jax.ops.segment_sum(jnp.ones((edge_attr.shape[0],), dtype=edge_attr.dtype), dst, num_segments=nb_node)
        denom = jnp.where(counts > 0, counts, jnp.ones_like(counts))
        return sums / denom[:, None]

    def _L1_gnn_ref(x, edge_index, edge_type, W1, root1, b1, W2, root2, b2):
        import jax, jax.numpy as jnp
        import numpy as np
        N_NODES = 3125
        N_EDGES = 100000
        NUM_REL = 8

        def _rgcn_layer(x, src, dst, edge_type, W, root, bias):
            out = x @ root + bias
            x_src = x[src]
            for r in range(W.shape[0]):
                mask = (edge_type == r).astype(x.dtype)
                s = jax.ops.segment_sum(x_src * mask[:, None], dst, num_segments=x.shape[0])
                cnt = jax.ops.segment_sum(mask, dst, num_segments=x.shape[0])
                agg = s / jnp.clip(cnt, 1.0)[:, None]
                out = out + agg @ W[r]
            return out
        src, dst = (edge_index[0], edge_index[1])
        h = _rgcn_layer(x, src, dst, edge_type, W1, root1, b1)
        h = jax.nn.relu(h)
        h = _rgcn_layer(h, src, dst, edge_type, W2, root2, b2)
        return h

    def _L2_gnn_ref(h_hyper, node_norm, rel_weight, loop_weight, rel_emb, src, dst, etype):
        import jax, jax.numpy as jnp
        import numpy as np
        C = 0.01
        EPS = 1e-06
        MIN_NORM = 1e-10
        BALL_EPS = 1e-05

        def _norm(x):
            return jnp.sqrt(jnp.clip(jnp.sum(x * x, axis=-1, keepdims=True), MIN_NORM))

        def log_map_zero(x, c):
            sc = jnp.sqrt(c)
            n = _norm(x)
            return jnp.arctanh(jnp.clip(sc * n, -1.0 + BALL_EPS, 1.0 - BALL_EPS)) * x / (sc * n)

        def exp_map_zero(v, c):
            sc = jnp.sqrt(c)
            n = _norm(v)
            return jnp.tanh(sc * n) * v / (sc * n)

        def project_to_ball(x, c):
            n = _norm(x)
            maxn = (1.0 - BALL_EPS) / jnp.sqrt(c)
            return jnp.where(n > maxn, x * (maxn / n), x)

        def mobius_add(x, y, c):
            x2 = jnp.sum(x * x, axis=-1, keepdims=True)
            y2 = jnp.sum(y * y, axis=-1, keepdims=True)
            xy = jnp.sum(x * y, axis=-1, keepdims=True)
            num = (1.0 + 2.0 * c * xy + c * y2) * x + (1.0 - c * x2) * y
            den = 1.0 + 2.0 * c * xy + c * c * x2 * y2
            return num / jnp.clip(den, MIN_NORM)
        c = C
        N = h_hyper.shape[0]
        h_tan = log_map_zero(h_hyper, c)
        msg_tan = jnp.einsum('ei,eio->eo', h_tan[src], rel_weight[etype])
        msg_tan = msg_tan + rel_emb[etype]
        msg = exp_map_zero(msg_tan, c)
        en = node_norm[dst, 0]
        norm_sum = jax.ops.segment_sum(en, dst, num_segments=N)
        w = en / (norm_sum[dst] + EPS)
        lam = 2.0 / (1.0 - c * jnp.sum(msg * msg, axis=-1) + EPS)
        wl = w * lam
        numer = jax.ops.segment_sum(wl[:, None] * msg, dst, num_segments=N)
        denom = jax.ops.segment_sum(wl, dst, num_segments=N) + EPS
        h_agg = project_to_ball(numer / denom[:, None], c)
        loop_hyp = exp_map_zero(h_tan @ loop_weight, c)
        h_new = mobius_add(h_agg, loop_hyp, c)
        return h_new

    def _L3_gnn_ref(node_features, edge_attr_e3nn, node_attr_scalar_raw, W_msg_tp, W_msg_lin, W_upd_tp, W_upd_lin, edge_index):
        import jax, jax.numpy as jnp
        import numpy as np
        N_NODES = 3125
        N_EDGES = 100000
        D_NODE = 16
        D_EDGE = 8
        D_HIDDEN = 16
        n_nodes = node_features.shape[0]
        row = edge_index[0]
        col = edge_index[1]
        norm_msg_tp = 1.0 / np.float32(np.sqrt(D_NODE * D_EDGE))
        norm_upd_tp = 1.0 / np.float32(np.sqrt(D_NODE * D_HIDDEN))
        norm_lin = 1.0 / np.float32(np.sqrt(D_HIDDEN))
        x_j = node_features[col]
        m = jnp.einsum('ei,ej,ijh->eh', x_j, edge_attr_e3nn, W_msg_tp) * norm_msg_tp
        m = jax.nn.silu(m)
        m = m @ W_msg_lin * norm_lin
        agg = jax.ops.segment_sum(m, row, num_segments=n_nodes)
        u = jnp.einsum('ni,nh,ihk->nk', node_features, agg, W_upd_tp) * norm_upd_tp
        u = jax.nn.silu(u)
        u = u @ W_upd_lin * norm_lin
        return node_features + u
    edge_index = jnp.stack([src, dst])
    deg = jnp.maximum(jax.ops.segment_sum(jnp.ones(dst.shape, jnp.float32), dst, num_segments=3125), 1.0)
    deg_isqrt = deg ** (-0.5)
    x = _layernorm(x + _L0_gnn_ref(x, edge_index, edge_attr_16), axis=-1)
    x = _layernorm(x + _L1_gnn_ref(x, edge_index, edge_type_8, L1_gnn_W1, L1_gnn_root1, L1_gnn_b1, L1_gnn_W2, L1_gnn_root2, L1_gnn_b2), axis=-1)
    x = _layernorm(x + _L2_gnn_ref(x, deg_isqrt[:, None], L2_gnn_rel_weight, L2_gnn_loop_weight, L2_gnn_rel_emb, src, dst, edge_type_230), axis=-1)
    x = _layernorm(x + _L3_gnn_ref(x, edge_attr_8, node_vec1, L3_gnn_W_msg_tp, L3_gnn_W_msg_lin, L3_gnn_W_upd_tp, L3_gnn_W_upd_lin, edge_index), axis=-1)
    return x

_drawn_inputs = setup_inputs


def setup_inputs(seed=0):
    import zlib

    import numpy as np

    out = dict(_drawn_inputs(seed))
    spreads = {'L1_gnn_b1': (0.0, 0.1), 'L1_gnn_b2': (0.0, 0.1)}
    factors = {'L2_gnn_rel_emb': 3.4}
    for name, (base, spread) in spreads.items():
        noise = np.random.default_rng([zlib.crc32(name.encode()), seed]).standard_normal(out[name].shape)
        drawn = base * np.exp(spread * noise) if base else spread * noise
        out[name] = jnp.asarray(drawn.astype(out[name].dtype))
    for name, factor in factors.items():
        out[name] = (out[name] * factor).astype(out[name].dtype)
    return out
```

```python
from contextlib import ExitStack

import concourse.bass as bass
from concourse import mybir

F32 = mybir.dt.float32
I32 = mybir.dt.int32
ALU = mybir.AluOpType
ACT = mybir.ActivationFunctionType
AX_X = mybir.AxisListType.X
RMAX = bass.bass_isa.ReduceOp.max

P = 128
N_NODES = 3125
N_EDGES = 103125
NW = -(-N_NODES // P)
T = -(-N_EDGES // P)
G = 13
NG = T // G
assert T % G == 0 and NG % 2 == 0
WPAD = 16
D = 16
R1 = 8
H1 = 32
R2 = 230
A8 = 8
BANK = 512
WIDE = NW * R1 * D
MOVE = max(WIDE, G * 2 * R1 * D)
TAB = R2 * D
CH = (TAB + D) // 8
LAST_TAB = TAB - 7 * CH

C = 0.01
EPS = 1e-6
MIN_NORM = 1e-10
BALL_EPS = 1e-5
LN_EPS = 1e-5
MAXN = (1.0 - BALL_EPS) / 0.1
SMALL_ATANH = 0.2
SUB = [(0, 7), (7, G)]


def build(nc, x, dst, src, tile_first, attr16, attr8, rel230, rel8, w1, root1, b1, w2, root2, b2,
          relw, loopw, relemb, wmsg, wmlin, wupd, wulin, out):
    x_table = nc.dram_tensor("x_table", [P * NW, D], F32, kind="Internal").ap()
    y_table = nc.dram_tensor("y_table", [P * NW * R1, D], F32, kind="Internal").ap()
    t_table = nc.dram_tensor("t_table", [P * NW * R2, D], F32, kind="Internal").ap()
    z_table = nc.dram_tensor("z_table", [P * NW, D], F32, kind="Internal").ap()

    ctx = ExitStack()
    with ctx:
        def sb(name, shape, dt=F32):
            return ctx.enter_context(nc.sbuf_tensor(name, shape, dt))

        def sem(name):
            return ctx.enter_context(nc.semaphore(name))

        rel_f = sb("rel_f", [P, T])
        rel230_f = sb("rel230_f", [P, T])
        dst_lane = sb("dst_lane", [P, T])
        dst_win = sb("dst_win", [P, T])
        dst_key = sb("dst_key", [P, T])
        src_lane = sb("src_lane", [P, T])
        src_win = sb("src_win", [P, T])
        src_row = sb("src_row", [P, T])
        dst_row = sb("dst_row", [P, T])
        gather_row = sb("gather_row", [P, T], I32)
        first_win = sb("first_win", [P, NG, WPAD], I32)
        big = sb("big", [P, T * D])
        weights_big = sb("weights_big", [P, TAB + D])
        moving = sb("moving", [P, 2, MOVE])
        hot_lane = sb("hot_lane", [P, 2, G, P])
        rows = sb("rows", [P, 2, G, D])
        row_index = sb("row_index", [P, 2, G], I32)
        hot_small = sb("hot_small", [P, G * NW])
        hot_wide = sb("hot_wide", [P, NW * R1])
        sq_e = sb("sq_e", [P, G, D])
        msg = sb("msg", [P, 2, G, D + 1])
        col = {n: sb("e_" + n, [P, G]) for n in ("ss", "ssc", "z", "t", "rz", "u", "a", "q", "f")}

        count = sb("count", [P, NW * R1])
        lane = sb("lane", [P, P])
        part = sb("part", [P, 1])
        ident = sb("ident", [P, P])
        zeros = sb("zeros", [P, BANK])
        flag = sb("flag", [P, 4])
        flag_i = sb("flag_i", [P, 1], I32)
        tick = sb("tick", [P, 1])
        w1_sb = sb("w1_sb", [P, H1])
        root1_sb = sb("root1_sb", [D + 1, H1])
        w2_sb = sb("w2_sb", [H1 + 1, R1 * D + D])
        wmsg_sb = sb("wmsg_sb", [P, D])
        wmlin_sb = sb("wmlin_sb", [D, D])
        wupd_sb = sb("wupd_sb", [P, 2, D])
        wulin_sb = sb("wulin_sb", [D, D])
        stat = sb("stat", [D + 1, 2, P])
        xin = sb("xin", [P, NW, D])
        xc = sb("xc", [P, NW, D])
        na = sb("na", [P, NW, D])
        nb = sb("nb", [P, NW, D])
        ncx = sb("ncx", [P, NW, D])
        x_one = sb("x_one", [P, NW, D + 1])
        h_one = sb("h_one", [P, NW, H1 + 1])
        base2 = sb("base2", [P, NW, D])
        loopv = sb("loopv", [P, NW, D])
        inv8 = sb("inv8", [P, NW, R1])
        deg = sb("deg", [P, NW])
        w_node = sb("w_node", [P, NW])
        nodeT = sb("nodeT", [H1 + 1, NW, P])
        s_ = {n: sb("n_" + n, [P, NW]) for n in ("a", "b", "c", "d", "e", "f", "g", "h")}

        acc = ctx.enter_context(nc.psum_tensor("acc", [P, 7 * BANK], F32))
        misc = ctx.enter_context(nc.psum_tensor("misc", [P, BANK], F32))

        acc_attr = acc[:, 0:2 * BANK].rearrange("p (w f) -> p w f", f=32)
        acc_rel = acc[:, :].rearrange("p (w f) -> p w f", f=P)
        acc_src = acc[:, 0:NW * D]
        zt_ps = acc[:, BANK:5 * BANK]
        m_ps = [acc[:, 5 * BANK:5 * BANK + G * D], acc[:, 6 * BANK:6 * BANK + G * D]]
        attr16_sb = big[:, :].rearrange("p (t d) -> p t d", d=D)
        stage = [big[:, 0:TAB], big[:, TAB:2 * TAB]]
        attr8_sb = big[:, 0:T * A8].rearrange("p (t d) -> p t d", d=A8)
        outer_e = [big[:, T * A8 + s * G * P:T * A8 + (s + 1) * G * P] for s in range(2)]
        outer_T = [weights_big[:, s * G * P:(s + 1) * G * P].rearrange("p (k e) -> p k e", e=P) for s in range(2)]
        int_a = moving[:, 0, 0:T].bitcast(I32)
        int_b = moving[:, 0, T:2 * T].bitcast(I32)
        int_c = moving[:, 0, 2 * T:3 * T].bitcast(I32)
        int_d = moving[:, 0, 3 * T:4 * T].bitcast(I32)
        int_e = moving[:, 1, 0:T].bitcast(I32)
        int_t = moving[:, 1, T:2 * T].bitcast(I32)
        flt_w = moving[:, 1, 2 * T:3 * T]
        flt_t = moving[:, 1, 3 * T:4 * T]
        flt_u = moving[:, 1, T:2 * T]

        s_edges = sem("edges_loaded")
        s_attr16 = sem("attr16_loaded")
        s_weights = sem("weights_loaded")
        s_attr8 = sem("attr8_loaded")
        s_consts = sem("constants_ready")
        s_iota = sem("iotas_ready")
        s_violation = sem("violation_ready")
        s_allviol = sem("violation_reduced")
        s_flag = sem("flag_ready")
        s_dve = sem("vector_step")
        s_toact = sem("node_operand_ready")
        s_fromact = sem("node_function_ready")
        s_topose = sem("node_operand_for_tensor")
        s_posed = sem("node_product_ready")
        s_seen = sem("row_index_seen")
        s_tangent = sem("tangent_transposed")
        s_table = sem("table_source_ready")
        s_written = sem("table_written")
        s_index = sem("gather_rows_ready")
        s_staged = sem("row_index_staged")
        s_landed = {ph: [sem(f"rows_landed_{ph}_{s}") for s in range(2)] for ph in ("l1a", "l1b", "l2", "l3")}
        PH = ("l0", "l1a", "l1b", "l2", "l3")
        s_ready = {ph: sem(f"messages_ready_{ph}") for ph in PH}
        s_used = {ph: sem(f"messages_used_{ph}") for ph in PH}
        s_wready = {ph: sem(f"wide_ready_{ph}") for ph in PH}
        s_wused = {ph: sem(f"wide_used_{ph}") for ph in PH}
        s_step = {ph: sem(f"message_step_{ph}") for ph in PH}
        s_summed = sem("sums_complete")
        s_sumread = sem("sums_read")
        s_norm = sem("squared_norms_ready")
        s_tanh = sem("tanh_ready")
        s_stat = sem("table_operand_ready")
        s_tabps = sem("table_product_ready")
        s_ev_a = sem("table_evacuated_by_scalar")
        s_ev_v = sem("table_evacuated_by_vector")
        s_tabst = [sem(f"table_stored_{s}") for s in range(2)]
        s_outer = sem("outer_ready")
        s_trans = sem("outer_transposed")
        s_outT = sem("outer_T_ready")
        s_mps = sem("message_product_ready")
        s_silu = sem("message_silu_ready")
        s_out = sem("output_ready")
        s_done = sem("output_stored")

        block = ctx.enter_context(nc.Block())

        def pairs(eng, body):
            body(0, 0, 0)
            body(1, 1, 0)
            with eng.Fori(1, NG // 2) as i:
                body(2 * i, 0, i)
                body(2 * i + 1, 1, i)

        def windows(eng, body):
            body(0, 0, 0)
            body(1, 1, 0)
            with eng.Fori(1, NW // 2) as i:
                body(2 * i, 0, i)
                body(2 * i + 1, 1, i)
            body(NW - 1, 0, NW // 2)

        def later(g):
            return not isinstance(g, int) or g >= 2

        def not_first(g):
            return not isinstance(g, int) or g >= 1

        def at(g):
            return bass.ds(g * G, G)

        PHASES = {
            "l0": (D + R1, acc_attr),
            "l1a": (R1 * D, acc_rel),
            "l1b": (R1 * D, acc_rel),
            "l2": (D + 1, acc_attr),
        }
        BANKS = {"l0": 2, "l1a": 7, "l1b": 7, "l2": 2, "l3": 1}

        def near(ph, s):
            f = PHASES[ph][0]
            return moving[:, s, 0:G * 2 * f].rearrange("p (k w f) -> p k w f", w=2, f=f)

        def wide(ph, s):
            f = PHASES[ph][0]
            return moving[:, s, 0:NW * f].rearrange("p (w f) -> p w f", f=f)

        @block.sync
        def _(sp):
            for to, frm in ((int_a, dst), (int_b, src), (int_c, rel8), (int_d, rel230),
                            (int_e, tile_first.partition_broadcast(P))):
                sp.dma_start(to, frm).then_inc(s_edges, 16)
            sp.dma_start(xin[:, :, :].rearrange("p w d -> p (w d)"), x).then_inc(s_edges, 16)
            sp.dma_start(big[:, :], attr16).then_inc(s_attr16, 16)
            sp.wait_ge(s_consts, 1)
            for to, frm in ((w1_sb[:, :], w1), (root1_sb[0:D, :], root1), (root1_sb[D:D + 1, :], b1),
                            (w2_sb[0:H1, 0:R1 * D], w2), (w2_sb[0:H1, R1 * D:], root2),
                            (w2_sb[H1:H1 + 1, R1 * D:], b2),
                            (weights_big[0:D, 0:TAB], relw), (weights_big[D:D + 1, 0:TAB], relemb),
                            (weights_big[0:D, TAB:], loopw),
                            (wmsg_sb[:, :], wmsg), (wmlin_sb[:, :], wmlin),
                            (wupd_sb[:, 0, :], wupd[0:P, :]), (wupd_sb[:, 1, :], wupd[P:2 * P, :]),
                            (wulin_sb[:, :], wulin)):
                sp.dma_start(to, frm).then_inc(s_weights, 16)
            sp.wait_ge(s_table, 1)
            sp.dma_start(x_table.rearrange("(p w) d -> p (w d)", p=P),
                         xc[:, :, :].rearrange("p w d -> p (w d)")).then_inc(s_written, 16)
            sp.wait_ge(s_table, 2)
            sp.dma_start(y_table.rearrange("(p w) d -> p (w d)", p=P), moving[:, 0, 0:WIDE]).then_inc(s_written, 16)
            t_rows = t_table.rearrange("(p w r) d -> p w (r d)", p=P, w=NW)

            def store(w, s, i):
                sp.wait_ge(s_ev_a, 4 * (w + 1))
                sp.wait_ge(s_ev_v, 4 * (w + 1))
                sp.dma_start(t_rows[:, bass.ds(w, 1), :], stage[s][:, None, :]).then_inc(s_tabst[s], 16)
            windows(sp, store)
            sp.wait_ge(s_tabst[0], 16 * (NW // 2 + 1))
            sp.wait_ge(s_tabst[1], 16 * (NW // 2))
            sp.dma_start(big[:, 0:T * A8], attr8).then_inc(s_attr8, 16)
            sp.wait_ge(s_table, 3)
            sp.dma_start(z_table.rearrange("(p w) d -> p (w d)", p=P),
                         xc[:, :, :].rearrange("p w d -> p (w d)")).then_inc(s_written, 16)
            sp.wait_ge(s_out, 1)
            sp.dma_start(out, xc[:, :, :].rearrange("p w d -> p (w d)")).then_inc(s_done, 16)
            sp.wait_ge(s_done, 16)

        @block.gpsimd
        def _(pool):
            nc.gpsimd.iota(count[:, :], [[1, NW * R1]], base=0, channel_multiplier=0,
                           allow_small_or_imprecise_dtypes=True)
            nc.gpsimd.iota(lane[:, :], [[1, P]], base=0, channel_multiplier=0, allow_small_or_imprecise_dtypes=True)
            nc.gpsimd.iota(part[:, :], [[0, 1]], base=0, channel_multiplier=1,
                           allow_small_or_imprecise_dtypes=True).then_inc(s_iota, 1)
            pool.wait_ge(s_violation, 1)
            nc.gpsimd.partition_all_reduce(flag[:, 1:2], flag[:, 0:1], P, RMAX).then_inc(s_allviol, 1)

            def gather(n, ph, table):
                def group(g, s, i):
                    if later(g):
                        pool.wait_ge(s_ready[ph] if ph != "l3" else s_outer, g - 1)
                        pool.wait_ge(s_landed[ph][s], 16 * G * i)
                    nc.gpsimd.tensor_copy(row_index[:, s, :], gather_row[:, at(g)]).then_inc(s_staged, 1)
                    pool.wait_ge(s_staged, n * NG + g + 1)
                    pool.sem_inc(s_seen, 1)
                    for k in range(G):
                        nc.gpsimd.indirect_dma_start(
                            out=rows[:, s, k, :], out_offset=None, in_=table,
                            in_offset=bass.IndirectOffsetOnAxis(ap=row_index[:, s, k:k + 1], axis=0),
                        ).then_inc(s_landed[ph][s], 16)
                pairs(pool, group)
                pool.wait_ge(s_landed[ph][0], 16 * G * NG // 2)
                pool.wait_ge(s_landed[ph][1], 16 * G * NG // 2)

            pool.wait_ge(s_index, 1)
            pool.wait_ge(s_written, 16)
            gather(0, "l1a", x_table)
            pool.wait_ge(s_index, 2)
            pool.wait_ge(s_written, 32)
            gather(1, "l1b", y_table)

            pool.wait_ge(s_tangent, 1)

            def operand(w, s, i):
                if later(w):
                    pool.wait_ge(s_tabps, 8 * (w - 1))
                nc.gpsimd.tensor_copy(stat[:, s, :], nodeT[0:D + 1, bass.ds(w, 1), :].rearrange("p o e -> p (o e)")
                                      ).then_inc(s_stat, 1)
            windows(pool, operand)
            pool.wait_ge(s_index, 3)
            pool.wait_ge(s_tabst[0], 16 * (NW // 2 + 1))
            pool.wait_ge(s_tabst[1], 16 * (NW // 2))
            gather(2, "l2", t_table)
            pool.wait_ge(s_index, 4)
            pool.wait_ge(s_written, 48)
            gather(3, "l3", z_table)

        @block.scalar
        def _(act):
            served = [0]

            def function(out_, in_, func, scale=1.0):
                served[0] += 1
                act.wait_ge(s_toact, served[0])
                nc.scalar.activation(out_, in_, func, scale=scale).then_inc(s_fromact, 1)

            function(s_["g"][:, :], s_["f"][:, :], ACT.Sqrt)
            function(s_["d"][:, :], s_["c"][:, :], ACT.Sqrt)
            function(s_["d"][:, :], s_["c"][:, :], ACT.Sqrt)
            function(s_["c"][:, :], s_["b"][:, :], ACT.Sqrt, scale=C)
            function(s_["g"][:, :], s_["f"][:, :], ACT.Ln)

            def evacuate(w, s, i):
                if later(w):
                    act.wait_ge(s_tabst[s], 16 * i)
                for c in (0, 2, 4, 6):
                    act.wait_ge(s_tabps, 8 * w + c + 1)
                    nc.scalar.copy(stage[s][:, c * CH:(c + 1) * CH], acc[:, c * BANK:c * BANK + CH]).then_inc(s_ev_a, 1)
            windows(act, evacuate)

            function(s_["c"][:, :], s_["b"][:, :], ACT.Sqrt, scale=C)
            function(s_["d"][:, :], s_["c"][:, :], ACT.Tanh)

            def hyperbolic(g, s, i):
                act.wait_ge(s_norm, g + 1)
                nc.scalar.activation(col["z"][:, :], col["ssc"][:, :], ACT.Sqrt, scale=C).then_inc(s_tanh, 1)
                act.wait_ge(s_tanh, 2 * g + 1)
                nc.scalar.activation(col["t"][:, :], col["z"][:, :], ACT.Tanh).then_inc(s_tanh, 1)
            pairs(act, hyperbolic)
            function(s_["c"][:, :], s_["b"][:, :], ACT.Sqrt)
            function(s_["d"][:, :], s_["c"][:, :], ACT.Sqrt)

            def last_layer(g, s, i):
                if later(g):
                    act.wait_ge(s_mps, g - 1)
                act.wait_ge(s_trans, g + 1)
                for c in range(0, G, 4):
                    n = min(4, G - c)
                    last = nc.scalar.copy(outer_T[s][:, c:c + n, :].rearrange("p k e -> p (k e)"),
                                          zt_ps[:, c * P:(c + n) * P])
                last.then_inc(s_outT, 1)
                act.wait_ge(s_mps, g + 1)
                if later(g):
                    act.wait_ge(s_ready["l3"], 2 * (g - 1))
                nc.scalar.activation(msg[:, s, :, 0:D], m_ps[s].rearrange("p (k d) -> p k d", d=D), ACT.Silu,
                                     scale=float((D * A8) ** -0.5)).then_inc(s_silu, 1)
            pairs(act, last_layer)
            function(nb[:, :, :], misc[:, 0:NW * D].rearrange("p (w d) -> p w d", d=D), ACT.Silu,
                     scale=float((D * D) ** -0.5))
            function(s_["d"][:, :], s_["c"][:, :], ACT.Sqrt)

        @block.vector
        def _(dve):
            V = nc.vector
            steps = [0]
            asked = [0]

            def link(ins):
                steps[0] += 1
                ins.then_inc(s_dve, 1)
                dve.wait_ge(s_dve, steps[0])

            def to_act(ins):
                asked[0] += 1
                ins.then_inc(s_toact, 1)
                dve.wait_ge(s_fromact, asked[0])

            def bc(ap, n):
                return ap[:, :, None].to_broadcast([P, ap.shape[1], n])

            def layer_norm(v):
                link(V.reduce_sum(s_["a"][:, :], v, AX_X))
                link(V.tensor_scalar(s_["a"][:, :], s_["a"][:, :], 1.0 / D, None, ALU.mult))
                link(V.tensor_tensor(na[:, :, :], v, bc(s_["a"], D), ALU.subtract))
                link(V.tensor_tensor(ncx[:, :, :], na[:, :, :], na[:, :, :], ALU.mult))
                link(V.reduce_sum(s_["b"][:, :], ncx[:, :, :], AX_X))
                to_act(V.tensor_scalar(s_["c"][:, :], s_["b"][:, :], 1.0 / D, LN_EPS, ALU.mult, ALU.add))
                link(V.reciprocal(s_["e"][:, :], s_["d"][:, :]))
                link(V.tensor_tensor(xc[:, :, :], na[:, :, :], bc(s_["e"], D), ALU.mult))

            link(V.memset(zeros[:, :], 0.0))
            link(V.memset(w2_sb[:, :], 0.0))
            link(V.memset(first_win[:, :, :], 0))
            link(V.memset(x_one[:, :, :], 1.0))
            link(V.memset(h_one[:, :, :], 1.0))
            V.memset(weights_big[:, TAB:], 0.0).then_inc(s_consts, 1)
            dve.wait_ge(s_iota, 1)
            V.tensor_scalar(ident[:, :], lane[:, :], part[:, 0:1], None, ALU.is_equal).then_inc(s_topose, 1)
            dve.wait_ge(s_edges, 6 * 16)

            def lanes_and_windows(ids, to_lane, to_win):
                link(V.tensor_scalar(int_t, ids, P - 1, None, ALU.bitwise_and))
                link(V.tensor_copy(to_lane, int_t))
                link(V.tensor_scalar(int_t, ids, P.bit_length() - 1, None, ALU.arith_shift_right))
                link(V.tensor_copy(to_win, int_t))
            lanes_and_windows(int_a, dst_lane[:, :], dst_win[:, :])
            lanes_and_windows(int_b, src_lane[:, :], src_win[:, :])
            link(V.tensor_scalar(int_t, int_e, P.bit_length() - 1, None, ALU.arith_shift_right))
            link(V.tensor_copy(flt_w, int_t))
            link(V.tensor_copy(rel_f[:, :], int_c))
            link(V.tensor_copy(rel230_f[:, :], int_d))
            link(V.scalar_tensor_tensor(src_row[:, :], src_lane[:, :], float(NW), src_win[:, :], ALU.mult, ALU.add))
            link(V.scalar_tensor_tensor(dst_row[:, :], dst_lane[:, :], float(NW), dst_win[:, :], ALU.mult, ALU.add))
            V.tensor_copy(gather_row[:, :], src_row[:, :]).then_inc(s_index, 1)
            link(V.tensor_tensor(flt_t, dst_win[:, :], flt_w, ALU.subtract))
            link(V.scalar_tensor_tensor(flt_u, flt_t, -1.0, flt_t, ALU.add, ALU.mult))
            V.reduce_max(flag[:, 0:1], flt_u, AX_X).then_inc(s_violation, 1)
            dve.wait_ge(s_allviol, 1)
            link(V.tensor_scalar(flag[:, 2:3], flag[:, 1:2], 0.0, None, ALU.is_equal))
            link(V.tensor_copy(flag_i[:, :], flag[:, 2:3]))
            link(V.tensor_scalar(flt_w, flt_w, flag[:, 2:3], None, ALU.mult))
            link(V.tensor_copy(first_win[:, :, 0:G], flt_w.rearrange("p (g k) -> p g k", k=G)))
            link(V.tensor_tensor(dst_win[:, :], dst_win[:, :], flt_w, ALU.subtract))
            link(V.scalar_tensor_tensor(dst_key[:, :], dst_win[:, :], float(R1), rel_f[:, :], ALU.mult, ALU.add))
            V.memset(tick[:, :], 0.0).then_inc(s_flag, 1)
            dve.wait_ge(s_flag, 1)
            narrow = dve.value_load(flag_i[0:1, 0:1], min_val=0, max_val=1)

            def hot_of(to, n, keys):
                return V.tensor_tensor(to, count[:, None, 0:n].to_broadcast([P, G, n]),
                                       keys[:, :, None].to_broadcast([P, G, n]), ALU.is_equal)

            def lane_hot(s, g, lanes):
                return V.tensor_tensor(hot_lane[:, s, :, :], lane[:, None, :].to_broadcast([P, G, P]),
                                       lanes[:, at(g)][:, :, None].to_broadcast([P, G, P]), ALU.is_equal)

            NORM_STEPS = 11

            def norms(s, g, base):
                v = rows[:, s, :, :]
                n = [0]

                def step(ins):
                    n[0] += 1
                    ins.then_inc(s_step["l2"], 1)
                    dve.wait_ge(s_step["l2"], base + n[0])
                step(V.tensor_tensor(sq_e[:, :, :], v, v, ALU.mult))
                step(V.reduce_sum(col["ss"][:, :], sq_e[:, :, :], AX_X))
                V.tensor_scalar(col["ssc"][:, :], col["ss"][:, :], MIN_NORM, None, ALU.max).then_inc(s_norm, 1)
                dve.wait_ge(s_tanh, 2 * g + 2)
                step(V.reciprocal(col["rz"][:, :], col["z"][:, :]))
                step(V.tensor_tensor(col["u"][:, :], col["t"][:, :], col["rz"][:, :], ALU.mult))
                step(V.tensor_tensor(col["a"][:, :], col["u"][:, :], col["u"][:, :], ALU.mult))
                step(V.tensor_tensor(col["a"][:, :], col["a"][:, :], col["ss"][:, :], ALU.mult))
                step(V.tensor_scalar(col["q"][:, :], col["a"][:, :], -C, 1.0 + EPS, ALU.mult, ALU.add))
                step(V.reciprocal(col["q"][:, :], col["q"][:, :]))
                step(V.tensor_scalar(msg[:, s, :, D], col["q"][:, :], 2.0, None, ALU.mult))
                step(V.tensor_tensor(col["f"][:, :], msg[:, s, :, D], col["u"][:, :], ALU.mult))
                step(V.tensor_tensor(msg[:, s, :, 0:D], v, bc(col["f"], D), ALU.mult))
                assert n[0] == NORM_STEPS

            def near_messages(ph):
                before = NORM_STEPS if ph == "l2" else 0

                def group(g, s, i):
                    if not_first(g):
                        dve.wait_ge(s_ready[ph], g)
                    if later(g):
                        dve.wait_ge(s_used[ph], g - 1)
                    if ph != "l0":
                        dve.wait_ge(s_landed[ph][s], 16 * G * (i + 1))
                    mv = near(ph, s)
                    if ph in ("l1a", "l1b"):
                        keys = hot_small[:, 0:G * 2 * R1].rearrange("p (k c) -> p k c", k=G)
                        hot_of(keys, 2 * R1, dst_key[:, at(g)]).then_inc(s_step[ph], 1)
                        dve.wait_ge(s_step[ph], g + 1)
                        V.tensor_tensor(mv.rearrange("p k w (r d) -> p k (w r) d", d=D),
                                        keys[:, :, :, None].to_broadcast([P, G, 2 * R1, D]),
                                        rows[:, s, :, :][:, :, None, :].to_broadcast([P, G, 2 * R1, D]), ALU.mult)
                    else:
                        val = attr16_sb[:, at(g), :]
                        if ph == "l2":
                            norms(s, g, (before + 1) * g)
                            val = msg[:, s, :, :]
                        wins = hot_small[:, 0:G * 2].rearrange("p (k w) -> p k w", k=G)
                        hot_of(wins, 2, dst_win[:, at(g)]).then_inc(s_step[ph], 1)
                        dve.wait_ge(s_step[ph], (before + 1) * (g + 1))
                        f = val.shape[2]
                        V.tensor_tensor(mv[:, :, :, 0:f], wins[:, :, :, None].to_broadcast([P, G, 2, f]),
                                        val[:, :, None, :].to_broadcast([P, G, 2, f]), ALU.mult)
                        if ph == "l0":
                            for w in range(2):
                                V.tensor_tensor(mv[:, :, w, D:D + R1],
                                                count[:, None, w * R1:(w + 1) * R1].to_broadcast([P, G, R1]),
                                                dst_key[:, at(g)][:, :, None].to_broadcast([P, G, R1]), ALU.is_equal)
                    lane_hot(s, g, dst_lane).then_inc(s_ready[ph], 1)
                pairs(dve, group)

            def wide_messages(ph):
                before = NORM_STEPS if ph == "l2" else 0
                by_key = ph in ("l1a", "l1b")
                n_keys = NW * R1 if by_key else NW
                keys = dst_key if by_key else dst_win
                hot = hot_wide[:, 0:n_keys]

                def group(g, s, i):
                    if not_first(g):
                        dve.wait_ge(s_ready[ph], g)
                    if later(g):
                        dve.wait_ge(s_wused[ph], G * (g - 1))
                    if ph != "l0":
                        dve.wait_ge(s_landed[ph][s], 16 * G * (i + 1))
                    if ph == "l2":
                        norms(s, g, (before + G) * g)
                    lane_hot(s, g, dst_lane)
                    for k in range(G):
                        tile = G * g + k
                        one = bass.ds(tile, 1)
                        if k:
                            dve.wait_ge(s_wready[ph], tile)
                        if not isinstance(g, int) or tile >= 2:
                            dve.wait_ge(s_wused[ph], tile - 1)
                        mv = wide(ph, (s * G + k) % 2)
                        V.tensor_tensor(hot, count[:, 0:n_keys], keys[:, one].to_broadcast([P, n_keys]),
                                        ALU.is_equal).then_inc(s_step[ph], 1)
                        dve.wait_ge(s_step[ph], (before + G) * g + before + k + 1)
                        if by_key:
                            last = V.tensor_tensor(mv.rearrange("p w (r d) -> p (w r) d", d=D),
                                                   hot[:, :, None].to_broadcast([P, n_keys, D]),
                                                   rows[:, s, k:k + 1, :].to_broadcast([P, n_keys, D]), ALU.mult)
                        elif ph == "l2":
                            last = V.tensor_tensor(mv, hot[:, :, None].to_broadcast([P, NW, D + 1]),
                                                   msg[:, s, k:k + 1, :].to_broadcast([P, NW, D + 1]), ALU.mult)
                        else:
                            V.tensor_tensor(mv[:, :, D:D + R1], count[:, 0:NW * R1].rearrange("p (w r) -> p w r", r=R1),
                                            dst_key[:, one][:, :, None].to_broadcast([P, NW, R1]), ALU.is_equal)
                            last = V.tensor_tensor(mv[:, :, 0:D], hot[:, :, None].to_broadcast([P, NW, D]),
                                                   attr16_sb[:, one, :].to_broadcast([P, NW, D]), ALU.mult)
                        last.then_inc(s_wready[ph], 1)
                    dve.wait_ge(s_wready[ph], G * (g + 1))
                    V.memset(tick[:, :], 0.0).then_inc(s_ready[ph], 1)
                pairs(dve, group)

            def messages(ph):
                with dve.If(narrow):
                    near_messages(ph)
                with dve.Else():
                    wide_messages(ph)

            def to_tensor(ins):
                posed[0] += 1
                ins.then_inc(s_topose, 1)
                dve.wait_ge(s_posed, posed[0])
            posed = [0]

            def flat(ap):
                return ap.rearrange("p w d -> p (w d)")

            dve.wait_ge(s_attr16, 16)
            messages("l0")
            dve.wait_ge(s_summed, 1)
            counts = acc_attr[:, 0:NW, D:D + R1]
            link(V.tensor_scalar(inv8[:, :, :], counts, 1.0, None, ALU.max))
            link(V.reciprocal(inv8[:, :, :], inv8[:, :, :]))
            link(V.reduce_sum(deg[:, :], counts, AX_X))
            to_act(V.tensor_scalar(s_["f"][:, :], deg[:, :], 1.0, None, ALU.max))
            link(V.reciprocal(s_["h"][:, :], s_["f"][:, :]))
            link(V.tensor_tensor(na[:, :, :], acc_attr[:, 0:NW, 0:D], bc(s_["h"], D), ALU.mult))
            link(V.tensor_tensor(nb[:, :, :], na[:, :, :], xin[:, :, :], ALU.add))
            link(V.reciprocal(s_["g"][:, :], s_["g"][:, :]))
            link(V.tensor_tensor(s_["f"][:, :], s_["g"][:, :], deg[:, :], ALU.mult))
            link(V.tensor_scalar(s_["f"][:, :], s_["f"][:, :], EPS, None, ALU.add))
            link(V.reciprocal(s_["f"][:, :], s_["f"][:, :]))
            link(V.tensor_tensor(w_node[:, :], s_["g"][:, :], s_["f"][:, :], ALU.mult))
            layer_norm(nb[:, :, :])
            V.tensor_copy(x_one[:, :, 0:D], xc[:, :, :]).then_inc(s_table, 1)

            messages("l1a")
            V.scalar_tensor_tensor(gather_row[:, :], src_row[:, :], float(R1), rel_f[:, :], ALU.mult, ALU.add
                                   ).then_inc(s_index, 1)
            dve.wait_ge(s_summed, 2)
            by_rel = inv8[:, :, :].rearrange("p w r -> p (w r)")[:, :, None].to_broadcast([P, NW * R1, D])
            sums = acc[:, 0:WIDE].rearrange("p (c d) -> p c d", d=D)
            means = moving[:, 0, 0:WIDE]
            to_tensor(V.tensor_tensor(means.rearrange("p (c d) -> p c d", d=D), sums, by_rel, ALU.mult))
            to_tensor(V.tensor_copy(moving[:, 1, 0:WIDE], acc[:, 0:NW * P]))
            to_tensor(V.tensor_copy(nodeT[0:D + 1, :, :].rearrange("p w e -> p (w e)"), acc[0:D + 1, 0:NW * P]))
            h_ps = acc[:, 0:NW * H1].rearrange("p (w f) -> p w f", f=H1)
            to_tensor(V.tensor_scalar(h_one[:, :, 0:H1], h_ps, 0.0, None, ALU.max))
            to_tensor(V.tensor_copy(nodeT[0:H1 + 1, :, :].rearrange("p w e -> p (w e)"), acc[0:H1 + 1, 0:NW * P]))
            V.tensor_copy(flat(base2[:, :, :]), misc[:, 0:NW * D])
            V.tensor_copy(moving[:, 0, 0:WIDE], acc[:, 0:WIDE]).then_inc(s_table, 1)
            dve.wait_ge(s_table, 2)
            V.memset(tick[:, :], 0.0).then_inc(s_sumread, 1)

            dve.wait_ge(s_written, 32)
            messages("l1b")
            V.scalar_tensor_tensor(gather_row[:, :], src_row[:, :], float(R2), rel230_f[:, :], ALU.mult, ALU.add
                                   ).then_inc(s_index, 1)
            dve.wait_ge(s_summed, 3)
            link(V.tensor_tensor(means.rearrange("p (c d) -> p c d", d=D), sums, by_rel, ALU.mult))
            link(V.reduce_sum(nb[:, :, :], means.rearrange("p (w r d) -> p w d r", r=R1, d=D), AX_X))
            link(V.tensor_tensor(nb[:, :, :], nb[:, :, :], base2[:, :, :], ALU.add))
            link(V.tensor_tensor(nb[:, :, :], nb[:, :, :], xc[:, :, :], ALU.add))
            layer_norm(nb[:, :, :])

            link(V.tensor_tensor(na[:, :, :], xc[:, :, :], xc[:, :, :], ALU.mult))
            link(V.reduce_sum(s_["a"][:, :], na[:, :, :], AX_X))
            to_act(V.tensor_scalar(s_["b"][:, :], s_["a"][:, :], MIN_NORM, None, ALU.max))
            link(V.tensor_scalar(s_["d"][:, :], s_["c"][:, :], 1.0 - BALL_EPS, -1.0 + BALL_EPS, ALU.min, ALU.max))
            link(V.tensor_scalar(s_["e"][:, :], s_["d"][:, :], 1.0, None, ALU.add))
            link(V.tensor_scalar(s_["a"][:, :], s_["d"][:, :], -1.0, 1.0, ALU.mult, ALU.add))
            link(V.reciprocal(s_["a"][:, :], s_["a"][:, :]))
            to_act(V.tensor_tensor(s_["f"][:, :], s_["e"][:, :], s_["a"][:, :], ALU.mult))
            link(V.reciprocal(s_["h"][:, :], s_["c"][:, :]))
            link(V.scalar_tensor_tensor(s_["e"][:, :], s_["g"][:, :], 0.5, s_["h"][:, :], ALU.mult, ALU.mult))
            link(V.tensor_tensor(s_["f"][:, :], s_["d"][:, :], s_["d"][:, :], ALU.mult))
            link(V.tensor_scalar(s_["a"][:, :], s_["f"][:, :], 1.0 / 13, 1.0 / 11, ALU.mult, ALU.add))
            for k in (9, 7, 5, 3, 1):
                link(V.tensor_tensor(s_["a"][:, :], s_["a"][:, :], s_["f"][:, :], ALU.mult))
                link(V.tensor_scalar(s_["a"][:, :], s_["a"][:, :], 1.0 / k, None, ALU.add))
            link(V.tensor_scalar(s_["b"][:, :], s_["c"][:, :], SMALL_ATANH, None, ALU.is_lt))
            link(V.tensor_tensor(s_["a"][:, :], s_["a"][:, :], s_["e"][:, :], ALU.subtract))
            link(V.tensor_tensor(s_["a"][:, :], s_["a"][:, :], s_["b"][:, :], ALU.mult))
            link(V.tensor_tensor(s_["e"][:, :], s_["e"][:, :], s_["a"][:, :], ALU.add))
            to_tensor(V.tensor_tensor(x_one[:, :, 0:D], xc[:, :, :], bc(s_["e"], D), ALU.mult))
            V.tensor_copy(nodeT[0:D + 1, :, :].rearrange("p w e -> p (w e)"), acc[0:D + 1, 0:NW * P]
                          ).then_inc(s_tangent, 1)

            def evacuate(w, s, i):
                if later(w):
                    dve.wait_ge(s_tabst[s], 16 * i)
                for c in (1, 3, 5):
                    dve.wait_ge(s_tabps, 8 * w + c + 1)
                    V.tensor_copy(stage[s][:, c * CH:(c + 1) * CH], acc[:, c * BANK:c * BANK + CH]).then_inc(s_ev_v, 1)
                dve.wait_ge(s_tabps, 8 * w + 8)
                V.tensor_copy(loopv[:, bass.ds(w, 1), :].rearrange("p o d -> p (o d)"), misc[:, LAST_TAB:CH])
                V.tensor_copy(stage[s][:, 7 * CH:TAB], misc[:, 0:LAST_TAB]).then_inc(s_ev_v, 1)
            windows(dve, evacuate)
            dve.wait_ge(s_ev_v, 4 * NW)
            link(V.tensor_tensor(na[:, :, :], loopv[:, :, :], loopv[:, :, :], ALU.mult))
            link(V.reduce_sum(s_["a"][:, :], na[:, :, :], AX_X))
            to_act(V.tensor_scalar(s_["b"][:, :], s_["a"][:, :], MIN_NORM, None, ALU.max))
            to_act(V.memset(tick[:, :], 0.0))
            link(V.reciprocal(s_["c"][:, :], s_["c"][:, :]))
            link(V.tensor_tensor(s_["c"][:, :], s_["c"][:, :], s_["d"][:, :], ALU.mult))
            link(V.tensor_tensor(loopv[:, :, :], loopv[:, :, :], bc(s_["c"], D), ALU.mult))
            V.memset(tick[:, :], 0.0).then_inc(s_sumread, 1)

            messages("l2")
            V.tensor_copy(gather_row[:, :], dst_row[:, :]).then_inc(s_index, 1)
            dve.wait_ge(s_summed, 4)
            link(V.tensor_tensor(s_["a"][:, :], w_node[:, :], acc_attr[:, 0:NW, D], ALU.mult))
            link(V.tensor_scalar(s_["a"][:, :], s_["a"][:, :], EPS, None, ALU.add))
            link(V.reciprocal(s_["a"][:, :], s_["a"][:, :]))
            link(V.tensor_tensor(s_["a"][:, :], s_["a"][:, :], w_node[:, :], ALU.mult))
            link(V.tensor_tensor(nb[:, :, :], acc_attr[:, 0:NW, 0:D], bc(s_["a"], D), ALU.mult))
            link(V.tensor_tensor(na[:, :, :], nb[:, :, :], nb[:, :, :], ALU.mult))
            link(V.reduce_sum(s_["a"][:, :], na[:, :, :], AX_X))
            to_act(V.tensor_scalar(s_["b"][:, :], s_["a"][:, :], MIN_NORM, None, ALU.max))
            link(V.reciprocal(s_["d"][:, :], s_["c"][:, :]))
            link(V.tensor_scalar(s_["d"][:, :], s_["d"][:, :], MAXN, 1.0, ALU.mult, ALU.min))
            link(V.tensor_tensor(nb[:, :, :], nb[:, :, :], bc(s_["d"], D), ALU.mult))
            link(V.tensor_tensor(na[:, :, :], nb[:, :, :], nb[:, :, :], ALU.mult))
            link(V.reduce_sum(s_["a"][:, :], na[:, :, :], AX_X))
            link(V.tensor_tensor(na[:, :, :], loopv[:, :, :], loopv[:, :, :], ALU.mult))
            link(V.reduce_sum(s_["b"][:, :], na[:, :, :], AX_X))
            link(V.tensor_tensor(na[:, :, :], loopv[:, :, :], nb[:, :, :], ALU.mult))
            link(V.reduce_sum(s_["c"][:, :], na[:, :, :], AX_X))
            link(V.tensor_scalar(s_["c"][:, :], s_["c"][:, :], 2 * C, 1.0, ALU.mult, ALU.add))
            link(V.scalar_tensor_tensor(s_["e"][:, :], s_["b"][:, :], C, s_["c"][:, :], ALU.mult, ALU.add))
            link(V.tensor_tensor(s_["f"][:, :], s_["a"][:, :], s_["b"][:, :], ALU.mult))
            link(V.scalar_tensor_tensor(s_["f"][:, :], s_["f"][:, :], C * C, s_["c"][:, :], ALU.mult, ALU.add))
            link(V.tensor_scalar(s_["f"][:, :], s_["f"][:, :], MIN_NORM, None, ALU.max))
            link(V.reciprocal(s_["f"][:, :], s_["f"][:, :]))
            link(V.tensor_scalar(s_["a"][:, :], s_["a"][:, :], -C, 1.0, ALU.mult, ALU.add))
            link(V.tensor_tensor(nb[:, :, :], nb[:, :, :], bc(s_["e"], D), ALU.mult))
            link(V.tensor_tensor(na[:, :, :], loopv[:, :, :], bc(s_["a"], D), ALU.mult))
            link(V.tensor_tensor(nb[:, :, :], nb[:, :, :], na[:, :, :], ALU.add))
            link(V.tensor_tensor(nb[:, :, :], nb[:, :, :], bc(s_["f"], D), ALU.mult))
            link(V.tensor_tensor(nb[:, :, :], nb[:, :, :], xc[:, :, :], ALU.add))
            layer_norm(nb[:, :, :])
            V.memset(tick[:, :], 0.0).then_inc(s_table, 1)
            dve.wait_ge(s_table, 3)
            V.memset(tick[:, :], 0.0).then_inc(s_sumread, 1)

            dve.wait_ge(s_attr8, 16)
            hot_src = hot_small[:, :].rearrange("p (k w) -> p k w", k=G)

            def outer(g, s, i):
                dve.wait_ge(s_landed["l3"][s], 16 * G * (i + 1))
                if later(g):
                    dve.wait_ge(s_trans, g - 1)
                V.tensor_tensor(outer_e[s].rearrange("p (k i j) -> p k i j", i=D, j=A8),
                                rows[:, s, :, :][:, :, :, None].to_broadcast([P, G, D, A8]),
                                attr8_sb[:, at(g), :][:, :, None, :].to_broadcast([P, G, D, A8]), ALU.mult
                                ).then_inc(s_outer, 1)

            def by_src(g, s):
                dve.wait_ge(s_silu, g + 1)
                if not_first(g):
                    dve.wait_ge(s_ready["l3"], 2 * g)
                hot_of(hot_src, NW, src_win[:, at(g)]).then_inc(s_step["l3"], 1)
                dve.wait_ge(s_step["l3"], g + 1)
                for q, (k0, k1) in enumerate(SUB):
                    if not_first(g):
                        dve.wait_ge(s_used["l3"], 2 * g - 1 + q)
                    if q == 0:
                        lane_hot(s, g, src_lane)
                    n = k1 - k0
                    V.tensor_tensor(moving[:, q, 0:n * NW * D].rearrange("p (k w d) -> p k w d", w=NW, d=D),
                                    hot_src[:, k0:k1, :][:, :, :, None].to_broadcast([P, n, NW, D]),
                                    msg[:, s, k0:k1, 0:D][:, :, None, :].to_broadcast([P, n, NW, D]), ALU.mult
                                    ).then_inc(s_ready["l3"], 1)

            def last_layer(g, s, i):
                outer(g, s, i)
                if not_first(g):
                    by_src(g - 1, 1 - s)
            pairs(dve, last_layer)
            by_src(NG - 1, 1)
            dve.wait_ge(s_summed, 5)

            lin = float(D ** -0.5)
            to_tensor(V.tensor_copy(flat(nb[:, :, :]), acc_src))
            to_tensor(V.tensor_copy(nodeT[0:D, :, :].rearrange("p w e -> p (w e)"), acc[0:D, 0:NW * P]))
            link(V.tensor_scalar(flat(na[:, :, :]), misc[:, 0:NW * D], lin, None, ALU.mult))
            pair_of = moving[:, :, :].rearrange("p s m -> p (s m)")[:, 0:NW * D * D]
            to_tensor(V.tensor_tensor(pair_of.rearrange("p (w i h) -> p w i h", i=D, h=D),
                                      xc[:, :, :, None].to_broadcast([P, NW, D, D]),
                                      na[:, :, None, :].to_broadcast([P, NW, D, D]), ALU.mult))
            to_tensor(V.tensor_copy(big[:, 0:NW * P], acc[:, 0:NW * P]))
            to_tensor(V.tensor_copy(big[:, NW * P:2 * NW * P], acc[:, 0:NW * P]))
            to_act(V.memset(tick[:, :], 0.0))
            to_tensor(V.memset(tick[:, :], 0.0))
            to_tensor(V.tensor_copy(nodeT[0:D, :, :].rearrange("p w e -> p (w e)"), acc[0:D, 0:NW * P]))
            link(V.tensor_scalar(flat(nb[:, :, :]), misc[:, 0:NW * D], lin, None, ALU.mult))
            link(V.scalar_tensor_tensor(nb[:, :, :], xc[:, :, :], 2.0, nb[:, :, :], ALU.mult, ALU.add))
            layer_norm(nb[:, :, :])
            V.memset(tick[:, :], 0.0).then_inc(s_out, 1)

        @block.tensor
        def _(pe):
            M = nc.tensor
            pe.wait_ge(s_topose, 1)
            pe.wait_ge(s_flag, 1)
            narrow = pe.value_load(flag_i[0:1, 0:1], min_val=0, max_val=1)
            turn = [1]
            loads = [0]

            def clear(ph):
                for b in range(BANKS[ph]):
                    M.matmul(acc[:, b * BANK:(b + 1) * BANK], zeros[:, 0:P], zeros[:, :], start=True, stop=True)

            def add(to, lanes, mv):
                return M.matmul(to, lanes, mv, start=False, stop=False, skip_group_check=True)

            def close():
                M.matmul(acc[:, 0:P], zeros[:, 0:P], zeros[:, 0:P], start=False, stop=True,
                         skip_group_check=True).then_inc(s_summed, 1)

            def scatter(ph):
                f, sums = PHASES[ph]
                per = 4 if f == P else 16

                def near_group(g, s, i):
                    loads[0] += 1
                    first = [pe.alloc_register(f"first_window_{loads[0]}_{k}") for k in range(G)]
                    pe.load(first, first_win[0:1, bass.ds(g, 1), 0:G])
                    wins = [pe.snap(r, donate=True, min_val=0, max_val=NW - 1) for r in first]
                    pe.wait_ge(s_ready[ph], g + 1)
                    mv = near(ph, s)
                    for k in range(G):
                        for w in range(2):
                            last = add(sums[:, bass.ds(wins[k] + w, 1), 0:f], hot_lane[:, s, k, :], mv[:, k, w, :])
                    last.then_inc(s_used[ph], 1)

                def wide_group(g, s, i):
                    for k in range(G):
                        pe.wait_ge(s_wready[ph], G * g + k + 1)
                        mv = wide(ph, (s * G + k) % 2)
                        for w in range(0, NW, per):
                            n = min(per, NW - w)
                            last = add(sums[:, w:w + n, 0:f], hot_lane[:, s, k, :], mv[:, w:w + n, :])
                        last.then_inc(s_wused[ph], 1)
                clear(ph)
                with pe.If(narrow):
                    pairs(pe, near_group)
                with pe.Else():
                    pairs(pe, wide_group)
                close()

            def operand_ready():
                turn[0] += 1
                pe.wait_ge(s_topose, turn[0])

            def transposes(block_of, n):
                for w in range(NW):
                    last = M.transpose(acc[0:n, w * P:(w + 1) * P], block_of(w), ident[:, :])
                last.then_inc(s_posed, 1)

            scatter("l0")
            pe.wait_ge(s_table, 1)
            scatter("l1a")
            pe.wait_ge(s_weights, 14 * 16)
            operand_ready()
            transposes(lambda w: moving[:, 0, w * P:(w + 1) * P], P)
            operand_ready()
            transposes(lambda w: x_one[:, w, :], D + 1)
            operand_ready()
            for w in range(NW):
                h_w = acc[:, w * H1:(w + 1) * H1]
                M.matmul(h_w, moving[:, 1, w * P:(w + 1) * P], w1_sb[:, :], start=True, stop=False)
                last = M.matmul(h_w, nodeT[0:D + 1, w, :], root1_sb[:, :], start=False, stop=True)
            last.then_inc(s_posed, 1)
            operand_ready()
            transposes(lambda w: h_one[:, w, :], H1 + 1)
            operand_ready()
            for w in range(NW):
                M.matmul(acc[:, w * P:(w + 1) * P], nodeT[0:H1 + 1, w, :], w2_sb[:, 0:R1 * D], start=True, stop=True)
                last = M.matmul(misc[:, w * D:(w + 1) * D], nodeT[0:H1 + 1, w, :], w2_sb[:, R1 * D:], start=True, stop=True)
            last.then_inc(s_posed, 1)
            pe.wait_ge(s_sumread, 1)
            scatter("l1b")
            operand_ready()
            transposes(lambda w: x_one[:, w, :], D + 1)

            def table(w, s, i):
                pe.wait_ge(s_stat, w + 1)
                for c in range(8):
                    if not_first(w):
                        if c % 2:
                            pe.wait_ge(s_ev_v, 4 * (w - 1) + c // 2 + 1)
                        else:
                            pe.wait_ge(s_ev_a, 4 * (w - 1) + c // 2 + 1)
                    to = misc[:, 0:CH] if c == 7 else acc[:, c * BANK:c * BANK + CH]
                    M.matmul(to, stat[:, s, :], weights_big[0:D + 1, c * CH:(c + 1) * CH], start=True, stop=True
                             ).then_inc(s_tabps, 1)
            windows(pe, table)
            pe.wait_ge(s_sumread, 2)
            scatter("l2")
            pe.wait_ge(s_sumread, 3)

            clear("l3")

            def transpose_outer(g, s):
                pe.wait_ge(s_outer, g + 1)
                if not_first(g):
                    pe.wait_ge(s_outT, g)
                for k in range(G):
                    last = M.transpose(zt_ps[:, k * P:(k + 1) * P], outer_e[s][:, k * P:(k + 1) * P], ident[:, :])
                last.then_inc(s_trans, 1)

            def message(g, s):
                pe.wait_ge(s_outT, g + 1)
                if later(g):
                    pe.wait_ge(s_silu, g - 1)
                for k in range(G):
                    last = M.matmul(m_ps[s][:, k * D:(k + 1) * D], outer_T[s][:, k, :], wmsg_sb[:, :],
                                    start=True, stop=True)
                last.then_inc(s_mps, 1)

            def add_by_src(g, s):
                for q, (k0, k1) in enumerate(SUB):
                    pe.wait_ge(s_ready["l3"], 2 * g + q + 1)
                    for k in range(k0, k1):
                        last = add(acc_src, hot_lane[:, s, k, :],
                                   moving[:, q, (k - k0) * NW * D:(k - k0 + 1) * NW * D])
                    last.then_inc(s_used["l3"], 1)

            def last_layer(g, s, i):
                transpose_outer(g, s)
                if not_first(g):
                    add_by_src(g - 1, 1 - s)
                message(g, s)
            pairs(pe, last_layer)
            add_by_src(NG - 1, 1)
            close()

            operand_ready()
            transposes(lambda w: nb[:, w, :], D)
            operand_ready()
            for w in range(NW):
                last = M.matmul(misc[:, w * D:(w + 1) * D], nodeT[0:D, w, :], wmlin_sb[:, :], start=True, stop=True)
            last.then_inc(s_posed, 1)
            operand_ready()
            pairs_flat = moving[:, :, :].rearrange("p s m -> p (s m)")
            transposes(lambda w: pairs_flat[:, w * P:(w + 1) * P], P)
            operand_ready()
            transposes(lambda w: pairs_flat[:, (NW + w) * P:(NW + w + 1) * P], P)
            operand_ready()
            for w in range(NW):
                for half in range(2):
                    j = 2 * w + half
                    last = M.matmul(misc[:, w * D:(w + 1) * D], big[:, j * P:(j + 1) * P], wupd_sb[:, half, :],
                                    start=(half == 0), stop=(half == 1))
            last.then_inc(s_posed, 1)
            operand_ready()
            transposes(lambda w: nb[:, w, :], D)
            operand_ready()
            for w in range(NW):
                last = M.matmul(misc[:, w * D:(w + 1) * D], nodeT[0:D, w, :], wulin_sb[:, :], start=True, stop=True)
            last.then_inc(s_posed, 1)


def kernel(x, src, dst, edge_attr_16, edge_attr_8, edge_type_230, edge_type_8, node_vec1, L1_gnn_W1, L1_gnn_root1,
           L1_gnn_b1, L1_gnn_W2, L1_gnn_root2, L1_gnn_b2, L2_gnn_rel_weight, L2_gnn_loop_weight, L2_gnn_rel_emb,
           L3_gnn_W_msg_tp, L3_gnn_W_msg_lin, L3_gnn_W_upd_tp, L3_gnn_W_upd_lin):
    import numpy as np
    import concourse.bacc as bacc
    from concourse.bass_utils import run_bass_kernel_spmd

    def edges(a, fill):
        a = np.asarray(a)
        pad = np.full((P * T - N_EDGES,) + a.shape[1:], fill, a.dtype)
        a = np.concatenate([a, pad]).reshape(T, P, -1)
        return np.ascontiguousarray(a.transpose(1, 0, 2).reshape(P, -1))

    def nodes(a):
        a = np.asarray(a)
        a = np.concatenate([a, np.zeros((P * NW - N_NODES, a.shape[1]), a.dtype)]).reshape(NW, P, -1)
        return np.ascontiguousarray(a.transpose(1, 0, 2).reshape(P, -1))

    past = P * NW - 1
    dst_e = edges(dst, past)
    relw = np.asarray(L2_gnn_rel_weight)
    arrays = {
        "x": nodes(x), "dst": dst_e, "src": edges(src, past), "tile_first": np.ascontiguousarray(dst_e[0:1]),
        "attr16": edges(edge_attr_16, 0), "attr8": edges(edge_attr_8, 0),
        "rel230": edges(edge_type_230, 0), "rel8": edges(edge_type_8, 0),
        "w1": np.asarray(L1_gnn_W1).reshape(R1 * D, H1), "root1": np.asarray(L1_gnn_root1),
        "b1": np.asarray(L1_gnn_b1).reshape(1, H1),
        "w2": np.ascontiguousarray(np.asarray(L1_gnn_W2).transpose(1, 0, 2).reshape(H1, R1 * D)),
        "root2": np.asarray(L1_gnn_root2), "b2": np.asarray(L1_gnn_b2).reshape(1, D),
        "relw": np.ascontiguousarray(relw.transpose(1, 0, 2).reshape(D, TAB)),
        "loopw": np.asarray(L2_gnn_loop_weight), "relemb": np.asarray(L2_gnn_rel_emb).reshape(1, TAB),
        "wmsg": np.asarray(L3_gnn_W_msg_tp).reshape(P, D), "wmlin": np.asarray(L3_gnn_W_msg_lin),
        "wupd": np.asarray(L3_gnn_W_upd_tp).reshape(2 * P, D), "wulin": np.asarray(L3_gnn_W_upd_lin),
    }
    nc = bacc.Bacc("TRN2", target_bir_lowering=False, num_devices=1)
    args = {k: nc.dram_tensor("in_" + k, a.shape, mybir.dt.from_np(a.dtype), kind="ExternalInput").ap()
            for k, a in arrays.items()}
    out = nc.dram_tensor("out", [P, NW * D], F32, kind="ExternalOutput").ap()
    build(nc, out=out, **args)
    r = run_bass_kernel_spmd(nc, [{"in_" + k: a for k, a in arrays.items()}], core_ids=[0])
    got = np.asarray(r.results[0]["out"]).reshape(P, NW, D).transpose(1, 0, 2).reshape(P * NW, D)
    return np.ascontiguousarray(got[:N_NODES])
```

```python
from contextlib import ExitStack

import concourse.bass as bass
from concourse import mybir

F32 = mybir.dt.float32
BF16 = mybir.dt.bfloat16
I32 = mybir.dt.int32
ALU = mybir.AluOpType
ACT = mybir.ActivationFunctionType
AX_X = mybir.AxisListType.X
RMAX = bass.bass_isa.ReduceOp.max

P = 128
N_NODES = 3125
N_EDGES = 103125
NW = -(-N_NODES // P)
T = -(-N_EDGES // P)
G = 13
NG = T // G
assert T % G == 0 and NG % 2 == 0
RUN = 3
RUNS = -(-G // RUN)
D = 16
R1 = 8
H1 = 32
R2 = 230
A8 = 8
BANK = 512
WIDE = NW * R1 * D
BN = P // R1
NB = P * NW // BN
BW = P // BN
F = D + 1
BANK_B = BANK // F - 1
BANKS_B = -(-NB // BANK_B)
SUMS_B = BANKS_B * BANK_B
SHIFT = P - BN
MOVE = SUMS_B * F
TAB = R2 * D
CH = (TAB + D) // 8
LAST_TAB = TAB - 7 * CH

K1 = D + 1
KX = 3 * K1
KS = 2 * KX

C = 0.01
EPS = 1e-6
MIN_NORM = 1e-10
BALL_EPS = 1e-5
LN_EPS = 1e-5
MAXN = (1.0 - BALL_EPS) / 0.1
SMALL_ATANH = 0.2
SUB = [(0, 7), (7, G)]


def build(nc, x, dst, src, tile_first, attr16, attr8, rel230, rel8, w1, root1, b1, w2, root2, b2,
          relw, loopw, relemb, wmsg, wmlin, wupd, wulin, out):
    x_table = nc.dram_tensor("x_table", [P * NW, D], F32, kind="Internal").ap()
    y_table = nc.dram_tensor("y_table", [P * NW * R1, D], F32, kind="Internal").ap()
    t_table = nc.dram_tensor("t_table", [P * NW * R2, D], F32, kind="Internal").ap()
    z_table = nc.dram_tensor("z_table", [P * NW, D], F32, kind="Internal").ap()

    ctx = ExitStack()
    with ctx:
        def sb(name, shape, dt=F32):
            return ctx.enter_context(nc.sbuf_tensor(name, shape, dt))

        def sem(name):
            return ctx.enter_context(nc.semaphore(name))

        rel_f = sb("rel_f", [P, T])
        rel230_f = sb("rel230_f", [P, T])
        dst_key = sb("dst_key", [P, T])
        dst_blk = sb("dst_blk", [P, T])
        src_lane = sb("src_lane", [P, T])
        src_win = sb("src_win", [P, T])
        src_row = sb("src_row", [P, T])
        dst_row = sb("dst_row", [P, T])
        gather_row = sb("gather_row", [P, T], I32)
        first_off = sb("first_off", [P, NG, RUNS], I32)
        big = sb("big", [P, T * D])
        weights_big = sb("weights_big", [P, TAB + D])
        moving = sb("moving", [P, 2, MOVE])
        hot_lane = sb("hot_lane", [P, 2, G, P])
        rows = sb("rows", [P, 2, G, D])
        row_index = sb("row_index", [P, 2, G], I32)
        hot_small = sb("hot_small", [P, G * NW])
        hot_wide = sb("hot_wide", [P, NB])
        sq_e = sb("sq_e", [P, G, D])
        msg = sb("msg", [P, 2, G, D + 1])
        col = {n: sb("e_" + n, [P, G]) for n in ("ss", "ssc", "z", "t", "rz", "u", "a", "q", "f")}

        count = sb("count", [P, 2 * P])
        select = sb("select", [P, R1 + 1, P + SHIFT])
        lane = sb("lane", [P, P])
        part = sb("part", [P, 1])
        ident = sb("ident", [P, P])
        zeros = sb("zeros", [P, BANK])
        flag = sb("flag", [P, 4])
        flag_i = sb("flag_i", [P, 1], I32)
        tick = sb("tick", [P, 1])
        part_i = sb("part_i", [P, 3], I32)
        part_f = sb("part_f", [P, 3 + R1])
        w1_sb = sb("w1_sb", [P, H1])
        root1_sb = sb("root1_sb", [D + 1, H1])
        w2_sb = sb("w2_sb", [H1 + 1, R1 * D + D])
        wmsg_sb = sb("wmsg_sb", [P, D])
        wmlin_sb = sb("wmlin_sb", [D, D])
        wupd_sb = sb("wupd_sb", [P, 2, D])
        wulin_sb = sb("wulin_sb", [D, D])
        stat = sb("stat", [KS, 2, P], BF16)
        tan_part = sb("tan_part", [P, 3, NW, D + 1], BF16)
        xin = sb("xin", [P, NW, D])
        xc = sb("xc", [P, NW, D])
        na = sb("na", [P, NW, D])
        nb = sb("nb", [P, NW, D])
        ncx = sb("ncx", [P, NW, D])
        x_one = sb("x_one", [P, NW, D + 1])
        h_one = sb("h_one", [P, NW, H1 + 1])
        base2 = sb("base2", [P, NW, D])
        loopv = sb("loopv", [P, NW, D])
        inv_key = sb("inv_key", [P, NB])
        deg = sb("deg", [P, NW])
        w_node = sb("w_node", [P, NW])
        nodeT = sb("nodeT", [H1 + 1, NW, P])
        s_ = {n: sb("n_" + n, [P, NW]) for n in ("a", "b", "c", "d", "e", "f", "g", "h")}

        acc = ctx.enter_context(nc.psum_tensor("acc", [P, 7 * BANK], F32))
        misc = ctx.enter_context(nc.psum_tensor("misc", [P, BANK], F32))

        acc_bank = acc[:, :].rearrange("p (b c) -> p b c", c=BANK)
        node_sums = misc[:, 0:NW * F].rearrange("p (w f) -> p w f", f=F)
        sums_b = moving[:, 0, 0:SUMS_B * F].rearrange("p (b f) -> p b f", f=F)
        acc_src = acc[:, 0:NW * D]
        zt_ps = acc[:, BANK:5 * BANK]
        m_ps = [acc[:, 5 * BANK:5 * BANK + G * D], acc[:, 6 * BANK:6 * BANK + G * D]]
        attr16_sb = big[:, :].rearrange("p (t d) -> p t d", d=D)
        stage = [big[:, 0:TAB], big[:, TAB:2 * TAB]]
        w_rows = weights_big[0:K1, :]
        w_part = [big[0:K1, i * (TAB + D) // 2:(i + 1) * (TAB + D) // 2].bitcast(BF16) for i in range(3)]
        w_high_mid = weights_big[0:KS, 0:(TAB + D) // 2].bitcast(BF16)
        w_low = weights_big[0:KX, (TAB + D) // 2:TAB + D].bitcast(BF16)
        tan_stack = moving[:, 0, 0:NW * KS].rearrange("p (w q) -> p w q", w=NW)
        tan_stack_T = moving[0:KS, 1, 0:NW * P // 2].bitcast(BF16).rearrange("p (w e) -> p w e", w=NW)
        attr8_sb = big[:, 0:T * A8].rearrange("p (t d) -> p t d", d=A8)
        outer_e = [big[:, T * A8 + s * G * P:T * A8 + (s + 1) * G * P] for s in range(2)]
        outer_T = [weights_big[:, s * G * P:(s + 1) * G * P].rearrange("p (k e) -> p k e", e=P) for s in range(2)]
        int_a = moving[:, 0, 0:T].bitcast(I32)
        int_b = moving[:, 0, T:2 * T].bitcast(I32)
        int_c = moving[:, 0, 2 * T:3 * T].bitcast(I32)
        int_d = moving[:, 0, 3 * T:4 * T].bitcast(I32)
        int_e = moving[:, 1, 0:T].bitcast(I32)
        int_t = moving[:, 1, T:2 * T].bitcast(I32)
        flt_w = moving[:, 1, 2 * T:3 * T]
        flt_t = moving[:, 1, 3 * T:4 * T]
        flt_u = moving[:, 1, T:2 * T]

        s_edges = sem("edges_loaded")
        s_attr16 = sem("attr16_loaded")
        s_weights = sem("weights_loaded")
        s_attr8 = sem("attr8_loaded")
        s_consts = sem("constants_ready")
        s_iota = sem("iotas_ready")
        s_violation = sem("violation_ready")
        s_allviol = sem("violation_reduced")
        s_flag = sem("flag_ready")
        s_dve = sem("vector_step")
        s_toact = sem("node_operand_ready")
        s_fromact = sem("node_function_ready")
        s_topose = sem("node_operand_for_tensor")
        s_posed = sem("node_product_ready")
        s_seen = sem("row_index_seen")
        s_tangent = sem("tangent_transposed")
        s_wsplit = sem("weight_parts_ready")
        s_wstack = sem("weight_parts_stacked")
        s_table = sem("table_source_ready")
        s_written = sem("table_written")
        s_index = sem("gather_rows_ready")
        s_staged = sem("row_index_staged")
        s_landed = {ph: [sem(f"rows_landed_{ph}_{s}") for s in range(2)] for ph in ("l1a", "l1b", "l2", "l3")}
        PH = ("l0", "l1a", "l1b", "l2", "l3")
        s_ready = {ph: sem(f"messages_ready_{ph}") for ph in PH}
        s_used = {ph: sem(f"messages_used_{ph}") for ph in PH}
        s_wready = {ph: sem(f"wide_ready_{ph}") for ph in PH}
        s_wused = {ph: sem(f"wide_used_{ph}") for ph in PH}
        s_step = {ph: sem(f"message_step_{ph}") for ph in PH}
        s_summed = sem("sums_complete")
        s_sumread = sem("sums_read")
        s_norm = sem("squared_norms_ready")
        s_tanh = sem("tanh_ready")
        s_stat = sem("table_operand_ready")
        s_tabps = sem("table_product_ready")
        s_ev_a = sem("table_evacuated_by_scalar")
        s_ev_v = sem("table_evacuated_by_vector")
        s_tabst = [sem(f"table_stored_{s}") for s in range(2)]
        s_outer = sem("outer_ready")
        s_trans = sem("outer_transposed")
        s_outT = sem("outer_T_ready")
        s_mps = sem("message_product_ready")
        s_silu = sem("message_silu_ready")
        s_out = sem("output_ready")
        s_done = sem("output_stored")

        block = ctx.enter_context(nc.Block())

        def pairs(eng, body, peel=2):
            for g in range(peel):
                body(g, g % 2, g // 2)
            with eng.Fori(peel // 2, NG // 2) as i:
                body(2 * i, 0, i)
                body(2 * i + 1, 1, i)

        def windows(eng, body):
            body(0, 0, 0)
            body(1, 1, 0)
            with eng.Fori(1, NW // 2) as i:
                body(2 * i, 0, i)
                body(2 * i + 1, 1, i)
            body(NW - 1, 0, NW // 2)

        def later(g):
            return not isinstance(g, int) or g >= 2

        def not_first(g):
            return not isinstance(g, int) or g >= 1

        def at(g):
            return bass.ds(g * G, G)

        COLUMNS = {"l0": F, "l1a": D, "l1b": D, "l2": F}

        means_b = moving[:, 1, 0:NB * D].rearrange("p (b d) -> p b d", d=D)

        def rel_ps(r):
            return misc[:, 0:NW * D] if r == R1 - 1 else acc[:, r * BANK:r * BANK + NW * D]

        def near(s):
            return moving[:, s, 0:G * 2 * F].rearrange("p (k b f) -> p k b f", b=2, f=F)

        def wide(s):
            return moving[:, s, 0:NB * F].rearrange("p (b f) -> p b f", f=F)

        @block.sync
        def _(sp):
            for to, frm in ((int_a, dst), (int_b, src), (int_c, rel8), (int_d, rel230),
                            (int_e, tile_first.partition_broadcast(P))):
                sp.dma_start(to, frm).then_inc(s_edges, 16)
            sp.dma_start(xin[:, :, :].rearrange("p w d -> p (w d)"), x).then_inc(s_edges, 16)
            sp.dma_start(big[:, :], attr16).then_inc(s_attr16, 16)
            sp.wait_ge(s_consts, 1)
            for to, frm in ((w1_sb[:, :], w1), (root1_sb[0:D, :], root1), (root1_sb[D:D + 1, :], b1),
                            (w2_sb[0:H1, 0:R1 * D], w2), (w2_sb[0:H1, R1 * D:], root2),
                            (w2_sb[H1:H1 + 1, R1 * D:], b2),
                            (weights_big[0:D, 0:TAB], relw), (weights_big[D:D + 1, 0:TAB], relemb),
                            (weights_big[0:D, TAB:], loopw),
                            (wmsg_sb[:, :], wmsg), (wmlin_sb[:, :], wmlin),
                            (wupd_sb[:, 0, :], wupd[0:P, :]), (wupd_sb[:, 1, :], wupd[P:2 * P, :]),
                            (wulin_sb[:, :], wulin)):
                sp.dma_start(to, frm).then_inc(s_weights, 16)
            sp.wait_ge(s_table, 1)
            sp.dma_start(x_table.rearrange("(p w) d -> p (w d)", p=P),
                         xc[:, :, :].rearrange("p w d -> p (w d)")).then_inc(s_written, 16)
            sp.wait_ge(s_wsplit, 3)
            for q in range(6):
                sp.dma_start(w_high_mid[q * K1:(q + 1) * K1, :], w_part[q // 3]).then_inc(s_wstack, 16)
            for q in range(3):
                sp.dma_start(w_low[q * K1:(q + 1) * K1, :], w_part[2]).then_inc(s_wstack, 16)
            sp.wait_ge(s_table, 2)
            sp.dma_start(y_table.rearrange("(p w) d -> p (w d)", p=P), moving[:, 0, 0:WIDE]).then_inc(s_written, 16)
            t_rows = t_table.rearrange("(p w r) d -> p w (r d)", p=P, w=NW)

            def store(w, s, i):
                sp.wait_ge(s_ev_a, 4 * (w + 1))
                sp.wait_ge(s_ev_v, 4 * (w + 1))
                sp.dma_start(t_rows[:, bass.ds(w, 1), :], stage[s][:, None, :]).then_inc(s_tabst[s], 16)
            windows(sp, store)
            sp.wait_ge(s_tabst[0], 16 * (NW // 2 + 1))
            sp.wait_ge(s_tabst[1], 16 * (NW // 2))
            sp.dma_start(big[:, 0:T * A8], attr8).then_inc(s_attr8, 16)
            sp.wait_ge(s_table, 3)
            sp.dma_start(z_table.rearrange("(p w) d -> p (w d)", p=P),
                         xc[:, :, :].rearrange("p w d -> p (w d)")).then_inc(s_written, 16)
            sp.wait_ge(s_out, 1)
            sp.dma_start(out, xc[:, :, :].rearrange("p w d -> p (w d)")).then_inc(s_done, 16)
            sp.wait_ge(s_done, 16)

        @block.gpsimd
        def _(pool):
            nc.gpsimd.iota(count[:, :], [[1, 2 * P]], base=0, channel_multiplier=0,
                           allow_small_or_imprecise_dtypes=True)
            nc.gpsimd.iota(lane[:, :], [[1, P]], base=0, channel_multiplier=0, allow_small_or_imprecise_dtypes=True)
            nc.gpsimd.iota(part[:, :], [[0, 1]], base=0, channel_multiplier=1,
                           allow_small_or_imprecise_dtypes=True).then_inc(s_iota, 1)
            pool.wait_ge(s_violation, 1)
            nc.gpsimd.partition_all_reduce(flag[:, 1:2], flag[:, 0:1], P, RMAX).then_inc(s_allviol, 1)

            def gather(n, ph, table):
                def group(g, s, i):
                    if later(g):
                        pool.wait_ge(s_ready[ph] if ph != "l3" else s_outer, g - 1)
                        pool.wait_ge(s_landed[ph][s], 16 * G * i)
                    nc.gpsimd.tensor_copy(row_index[:, s, :], gather_row[:, at(g)]).then_inc(s_staged, 1)
                    pool.wait_ge(s_staged, n * NG + g + 1)
                    pool.sem_inc(s_seen, 1)
                    for k in range(G):
                        nc.gpsimd.indirect_dma_start(
                            out=rows[:, s, k, :], out_offset=None, in_=table,
                            in_offset=bass.IndirectOffsetOnAxis(ap=row_index[:, s, k:k + 1], axis=0),
                        ).then_inc(s_landed[ph][s], 16)
                pairs(pool, group)
                pool.wait_ge(s_landed[ph][0], 16 * G * NG // 2)
                pool.wait_ge(s_landed[ph][1], 16 * G * NG // 2)

            pool.wait_ge(s_index, 1)
            pool.wait_ge(s_written, 16)
            gather(0, "l1a", x_table)
            pool.wait_ge(s_index, 2)
            pool.wait_ge(s_written, 32)
            gather(1, "l1b", y_table)

            pool.wait_ge(s_tangent, 1)

            def operand(w, s, i):
                if later(w):
                    pool.wait_ge(s_tabps, 8 * (w - 1))
                nc.gpsimd.tensor_copy(stat[:, s, :], tan_stack_T[:, bass.ds(w, 1), :].rearrange("p o e -> p (o e)")
                                      ).then_inc(s_stat, 1)
            windows(pool, operand)
            pool.wait_ge(s_index, 3)
            pool.wait_ge(s_tabst[0], 16 * (NW // 2 + 1))
            pool.wait_ge(s_tabst[1], 16 * (NW // 2))
            gather(2, "l2", t_table)
            pool.wait_ge(s_index, 4)
            pool.wait_ge(s_written, 48)
            gather(3, "l3", z_table)

        @block.scalar
        def _(act):
            served = [0]

            def function(out_, in_, func, scale=1.0):
                served[0] += 1
                act.wait_ge(s_toact, served[0])
                nc.scalar.activation(out_, in_, func, scale=scale).then_inc(s_fromact, 1)

            function(s_["g"][:, :], s_["f"][:, :], ACT.Sqrt)
            function(s_["d"][:, :], s_["c"][:, :], ACT.Sqrt)
            function(s_["d"][:, :], s_["c"][:, :], ACT.Sqrt)
            function(s_["c"][:, :], s_["b"][:, :], ACT.Sqrt, scale=C)
            function(s_["g"][:, :], s_["f"][:, :], ACT.Ln)

            def evacuate(w, s, i):
                if later(w):
                    act.wait_ge(s_tabst[s], 16 * i)
                for c in (0, 2, 4, 6):
                    act.wait_ge(s_tabps, 8 * w + c + 1)
                    nc.scalar.copy(stage[s][:, c * CH:(c + 1) * CH], acc[:, c * BANK:c * BANK + CH]).then_inc(s_ev_a, 1)
            windows(act, evacuate)

            function(s_["c"][:, :], s_["b"][:, :], ACT.Sqrt, scale=C)
            function(s_["d"][:, :], s_["c"][:, :], ACT.Tanh)

            def hyperbolic(g, s, i):
                act.wait_ge(s_norm, g + 1)
                nc.scalar.activation(col["z"][:, :], col["ssc"][:, :], ACT.Sqrt, scale=C).then_inc(s_tanh, 1)
                act.wait_ge(s_tanh, 2 * g + 1)
                nc.scalar.activation(col["t"][:, :], col["z"][:, :], ACT.Tanh).then_inc(s_tanh, 1)
            pairs(act, hyperbolic)
            function(s_["c"][:, :], s_["b"][:, :], ACT.Sqrt)
            function(s_["d"][:, :], s_["c"][:, :], ACT.Sqrt)

            def last_layer(g, s, i):
                if later(g):
                    act.wait_ge(s_mps, g - 1)
                act.wait_ge(s_trans, g + 1)
                for c in range(0, G, 4):
                    n = min(4, G - c)
                    last = nc.scalar.copy(outer_T[s][:, c:c + n, :].rearrange("p k e -> p (k e)"),
                                          zt_ps[:, c * P:(c + n) * P])
                last.then_inc(s_outT, 1)
                act.wait_ge(s_mps, g + 1)
                if later(g):
                    act.wait_ge(s_ready["l3"], 2 * (g - 1))
                nc.scalar.activation(msg[:, s, :, 0:D], m_ps[s].rearrange("p (k d) -> p k d", d=D), ACT.Silu,
                                     scale=float((D * A8) ** -0.5)).then_inc(s_silu, 1)
            pairs(act, last_layer)
            function(nb[:, :, :], misc[:, 0:NW * D].rearrange("p (w d) -> p w d", d=D), ACT.Silu,
                     scale=float((D * D) ** -0.5))
            function(s_["d"][:, :], s_["c"][:, :], ACT.Sqrt)

        @block.vector
        def _(dve):
            V = nc.vector
            steps = [0]
            asked = [0]

            def link(ins):
                steps[0] += 1
                ins.then_inc(s_dve, 1)
                dve.wait_ge(s_dve, steps[0])

            def to_act(ins):
                asked[0] += 1
                ins.then_inc(s_toact, 1)
                dve.wait_ge(s_fromact, asked[0])

            def bc(ap, n):
                return ap[:, :, None].to_broadcast([P, ap.shape[1], n])

            def layer_norm(v):
                link(V.reduce_sum(s_["a"][:, :], v, AX_X))
                link(V.tensor_scalar(s_["a"][:, :], s_["a"][:, :], 1.0 / D, None, ALU.mult))
                link(V.tensor_tensor(na[:, :, :], v, bc(s_["a"], D), ALU.subtract))
                link(V.tensor_tensor(ncx[:, :, :], na[:, :, :], na[:, :, :], ALU.mult))
                link(V.reduce_sum(s_["b"][:, :], ncx[:, :, :], AX_X))
                to_act(V.tensor_scalar(s_["c"][:, :], s_["b"][:, :], 1.0 / D, LN_EPS, ALU.mult, ALU.add))
                link(V.reciprocal(s_["e"][:, :], s_["d"][:, :]))
                link(V.tensor_tensor(xc[:, :, :], na[:, :, :], bc(s_["e"], D), ALU.mult))

            link(V.memset(zeros[:, :], 0.0))
            link(V.memset(w2_sb[:, :], 0.0))
            link(V.memset(x_one[:, :, :], 1.0))
            link(V.memset(h_one[:, :, :], 1.0))
            V.memset(weights_big[:, TAB:], 0.0).then_inc(s_consts, 1)
            dve.wait_ge(s_iota, 1)
            V.tensor_scalar(ident[:, :], lane[:, :], part[:, 0:1], None, ALU.is_equal).then_inc(s_topose, 1)
            dve.wait_ge(s_edges, 6 * 16)

            def bits(to, ids, op, n):
                link(V.tensor_scalar(int_t, ids, n, None, op))
                link(V.tensor_copy(to, int_t))
            SHR = ALU.arith_shift_right
            bits(dst_key[:, :], int_a, ALU.bitwise_and, BN - 1)
            bits(dst_blk[:, :], int_a, SHR, BN.bit_length() - 1)
            bits(flt_w, int_e, SHR, BN.bit_length() - 1)
            bits(src_row[:, :], int_a, ALU.bitwise_and, P - 1)
            bits(flt_t, int_a, SHR, P.bit_length() - 1)
            link(V.scalar_tensor_tensor(dst_row[:, :], src_row[:, :], float(NW), flt_t, ALU.mult, ALU.add))
            bits(src_lane[:, :], int_b, ALU.bitwise_and, P - 1)
            bits(src_win[:, :], int_b, SHR, P.bit_length() - 1)
            link(V.tensor_copy(rel_f[:, :], int_c))
            link(V.tensor_copy(rel230_f[:, :], int_d))
            link(V.scalar_tensor_tensor(src_row[:, :], src_lane[:, :], float(NW), src_win[:, :], ALU.mult, ALU.add))
            V.tensor_copy(gather_row[:, :], src_row[:, :]).then_inc(s_index, 1)
            link(V.scalar_tensor_tensor(dst_key[:, :], dst_key[:, :], float(R1), rel_f[:, :], ALU.mult, ALU.add))
            link(V.tensor_tensor(flt_t, dst_blk[:, :], flt_w, ALU.subtract))
            link(V.scalar_tensor_tensor(flt_u, flt_t, -1.0, flt_t, ALU.add, ALU.mult))
            V.reduce_max(flag[:, 0:1], flt_u, AX_X).then_inc(s_violation, 1)
            dve.wait_ge(s_allviol, 1)
            link(V.tensor_scalar(flag[:, 2:3], flag[:, 1:2], 0.0, None, ALU.is_equal))
            link(V.tensor_copy(flag_i[:, :], flag[:, 2:3]))
            link(V.tensor_scalar(flt_w, flt_w, flag[:, 2:3], None, ALU.mult))
            link(V.tensor_tensor(dst_blk[:, :], dst_blk[:, :], flt_w, ALU.subtract))
            link(V.tensor_scalar(flt_t, flt_w, float(BANK_B), None, ALU.is_ge))
            for b in range(2, BANKS_B):
                link(V.scalar_tensor_tensor(flt_t, flt_w, float(b * BANK_B), flt_t, ALU.is_ge, ALU.add))
            link(V.tensor_scalar(flt_t, flt_t, float(BANK - BANK_B * F), None, ALU.mult))
            link(V.scalar_tensor_tensor(flt_t, flt_w, float(F), flt_t, ALU.mult, ALU.add))
            link(V.tensor_copy(first_off[:, :, :], flt_t.rearrange("p (g k) -> p g k", k=G)[:, :, 0:G:RUN]))
            V.memset(tick[:, :], 0.0).then_inc(s_flag, 1)
            link(V.tensor_copy(part_i[:, 0:1], part[:, 0:1]))
            link(V.tensor_scalar(part_i[:, 1:2], part_i[:, 0:1], R1 - 1, None, ALU.bitwise_and))
            link(V.tensor_scalar(part_i[:, 2:3], part_i[:, 0:1], R1.bit_length() - 1, None, SHR))
            link(V.tensor_copy(part_f[:, 0:3], part_i[:, :]))
            link(V.tensor_scalar(part_f[:, 2:3], part_f[:, 2:3], float(SHIFT), None, ALU.add))
            link(V.tensor_scalar(part_f[:, 3:3 + R1], count[:, 0:R1], part_f[:, 1:2], None, ALU.is_equal))
            link(V.tensor_scalar(select[:, R1, :], count[:, 0:P + SHIFT], part_f[:, 2:3], None, ALU.is_equal))
            link(V.tensor_tensor(select[:, 0:R1, :], select[:, R1:R1 + 1, :].to_broadcast([P, R1, P + SHIFT]),
                                 part_f[:, 3:3 + R1][:, :, None].to_broadcast([P, R1, P + SHIFT]), ALU.mult))
            dve.wait_ge(s_flag, 1)
            narrow = dve.value_load(flag_i[0:1, 0:1], min_val=0, max_val=1)

            def hot_of(to, n, keys):
                return V.tensor_tensor(to, count[:, None, 0:n].to_broadcast([P, G, n]),
                                       keys[:, :, None].to_broadcast([P, G, n]), ALU.is_equal)

            NORM_STEPS = 11

            def norms(s, g, base):
                v = rows[:, s, :, :]
                n = [0]

                def step(ins):
                    n[0] += 1
                    ins.then_inc(s_step["l2"], 1)
                    dve.wait_ge(s_step["l2"], base + n[0])
                step(V.tensor_tensor(sq_e[:, :, :], v, v, ALU.mult))
                step(V.reduce_sum(col["ss"][:, :], sq_e[:, :, :], AX_X))
                V.tensor_scalar(col["ssc"][:, :], col["ss"][:, :], MIN_NORM, None, ALU.max).then_inc(s_norm, 1)
                dve.wait_ge(s_tanh, 2 * g + 2)
                step(V.reciprocal(col["rz"][:, :], col["z"][:, :]))
                step(V.tensor_tensor(col["u"][:, :], col["t"][:, :], col["rz"][:, :], ALU.mult))
                step(V.tensor_tensor(col["a"][:, :], col["u"][:, :], col["u"][:, :], ALU.mult))
                step(V.tensor_tensor(col["a"][:, :], col["a"][:, :], col["ss"][:, :], ALU.mult))
                step(V.tensor_scalar(col["q"][:, :], col["a"][:, :], -C, 1.0 + EPS, ALU.mult, ALU.add))
                step(V.reciprocal(col["q"][:, :], col["q"][:, :]))
                step(V.tensor_scalar(msg[:, s, :, D], col["q"][:, :], 2.0, None, ALU.mult))
                step(V.tensor_tensor(col["f"][:, :], msg[:, s, :, D], col["u"][:, :], ALU.mult))
                step(V.tensor_tensor(msg[:, s, :, 0:D], v, bc(col["f"], D), ALU.mult))
                assert n[0] == NORM_STEPS

            def near_messages(ph):
                before = NORM_STEPS if ph == "l2" else 0

                def group(g, s, i):
                    if not_first(g):
                        dve.wait_ge(s_ready[ph], g)
                    if later(g):
                        dve.wait_ge(s_used[ph], g - 1)
                    if ph == "l0":
                        val = attr16_sb[:, at(g), :]
                    else:
                        dve.wait_ge(s_landed[ph][s], 16 * G * (i + 1))
                        val = rows[:, s, :, :]
                    if ph == "l2":
                        norms(s, g, (before + 1) * g)
                        val = msg[:, s, :, :]
                    mv = near(s)
                    f = val.shape[2]
                    blocks = hot_small[:, 0:G * 2].rearrange("p (k b) -> p k b", k=G)
                    hot_of(blocks, 2, dst_blk[:, at(g)]).then_inc(s_step[ph], 1)
                    dve.wait_ge(s_step[ph], (before + 1) * (g + 1))
                    V.tensor_tensor(mv[:, :, :, 0:f], blocks[:, :, :, None].to_broadcast([P, G, 2, f]),
                                    val[:, :, None, :].to_broadcast([P, G, 2, f]), ALU.mult)
                    if ph == "l0":
                        V.tensor_copy(mv[:, :, :, D], blocks)
                    hot_of(hot_lane[:, s, :, :], P, dst_key[:, at(g)]).then_inc(s_ready[ph], 1)
                pairs(dve, group)

            def wide_messages(ph):
                before = NORM_STEPS if ph == "l2" else 0
                hot = hot_wide[:, :]

                def group(g, s, i):
                    if not_first(g):
                        dve.wait_ge(s_ready[ph], g)
                    if later(g):
                        dve.wait_ge(s_wused[ph], G * (g - 1))
                    if ph != "l0":
                        dve.wait_ge(s_landed[ph][s], 16 * G * (i + 1))
                    if ph == "l2":
                        norms(s, g, (before + G) * g)
                    hot_of(hot_lane[:, s, :, :], P, dst_key[:, at(g)])
                    for k in range(G):
                        tile = G * g + k
                        one = bass.ds(tile, 1)
                        val = {"l0": attr16_sb[:, one, :], "l2": msg[:, s, k:k + 1, :]}.get(ph, rows[:, s, k:k + 1, :])
                        f = val.shape[2]
                        if k:
                            dve.wait_ge(s_wready[ph], tile)
                        if not isinstance(g, int) or tile >= 2:
                            dve.wait_ge(s_wused[ph], tile - 1)
                        mv = wide((s * G + k) % 2)
                        V.tensor_tensor(hot, count[:, 0:NB], dst_blk[:, one].to_broadcast([P, NB]),
                                        ALU.is_equal).then_inc(s_step[ph], 1)
                        dve.wait_ge(s_step[ph], (before + G) * g + before + k + 1)
                        if ph == "l0":
                            V.tensor_copy(mv[:, :, D], hot)
                        V.tensor_tensor(mv[:, :, 0:f], hot[:, :, None].to_broadcast([P, NB, f]),
                                        val.to_broadcast([P, NB, f]), ALU.mult).then_inc(s_wready[ph], 1)
                    dve.wait_ge(s_wready[ph], G * (g + 1))
                    V.memset(tick[:, :], 0.0).then_inc(s_ready[ph], 1)
                pairs(dve, group)

            def messages(ph):
                with dve.If(narrow):
                    near_messages(ph)
                with dve.Else():
                    wide_messages(ph)

            def to_tensor(ins):
                posed[0] += 1
                ins.then_inc(s_topose, 1)
                dve.wait_ge(s_posed, posed[0])
            posed = [0]

            def flat(ap):
                return ap.rearrange("p w d -> p (w d)")

            def sums_out(n):
                dve.wait_ge(s_summed, n)
                link(V.tensor_copy(sums_b.rearrange("p (k b) f -> p k (b f)", k=BANKS_B), acc_bank[:, :, 0:BANK_B * F]))
                firsts = sums_b.rearrange("p (k b) f -> p k b f", k=BANKS_B)[:, 1:, 0, :]
                return V.tensor_tensor(firsts, firsts, acc_bank[:, 0:BANKS_B - 1, BANK_B * F:(BANK_B + 1) * F], ALU.add)

            dve.wait_ge(s_attr16, 16)
            messages("l0")
            to_tensor(sums_out(1))
            link(V.tensor_scalar(inv_key[:, :], sums_b[:, 0:NB, D], 1.0, None, ALU.max))
            link(V.reciprocal(inv_key[:, :], inv_key[:, :]))
            link(V.tensor_copy(deg[:, :], node_sums[:, :, D]))
            to_act(V.tensor_scalar(s_["f"][:, :], deg[:, :], 1.0, None, ALU.max))
            link(V.reciprocal(s_["h"][:, :], s_["f"][:, :]))
            link(V.tensor_tensor(na[:, :, :], node_sums[:, :, 0:D], bc(s_["h"], D), ALU.mult))
            link(V.tensor_tensor(nb[:, :, :], na[:, :, :], xin[:, :, :], ALU.add))
            link(V.reciprocal(s_["g"][:, :], s_["g"][:, :]))
            link(V.tensor_tensor(s_["f"][:, :], s_["g"][:, :], deg[:, :], ALU.mult))
            link(V.tensor_scalar(s_["f"][:, :], s_["f"][:, :], EPS, None, ALU.add))
            link(V.reciprocal(s_["f"][:, :], s_["f"][:, :]))
            link(V.tensor_tensor(w_node[:, :], s_["g"][:, :], s_["f"][:, :], ALU.mult))
            layer_norm(nb[:, :, :])
            V.tensor_copy(x_one[:, :, 0:D], xc[:, :, :]).then_inc(s_table, 1)

            dve.wait_ge(s_weights, 14 * 16)
            for i in range(3):
                V.tensor_copy(w_part[i], w_rows).then_inc(s_wsplit, 1)
                if i < 2:
                    dve.wait_ge(s_wsplit, i + 1)
                    link(V.tensor_tensor(w_rows, w_rows, w_part[i], ALU.subtract))

            messages("l1a")
            V.scalar_tensor_tensor(gather_row[:, :], src_row[:, :], float(R1), rel_f[:, :], ALU.mult, ALU.add
                                   ).then_inc(s_index, 1)
            link(sums_out(2))
            to_tensor(V.tensor_tensor(means_b, sums_b[:, 0:NB, 0:D], inv_key[:, :, None].to_broadcast([P, NB, D]), ALU.mult))
            means = moving[:, 0, 0:WIDE].rearrange("p (w r d) -> p w r d", r=R1, d=D)
            for r in range(R1):
                last = V.tensor_copy(means[:, :, r, :], rel_ps(r).rearrange("p (w d) -> p w d", d=D))
            to_tensor(last)
            to_tensor(V.tensor_copy(moving[:, 1, 0:WIDE], acc[:, 0:NW * P]))
            to_tensor(V.tensor_copy(nodeT[0:D + 1, :, :].rearrange("p w e -> p (w e)"), acc[0:D + 1, 0:NW * P]))
            h_ps = acc[:, 0:NW * H1].rearrange("p (w f) -> p w f", f=H1)
            to_tensor(V.tensor_scalar(h_one[:, :, 0:H1], h_ps, 0.0, None, ALU.max))
            to_tensor(V.tensor_copy(nodeT[0:H1 + 1, :, :].rearrange("p w e -> p (w e)"), acc[0:H1 + 1, 0:NW * P]))
            V.tensor_copy(flat(base2[:, :, :]), misc[:, 0:NW * D])
            V.tensor_copy(moving[:, 0, 0:WIDE], acc[:, 0:WIDE]).then_inc(s_table, 1)
            dve.wait_ge(s_table, 2)
            V.memset(tick[:, :], 0.0).then_inc(s_sumread, 1)

            dve.wait_ge(s_written, 32)
            messages("l1b")
            V.scalar_tensor_tensor(gather_row[:, :], src_row[:, :], float(R2), rel230_f[:, :], ALU.mult, ALU.add
                                   ).then_inc(s_index, 1)
            link(sums_out(3))
            to_tensor(V.tensor_tensor(means_b, sums_b[:, 0:NB, 0:D], inv_key[:, :, None].to_broadcast([P, NB, D]), ALU.mult))
            link(V.tensor_tensor(flat(nb[:, :, :]), misc[:, 0:NW * D], flat(base2[:, :, :]), ALU.add))
            link(V.tensor_tensor(nb[:, :, :], nb[:, :, :], xc[:, :, :], ALU.add))
            layer_norm(nb[:, :, :])

            link(V.tensor_tensor(na[:, :, :], xc[:, :, :], xc[:, :, :], ALU.mult))
            link(V.reduce_sum(s_["a"][:, :], na[:, :, :], AX_X))
            to_act(V.tensor_scalar(s_["b"][:, :], s_["a"][:, :], MIN_NORM, None, ALU.max))
            link(V.tensor_scalar(s_["d"][:, :], s_["c"][:, :], 1.0 - BALL_EPS, -1.0 + BALL_EPS, ALU.min, ALU.max))
            link(V.tensor_scalar(s_["e"][:, :], s_["d"][:, :], 1.0, None, ALU.add))
            link(V.tensor_scalar(s_["a"][:, :], s_["d"][:, :], -1.0, 1.0, ALU.mult, ALU.add))
            link(V.reciprocal(s_["a"][:, :], s_["a"][:, :]))
            to_act(V.tensor_tensor(s_["f"][:, :], s_["e"][:, :], s_["a"][:, :], ALU.mult))
            link(V.reciprocal(s_["h"][:, :], s_["c"][:, :]))
            link(V.scalar_tensor_tensor(s_["e"][:, :], s_["g"][:, :], 0.5, s_["h"][:, :], ALU.mult, ALU.mult))
            link(V.tensor_tensor(s_["f"][:, :], s_["d"][:, :], s_["d"][:, :], ALU.mult))
            link(V.tensor_scalar(s_["a"][:, :], s_["f"][:, :], 1.0 / 13, 1.0 / 11, ALU.mult, ALU.add))
            for k in (9, 7, 5, 3, 1):
                link(V.tensor_tensor(s_["a"][:, :], s_["a"][:, :], s_["f"][:, :], ALU.mult))
                link(V.tensor_scalar(s_["a"][:, :], s_["a"][:, :], 1.0 / k, None, ALU.add))
            link(V.tensor_scalar(s_["b"][:, :], s_["c"][:, :], SMALL_ATANH, None, ALU.is_lt))
            link(V.tensor_tensor(s_["a"][:, :], s_["a"][:, :], s_["e"][:, :], ALU.subtract))
            link(V.tensor_tensor(s_["a"][:, :], s_["a"][:, :], s_["b"][:, :], ALU.mult))
            link(V.tensor_tensor(s_["e"][:, :], s_["e"][:, :], s_["a"][:, :], ALU.add))
            link(V.tensor_tensor(x_one[:, :, 0:D], xc[:, :, :], bc(s_["e"], D), ALU.mult))
            for i in range(3):
                link(V.tensor_copy(tan_part[:, i, :, :], x_one[:, :, :]))
                if i < 2:
                    link(V.tensor_tensor(x_one[:, :, :], x_one[:, :, :], tan_part[:, i, :, :], ALU.subtract))
            for q in range(6):
                last = V.tensor_copy(tan_stack[:, :, q * K1:(q + 1) * K1], tan_part[:, q % 3, :, :])
            to_tensor(last)
            V.tensor_copy(tan_stack_T.rearrange("p w e -> p (w e)"), acc[0:KS, 0:NW * P]).then_inc(s_tangent, 1)

            def evacuate(w, s, i):
                if later(w):
                    dve.wait_ge(s_tabst[s], 16 * i)
                for c in (1, 3, 5):
                    dve.wait_ge(s_tabps, 8 * w + c + 1)
                    V.tensor_copy(stage[s][:, c * CH:(c + 1) * CH], acc[:, c * BANK:c * BANK + CH]).then_inc(s_ev_v, 1)
                dve.wait_ge(s_tabps, 8 * w + 8)
                V.tensor_copy(loopv[:, bass.ds(w, 1), :].rearrange("p o d -> p (o d)"), misc[:, LAST_TAB:CH])
                V.tensor_copy(stage[s][:, 7 * CH:TAB], misc[:, 0:LAST_TAB]).then_inc(s_ev_v, 1)
            windows(dve, evacuate)
            dve.wait_ge(s_ev_v, 4 * NW)
            link(V.tensor_tensor(na[:, :, :], loopv[:, :, :], loopv[:, :, :], ALU.mult))
            link(V.reduce_sum(s_["a"][:, :], na[:, :, :], AX_X))
            to_act(V.tensor_scalar(s_["b"][:, :], s_["a"][:, :], MIN_NORM, None, ALU.max))
            to_act(V.memset(tick[:, :], 0.0))
            link(V.reciprocal(s_["c"][:, :], s_["c"][:, :]))
            link(V.tensor_tensor(s_["c"][:, :], s_["c"][:, :], s_["d"][:, :], ALU.mult))
            link(V.tensor_tensor(loopv[:, :, :], loopv[:, :, :], bc(s_["c"], D), ALU.mult))
            V.memset(tick[:, :], 0.0).then_inc(s_sumread, 1)

            messages("l2")
            V.tensor_copy(gather_row[:, :], dst_row[:, :]).then_inc(s_index, 1)
            to_tensor(sums_out(4))
            link(V.tensor_tensor(s_["a"][:, :], w_node[:, :], node_sums[:, :, D], ALU.mult))
            link(V.tensor_scalar(s_["a"][:, :], s_["a"][:, :], EPS, None, ALU.add))
            link(V.reciprocal(s_["a"][:, :], s_["a"][:, :]))
            link(V.tensor_tensor(s_["a"][:, :], s_["a"][:, :], w_node[:, :], ALU.mult))
            link(V.tensor_tensor(nb[:, :, :], node_sums[:, :, 0:D], bc(s_["a"], D), ALU.mult))
            link(V.tensor_tensor(na[:, :, :], nb[:, :, :], nb[:, :, :], ALU.mult))
            link(V.reduce_sum(s_["a"][:, :], na[:, :, :], AX_X))
            to_act(V.tensor_scalar(s_["b"][:, :], s_["a"][:, :], MIN_NORM, None, ALU.max))
            link(V.reciprocal(s_["d"][:, :], s_["c"][:, :]))
            link(V.tensor_scalar(s_["d"][:, :], s_["d"][:, :], MAXN, 1.0, ALU.mult, ALU.min))
            link(V.tensor_tensor(nb[:, :, :], nb[:, :, :], bc(s_["d"], D), ALU.mult))
            link(V.tensor_tensor(na[:, :, :], nb[:, :, :], nb[:, :, :], ALU.mult))
            link(V.reduce_sum(s_["a"][:, :], na[:, :, :], AX_X))
            link(V.tensor_tensor(na[:, :, :], loopv[:, :, :], loopv[:, :, :], ALU.mult))
            link(V.reduce_sum(s_["b"][:, :], na[:, :, :], AX_X))
            link(V.tensor_tensor(na[:, :, :], loopv[:, :, :], nb[:, :, :], ALU.mult))
            link(V.reduce_sum(s_["c"][:, :], na[:, :, :], AX_X))
            link(V.tensor_scalar(s_["c"][:, :], s_["c"][:, :], 2 * C, 1.0, ALU.mult, ALU.add))
            link(V.scalar_tensor_tensor(s_["e"][:, :], s_["b"][:, :], C, s_["c"][:, :], ALU.mult, ALU.add))
            link(V.tensor_tensor(s_["f"][:, :], s_["a"][:, :], s_["b"][:, :], ALU.mult))
            link(V.scalar_tensor_tensor(s_["f"][:, :], s_["f"][:, :], C * C, s_["c"][:, :], ALU.mult, ALU.add))
            link(V.tensor_scalar(s_["f"][:, :], s_["f"][:, :], MIN_NORM, None, ALU.max))
            link(V.reciprocal(s_["f"][:, :], s_["f"][:, :]))
            link(V.tensor_scalar(s_["a"][:, :], s_["a"][:, :], -C, 1.0, ALU.mult, ALU.add))
            link(V.tensor_tensor(nb[:, :, :], nb[:, :, :], bc(s_["e"], D), ALU.mult))
            link(V.tensor_tensor(na[:, :, :], loopv[:, :, :], bc(s_["a"], D), ALU.mult))
            link(V.tensor_tensor(nb[:, :, :], nb[:, :, :], na[:, :, :], ALU.add))
            link(V.tensor_tensor(nb[:, :, :], nb[:, :, :], bc(s_["f"], D), ALU.mult))
            link(V.tensor_tensor(nb[:, :, :], nb[:, :, :], xc[:, :, :], ALU.add))
            layer_norm(nb[:, :, :])
            V.memset(tick[:, :], 0.0).then_inc(s_table, 1)
            dve.wait_ge(s_table, 3)
            V.memset(tick[:, :], 0.0).then_inc(s_sumread, 1)

            dve.wait_ge(s_attr8, 16)
            hot_src = hot_small[:, :].rearrange("p (k w) -> p k w", k=G)

            def outer(g, s, i):
                dve.wait_ge(s_landed["l3"][s], 16 * G * (i + 1))
                if later(g):
                    dve.wait_ge(s_trans, g - 1)
                V.tensor_tensor(outer_e[s].rearrange("p (k i j) -> p k i j", i=D, j=A8),
                                rows[:, s, :, :][:, :, :, None].to_broadcast([P, G, D, A8]),
                                attr8_sb[:, at(g), :][:, :, None, :].to_broadcast([P, G, D, A8]), ALU.mult
                                ).then_inc(s_outer, 1)

            def by_src(g, s):
                if not_first(g):
                    dve.wait_ge(s_ready["l3"], 2 * g)
                if later(g):
                    dve.wait_ge(s_used["l3"], 2 * g - 2)
                hot_of(hot_src, NW, src_win[:, at(g)])
                hot_of(hot_lane[:, s, :, :], P, src_lane[:, at(g)]).then_inc(s_step["l3"], 1)
                dve.wait_ge(s_step["l3"], g + 1)
                dve.wait_ge(s_silu, g + 1)
                for q, (k0, k1) in enumerate(SUB):
                    if not_first(g):
                        dve.wait_ge(s_used["l3"], 2 * g - 1 + q)
                    n = k1 - k0
                    V.tensor_tensor(moving[:, q, 0:n * NW * D].rearrange("p (k w d) -> p k w d", w=NW, d=D),
                                    hot_src[:, k0:k1, :][:, :, :, None].to_broadcast([P, n, NW, D]),
                                    msg[:, s, k0:k1, 0:D][:, :, None, :].to_broadcast([P, n, NW, D]), ALU.mult
                                    ).then_inc(s_ready["l3"], 1)

            def last_layer(g, s, i):
                outer(g, s, i)
                if later(g):
                    by_src(g - 2, s)
            pairs(dve, last_layer, peel=4)
            by_src(NG - 2, 0)
            by_src(NG - 1, 1)
            dve.wait_ge(s_summed, 5)

            lin = float(D ** -0.5)
            to_tensor(V.tensor_copy(flat(nb[:, :, :]), acc_src))
            to_tensor(V.tensor_copy(nodeT[0:D, :, :].rearrange("p w e -> p (w e)"), acc[0:D, 0:NW * P]))
            link(V.tensor_scalar(flat(na[:, :, :]), misc[:, 0:NW * D], lin, None, ALU.mult))
            pair_of = moving[:, :, :].rearrange("p s m -> p (s m)")[:, 0:NW * D * D]
            to_tensor(V.tensor_tensor(pair_of.rearrange("p (w i h) -> p w i h", i=D, h=D),
                                      xc[:, :, :, None].to_broadcast([P, NW, D, D]),
                                      na[:, :, None, :].to_broadcast([P, NW, D, D]), ALU.mult))
            to_tensor(V.tensor_copy(big[:, 0:NW * P], acc[:, 0:NW * P]))
            to_tensor(V.tensor_copy(big[:, NW * P:2 * NW * P], acc[:, 0:NW * P]))
            to_act(V.memset(tick[:, :], 0.0))
            to_tensor(V.memset(tick[:, :], 0.0))
            to_tensor(V.tensor_copy(nodeT[0:D, :, :].rearrange("p w e -> p (w e)"), acc[0:D, 0:NW * P]))
            link(V.tensor_scalar(flat(nb[:, :, :]), misc[:, 0:NW * D], lin, None, ALU.mult))
            link(V.scalar_tensor_tensor(nb[:, :, :], xc[:, :, :], 2.0, nb[:, :, :], ALU.mult, ALU.add))
            layer_norm(nb[:, :, :])
            V.memset(tick[:, :], 0.0).then_inc(s_out, 1)

        @block.tensor
        def _(pe):
            M = nc.tensor
            pe.wait_ge(s_topose, 1)
            pe.wait_ge(s_flag, 1)
            narrow = pe.value_load(flag_i[0:1, 0:1], min_val=0, max_val=1)
            turn = [1]
            loads = [0]

            def clear(banks):
                for b in range(banks):
                    M.matmul(acc[:, b * BANK:(b + 1) * BANK], zeros[:, 0:P], zeros[:, :], start=True, stop=True)

            def add(to, lanes, mv):
                return M.matmul(to, lanes, mv, start=False, stop=False, skip_group_check=True)

            def close():
                M.matmul(acc[:, 0:P], zeros[:, 0:P], zeros[:, 0:P], start=False, stop=True,
                         skip_group_check=True).then_inc(s_summed, 1)

            def scatter(ph):
                f = COLUMNS[ph]

                def near_group(g, s, i):
                    loads[0] += 1
                    first = [pe.alloc_register(f"first_column_{loads[0]}_{k}") for k in range(RUNS)]
                    pe.load(first, first_off[0:1, bass.ds(g, 1), :])
                    cols = [pe.snap(r, donate=True, min_val=0, max_val=7 * BANK - 2 * F) for r in first]
                    pe.wait_ge(s_ready[ph], g + 1)
                    for k in range(G):
                        to = acc[:, bass.ds(cols[k // RUN], 2 * F)].rearrange("p (b f) -> p b f", f=F)
                        last = add(to[:, :, 0:f], hot_lane[:, s, k, :], near(s)[:, k, :, 0:f])
                    last.then_inc(s_used[ph], 1)

                def wide_group(g, s, i):
                    for k in range(G):
                        pe.wait_ge(s_wready[ph], G * g + k + 1)
                        mv = wide((s * G + k) % 2)
                        for b in range(BANKS_B):
                            n = min(BANK_B, NB - b * BANK_B)
                            to = acc_bank[:, b, 0:n * F].rearrange("p (b f) -> p b f", f=F)
                            last = add(to[:, :, 0:f], hot_lane[:, s, k, :], mv[:, b * BANK_B:b * BANK_B + n, 0:f])
                        last.then_inc(s_wused[ph], 1)
                clear(BANKS_B)
                with pe.If(narrow):
                    pairs(pe, near_group)
                with pe.Else():
                    pairs(pe, wide_group)
                close()

            def to_nodes(to, of, r):
                for b in range(BW):
                    last = M.matmul(to, select[:, r, SHIFT - BN * b:SHIFT - BN * b + P],
                                    of[:, b:NB:BW, :], start=(b == 0), stop=(b == BW - 1))
                return last

            def operand_ready():
                turn[0] += 1
                pe.wait_ge(s_topose, turn[0])

            def transposes(block_of, n):
                for w in range(NW):
                    last = M.transpose(acc[0:n, w * P:(w + 1) * P], block_of(w), ident[:, :])
                last.then_inc(s_posed, 1)

            scatter("l0")
            operand_ready()
            to_nodes(misc[:, 0:NW * F], sums_b, R1).then_inc(s_posed, 1)
            scatter("l1a")
            pe.wait_ge(s_weights, 14 * 16)
            operand_ready()
            for r in range(R1):
                last = to_nodes(rel_ps(r), means_b, r)
            last.then_inc(s_posed, 1)
            operand_ready()
            transposes(lambda w: moving[:, 0, w * P:(w + 1) * P], P)
            operand_ready()
            transposes(lambda w: x_one[:, w, :], D + 1)
            operand_ready()
            for w in range(NW):
                h_w = acc[:, w * H1:(w + 1) * H1]
                M.matmul(h_w, moving[:, 1, w * P:(w + 1) * P], w1_sb[:, :], start=True, stop=False)
                last = M.matmul(h_w, nodeT[0:D + 1, w, :], root1_sb[:, :], start=False, stop=True)
            last.then_inc(s_posed, 1)
            operand_ready()
            transposes(lambda w: h_one[:, w, :], H1 + 1)
            operand_ready()
            for w in range(NW):
                M.matmul(acc[:, w * P:(w + 1) * P], nodeT[0:H1 + 1, w, :], w2_sb[:, 0:R1 * D], start=True, stop=True)
                last = M.matmul(misc[:, w * D:(w + 1) * D], nodeT[0:H1 + 1, w, :], w2_sb[:, R1 * D:], start=True, stop=True)
            last.then_inc(s_posed, 1)
            pe.wait_ge(s_sumread, 1)
            scatter("l1b")
            operand_ready()
            to_nodes(misc[:, 0:NW * D], means_b, R1).then_inc(s_posed, 1)
            operand_ready()
            transposes(lambda w: tan_stack[:, w, :], KS)
            pe.wait_ge(s_wstack, 16 * 9)

            def table(w, s, i):
                pe.wait_ge(s_stat, w + 1)
                for c in range(8):
                    if not_first(w):
                        if c % 2:
                            pe.wait_ge(s_ev_v, 4 * (w - 1) + c // 2 + 1)
                        else:
                            pe.wait_ge(s_ev_a, 4 * (w - 1) + c // 2 + 1)
                    to = misc[:, 0:CH] if c == 7 else acc[:, c * BANK:c * BANK + CH]
                    M.matmul(to, stat[:, s, :], w_high_mid[:, c * CH:(c + 1) * CH], start=True, stop=False)
                    M.matmul(to, stat[0:KX, s, :], w_low[:, c * CH:(c + 1) * CH], start=False, stop=True
                             ).then_inc(s_tabps, 1)
            windows(pe, table)
            pe.wait_ge(s_sumread, 2)
            scatter("l2")
            operand_ready()
            to_nodes(misc[:, 0:NW * F], sums_b, R1).then_inc(s_posed, 1)
            clear(1)

            def transpose_outer(g, s):
                pe.wait_ge(s_outer, g + 1)
                if not_first(g):
                    pe.wait_ge(s_outT, g)
                for k in range(G):
                    last = M.transpose(zt_ps[:, k * P:(k + 1) * P], outer_e[s][:, k * P:(k + 1) * P], ident[:, :])
                last.then_inc(s_trans, 1)

            def message(g, s):
                pe.wait_ge(s_outT, g + 1)
                if later(g):
                    pe.wait_ge(s_silu, g - 1)
                for k in range(G):
                    last = M.matmul(m_ps[s][:, k * D:(k + 1) * D], outer_T[s][:, k, :], wmsg_sb[:, :],
                                    start=True, stop=True)
                last.then_inc(s_mps, 1)

            def add_by_src(g, s):
                for q, (k0, k1) in enumerate(SUB):
                    pe.wait_ge(s_ready["l3"], 2 * g + q + 1)
                    for k in range(k0, k1):
                        last = add(acc_src, hot_lane[:, s, k, :],
                                   moving[:, q, (k - k0) * NW * D:(k - k0 + 1) * NW * D])
                    last.then_inc(s_used["l3"], 1)

            def last_layer(g, s, i):
                transpose_outer(g, s)
                if later(g):
                    add_by_src(g - 2, s)
                message(g, s)
            pairs(pe, last_layer, peel=4)
            add_by_src(NG - 2, 0)
            add_by_src(NG - 1, 1)
            close()

            operand_ready()
            transposes(lambda w: nb[:, w, :], D)
            operand_ready()
            for w in range(NW):
                last = M.matmul(misc[:, w * D:(w + 1) * D], nodeT[0:D, w, :], wmlin_sb[:, :], start=True, stop=True)
            last.then_inc(s_posed, 1)
            operand_ready()
            pairs_flat = moving[:, :, :].rearrange("p s m -> p (s m)")
            transposes(lambda w: pairs_flat[:, w * P:(w + 1) * P], P)
            operand_ready()
            transposes(lambda w: pairs_flat[:, (NW + w) * P:(NW + w + 1) * P], P)
            operand_ready()
            for w in range(NW):
                for half in range(2):
                    j = 2 * w + half
                    last = M.matmul(misc[:, w * D:(w + 1) * D], big[:, j * P:(j + 1) * P], wupd_sb[:, half, :],
                                    start=(half == 0), stop=(half == 1))
            last.then_inc(s_posed, 1)
            operand_ready()
            transposes(lambda w: nb[:, w, :], D)
            operand_ready()
            for w in range(NW):
                last = M.matmul(misc[:, w * D:(w + 1) * D], nodeT[0:D, w, :], wulin_sb[:, :], start=True, stop=True)
            last.then_inc(s_posed, 1)


def kernel(x, src, dst, edge_attr_16, edge_attr_8, edge_type_230, edge_type_8, node_vec1, L1_gnn_W1, L1_gnn_root1,
           L1_gnn_b1, L1_gnn_W2, L1_gnn_root2, L1_gnn_b2, L2_gnn_rel_weight, L2_gnn_loop_weight, L2_gnn_rel_emb,
           L3_gnn_W_msg_tp, L3_gnn_W_msg_lin, L3_gnn_W_upd_tp, L3_gnn_W_upd_lin):
    import numpy as np
    import concourse.bacc as bacc
    from concourse.bass_utils import run_bass_kernel_spmd

    def edges(a, fill):
        a = np.asarray(a)
        pad = np.full((P * T - N_EDGES,) + a.shape[1:], fill, a.dtype)
        a = np.concatenate([a, pad]).reshape(T, P, -1)
        return np.ascontiguousarray(a.transpose(1, 0, 2).reshape(P, -1))

    def nodes(a):
        a = np.asarray(a)
        a = np.concatenate([a, np.zeros((P * NW - N_NODES, a.shape[1]), a.dtype)]).reshape(NW, P, -1)
        return np.ascontiguousarray(a.transpose(1, 0, 2).reshape(P, -1))

    past = (N_NODES - 1) | (BN - 1)
    assert past >= N_NODES
    dst_e = edges(dst, past)
    run_first = np.repeat(dst_e[0].reshape(NG, G)[:, ::RUN], RUN, axis=1)[:, :G].reshape(1, T)
    relw = np.asarray(L2_gnn_rel_weight)
    arrays = {
        "x": nodes(x), "dst": dst_e, "src": edges(src, past), "tile_first": run_first,
        "attr16": edges(edge_attr_16, 0), "attr8": edges(edge_attr_8, 0),
        "rel230": edges(edge_type_230, 0), "rel8": edges(edge_type_8, 0),
        "w1": np.asarray(L1_gnn_W1).reshape(R1 * D, H1), "root1": np.asarray(L1_gnn_root1),
        "b1": np.asarray(L1_gnn_b1).reshape(1, H1),
        "w2": np.ascontiguousarray(np.asarray(L1_gnn_W2).transpose(1, 0, 2).reshape(H1, R1 * D)),
        "root2": np.asarray(L1_gnn_root2), "b2": np.asarray(L1_gnn_b2).reshape(1, D),
        "relw": np.ascontiguousarray(relw.transpose(1, 0, 2).reshape(D, TAB)),
        "loopw": np.asarray(L2_gnn_loop_weight), "relemb": np.asarray(L2_gnn_rel_emb).reshape(1, TAB),
        "wmsg": np.asarray(L3_gnn_W_msg_tp).reshape(P, D), "wmlin": np.asarray(L3_gnn_W_msg_lin),
        "wupd": np.asarray(L3_gnn_W_upd_tp).reshape(2 * P, D), "wulin": np.asarray(L3_gnn_W_upd_lin),
    }
    nc = bacc.Bacc("TRN2", target_bir_lowering=False, num_devices=1)
    args = {k: nc.dram_tensor("in_" + k, a.shape, mybir.dt.from_np(a.dtype), kind="ExternalInput").ap()
            for k, a in arrays.items()}
    out = nc.dram_tensor("out", [P, NW * D], F32, kind="ExternalOutput").ap()
    build(nc, out=out, **args)
    r = run_bass_kernel_spmd(nc, [{"in_" + k: a for k, a in arrays.items()}], core_ids=[0])
    got = np.asarray(r.results[0]["out"]).reshape(P, NW, D).transpose(1, 0, 2).reshape(P * NW, D)
    return np.ascontiguousarray(got[:N_NODES])
```

```python
from contextlib import ExitStack

import concourse.bass as bass
from concourse import mybir

F32 = mybir.dt.float32
BF16 = mybir.dt.bfloat16
I32 = mybir.dt.int32
ALU = mybir.AluOpType
ACT = mybir.ActivationFunctionType
AX_X = mybir.AxisListType.X
RMAX = bass.bass_isa.ReduceOp.max

P = 128
N_NODES = 3125
N_EDGES = 103125
NW = -(-N_NODES // P)
T = -(-N_EDGES // P)
G = 13
NG = T // G
assert T % G == 0 and NG % 2 == 0
ON_CHIP = {"l1a": 4}
FEED = 3
MAX_ON = max(ON_CHIP.values())
RUN = 3
RUNS = -(-G // RUN)
D = 16
R1 = 8
H1 = 32
R2 = 230
A8 = 8
BANK = 512
WIDE = NW * R1 * D
BN = P // R1
NB = P * NW // BN
BW = P // BN
F = D + 1
BANK_B = BANK // F - 1
BANKS_B = -(-NB // BANK_B)
SUMS_B = BANKS_B * BANK_B
BN0 = 32
NB0 = P * NW // BN0
BW0 = P // BN0
F0 = D + R1
BANK_B0 = BANK // F0 - 1
BANKS_B0 = -(-NB0 // BANK_B0)
assert NB0 % BANKS_B0 == 0 and NB0 // BANKS_B0 == BANK_B0
NB_HALF = NB // 2
SHIFT0 = P - BN0
SHIFT = P - BN
MOVE = SUMS_B * F
TAB = R2 * D
CH = (TAB + D) // 8
LAST_TAB = TAB - 7 * CH

K1 = D + 1
KX = 3 * K1
KS = 2 * KX

C = 0.01
EPS = 1e-6
MIN_NORM = 1e-10
BALL_EPS = 1e-5
LN_EPS = 1e-5
MAXN = (1.0 - BALL_EPS) / 0.1
SMALL_ATANH = 0.2
SUB = [(0, 7), (7, G)]


def build(nc, x, dst, src, src_flat, tile_first, attr16, attr8, rel230, rel8, w1, root1, b1, w2, root2, b2,
          relw, loopw, relemb, wmsg, wmlin, wupd, wulin, out):
    x_table = nc.dram_tensor("x_table", [P * NW, D], F32, kind="Internal").ap()
    y_table = nc.dram_tensor("y_table", [P * NW * R1, D], F32, kind="Internal").ap()
    t_table = nc.dram_tensor("t_table", [P * NW * R2, D], F32, kind="Internal").ap()
    z_table = nc.dram_tensor("z_table", [P * NW, D], F32, kind="Internal").ap()

    inv_table = nc.dram_tensor("inv_table", [P * NW, R1], F32, kind="Internal").ap()
    lane_rows = nc.dram_tensor("lane_rows", [P, T], BF16, kind="Internal").ap()

    ctx = ExitStack()
    with ctx:
        def sb(name, shape, dt=F32):
            return ctx.enter_context(nc.sbuf_tensor(name, shape, dt))

        def sem(name):
            return ctx.enter_context(nc.semaphore(name))

        rel_f = sb("rel_f", [P, T])
        rel230_f = sb("rel230_f", [P, T])
        dst_key = sb("dst_key", [P, T])
        dst_blk = sb("dst_blk", [P, T])
        dst_key0 = sb("dst_key0", [P, T])
        dst_blk0 = sb("dst_blk0", [P, T])
        first_off0 = sb("first_off0", [P, NG, RUNS], I32)
        select0 = sb("select0", [BN0, P + SHIFT0])
        inv_rel = sb("inv_rel", [P, NW, R1])
        inv_T = sb("inv_T", [NB_HALF, 2, P])
        src_lane = sb("src_lane", [P, T])
        src_win = sb("src_win", [P, T])
        src_row = sb("src_row", [P, T])
        dst_row = sb("dst_row", [P, T])
        gather_row = sb("gather_row", [P, T], I32)
        first_off = sb("first_off", [P, NG, RUNS], I32)
        big = sb("big", [P, T * D])
        weights_big = sb("weights_big", [P, TAB + D])
        moving = sb("moving", [P, 2, MOVE])
        hot_lane = sb("hot_lane", [P, 2, G, P])
        rows = sb("rows", [P, 2, G, D])
        row_index = sb("row_index", [P, 2, G], I32)
        hot_small = sb("hot_small", [P, G * NW])
        hot_wide = sb("hot_wide", [P, NB])
        hot_window = sb("hot_window", [P, MAX_ON, NW])
        sq_e = sb("sq_e", [P, G, D])
        msg = sb("msg", [P, 2, G, D + 1])
        col = {n: sb("e_" + n, [P, G]) for n in ("ss", "ssc", "z", "t", "rz", "u", "a", "q", "f")}

        count = sb("count", [P, 2 * P])
        select = sb("select", [P, R1 + 1, P + SHIFT])
        lane = sb("lane", [P, P])
        part = sb("part", [P, 1])
        ident = sb("ident", [P, P])
        zeros = sb("zeros", [P, BANK])
        flag = sb("flag", [P, 4])
        flag_i = sb("flag_i", [P, 1], I32)
        tick = sb("tick", [P, 1])
        part_i = sb("part_i", [P, 3], I32)
        part_f = sb("part_f", [P, 3 + R1])
        w1_sb = sb("w1_sb", [P, H1])
        root1_sb = sb("root1_sb", [D + 1, H1])
        w2_sb = sb("w2_sb", [H1 + 1, R1 * D + D])
        wmsg_sb = sb("wmsg_sb", [P, D])
        wmlin_sb = sb("wmlin_sb", [D, D])
        wupd_sb = sb("wupd_sb", [P, 2, D])
        wulin_sb = sb("wulin_sb", [D, D])
        stat = sb("stat", [KS, 2, P], BF16)
        tan_part = sb("tan_part", [P, 3, NW, D + 1], BF16)
        xin = sb("xin", [P, NW, D])
        xc = sb("xc", [P, NW, D])
        na = sb("na", [P, NW, D])
        nb = sb("nb", [P, NW, D])
        ncx = sb("ncx", [P, NW, D])
        x_one = sb("x_one", [P, NW, D + 1])
        base2 = sb("base2", [P, NW, D])
        loopv = sb("loopv", [P, NW, D])
        inv_key = sb("inv_key", [P, NB])
        deg = sb("deg", [P, NW])
        w_node = sb("w_node", [P, NW])
        nodeT = sb("nodeT", [H1 + 1, NW, P])
        s_ = {n: sb("n_" + n, [P, NW]) for n in ("a", "b", "c", "d", "e", "f", "g", "h")}

        acc = ctx.enter_context(nc.psum_tensor("acc", [P, 7 * BANK], F32))
        misc = ctx.enter_context(nc.psum_tensor("misc", [P, BANK], F32))

        acc_bank = acc[:, :].rearrange("p (b c) -> p b c", c=BANK)
        node_sums = misc[:, 0:NW * F].rearrange("p (w f) -> p w f", f=F)
        sums_0 = moving[0:BN0, 0, 0:NB0 * F0].rearrange("p (b f) -> p b f", f=F0)
        counts_ps = acc[:, BANKS_B0 * BANK:BANKS_B0 * BANK + NW * R1]
        sums_b = moving[:, 0, 0:SUMS_B * F].rearrange("p (b f) -> p b f", f=F)
        acc_src = acc[:, 0:NW * D]
        zt_ps = acc[:, BANK:5 * BANK]
        m_ps = [acc[:, 5 * BANK:5 * BANK + G * D], acc[:, 6 * BANK:6 * BANK + G * D]]
        attr16_sb = big[:, :].rearrange("p (t d) -> p t d", d=D)
        stage = [big[:, 0:TAB], big[:, TAB:2 * TAB]]
        w_rows = weights_big[0:K1, :]
        w_part = [big[0:K1, i * (TAB + D) // 2:(i + 1) * (TAB + D) // 2].bitcast(BF16) for i in range(3)]
        w_high_mid = weights_big[0:KS, 0:(TAB + D) // 2].bitcast(BF16)
        w_low = weights_big[0:KX, (TAB + D) // 2:TAB + D].bitcast(BF16)
        tan_stack = moving[:, 0, 0:NW * KS].rearrange("p (w q) -> p w q", w=NW)
        tan_stack_T = moving[0:KS, 1, 0:NW * P // 2].bitcast(BF16).rearrange("p (w e) -> p w e", w=NW)
        attr8_sb = big[:, 0:T * A8].rearrange("p (t d) -> p t d", d=A8)
        outer_e = [big[:, T * A8 + s * G * P:T * A8 + (s + 1) * G * P] for s in range(2)]
        outer_T = [weights_big[:, s * G * P:(s + 1) * G * P].rearrange("p (k e) -> p k e", e=P) for s in range(2)]
        own = 2 * G * P + T * A8
        hot_T = [big[:, own + s * MAX_ON * P // 2:own + (s + 1) * MAX_ON * P // 2].bitcast(BF16) for s in range(2)]
        own += MAX_ON * P
        lane_row = [big[:, own + s * MAX_ON * P // 2:own + (s + 1) * MAX_ON * P // 2].bitcast(BF16) for s in range(2)]
        own += MAX_ON * P
        all_windows = [big[:, own + s * NW * D:own + (s + 1) * NW * D] for s in range(2)]
        own += 2 * NW * D
        x_part = [big[:, own + i * NW * D // 2:own + (i + 1) * NW * D // 2].bitcast(BF16) for i in range(3)]
        own += 3 * NW * D // 2
        assert own <= T * D
        hot_flat = hot_lane[:, :, :, :].rearrange("p s k e -> p (s k e)")
        flat_i = hot_flat[:, 0:T].bitcast(I32)
        flat_b = hot_flat[:, T:T + T // 2].bitcast(BF16)
        int_a = moving[:, 0, 0:T].bitcast(I32)
        int_b = moving[:, 0, T:2 * T].bitcast(I32)
        int_c = moving[:, 0, 2 * T:3 * T].bitcast(I32)
        int_d = moving[:, 0, 3 * T:4 * T].bitcast(I32)
        int_e = moving[:, 1, 0:T].bitcast(I32)
        int_t = moving[:, 1, T:2 * T].bitcast(I32)
        flt_w = moving[:, 1, 2 * T:3 * T]
        flt_t = moving[:, 1, 3 * T:4 * T]
        flt_u = moving[:, 1, T:2 * T]

        s_edges = sem("edges_loaded")
        s_attr16 = sem("attr16_loaded")
        s_weights = sem("weights_loaded")
        s_attr8 = sem("attr8_loaded")
        s_consts = sem("constants_ready")
        s_iota = sem("iotas_ready")
        s_violation = sem("violation_ready")
        s_allviol = sem("violation_reduced")
        s_flag = sem("flag_ready")
        s_dve = sem("vector_step")
        s_toact = sem("node_operand_ready")
        s_fromact = sem("node_function_ready")
        s_topose = sem("node_operand_for_tensor")
        s_posed = sem("node_product_ready")
        s_seen = sem("row_index_seen")
        s_tangent = sem("tangent_transposed")
        s_wsplit = sem("weight_parts_ready")
        s_wstack = sem("weight_parts_stacked")
        s_table = sem("table_source_ready")
        s_written = sem("table_written")
        s_index = sem("gather_rows_ready")
        s_staged = sem("row_index_staged")
        s_landed = {ph: [sem(f"rows_landed_{ph}_{s}") for s in range(2)] for ph in ("l1a", "l1b", "l2", "l3")}
        PH = ("l0", "l1a", "l1b", "l2", "l3")
        s_ready = {ph: sem(f"messages_ready_{ph}") for ph in PH}
        s_used = {ph: sem(f"messages_used_{ph}") for ph in PH}
        s_wready = {ph: sem(f"wide_ready_{ph}") for ph in PH}
        s_wused = {ph: sem(f"wide_used_{ph}") for ph in PH}
        s_step = {ph: sem(f"message_step_{ph}") for ph in PH}
        s_summed = sem("sums_complete")
        s_sumread = sem("sums_read")
        s_norm = sem("squared_norms_ready")
        s_tanh = sem("tanh_ready")
        s_stat = sem("table_operand_ready")
        s_tabps = sem("table_product_ready")
        s_ev_a = sem("table_evacuated_by_scalar")
        s_ev_v = sem("table_evacuated_by_vector")
        s_tabst = [sem(f"table_stored_{s}") for s in range(2)]
        s_outer = sem("outer_ready")
        s_trans = sem("outer_transposed")
        s_outT = sem("outer_T_ready")
        s_mps = sem("message_product_ready")
        s_silu = sem("message_silu_ready")
        s_out = sem("output_ready")
        s_done = sem("output_stored")

        s_inv = sem("inverse_counts_ready")
        s_invst = sem("inverse_counts_stored")
        s_invld = sem("inverse_counts_loaded")
        s_flat = sem("flat_indices_loaded")
        s_lanes = sem("lane_rows_ready")
        s_lstored = sem("lane_rows_stored")
        s_xpart = sem("feature_parts_ready")
        s_lrow = {ph: [sem(f"lane_row_loaded_{ph}_{s}") for s in range(2)] for ph in ON_CHIP}
        s_hotT = {ph: sem(f"hot_T_ready_{ph}") for ph in ON_CHIP}
        s_allw = {ph: sem(f"all_windows_ready_{ph}") for ph in ON_CHIP}
        s_kept = {ph: sem(f"own_window_kept_{ph}") for ph in ON_CHIP}
        s_hotw = {ph: sem(f"hot_window_ready_{ph}") for ph in ON_CHIP}
        s_row = {ph: sem(f"row_on_chip_ready_{ph}") for ph in ON_CHIP}

        block = ctx.enter_context(nc.Block())

        def pairs(eng, body, peel=2, tail=0):
            for g in range(peel):
                body(g, g % 2, g // 2)
            with eng.Fori(peel // 2, (NG - tail) // 2) as i:
                body(2 * i, 0, i)
                body(2 * i + 1, 1, i)
            for g in range(NG - tail, NG):
                body(g, g % 2, g // 2)

        def windows(eng, body):
            body(0, 0, 0)
            body(1, 1, 0)
            with eng.Fori(1, NW // 2) as i:
                body(2 * i, 0, i)
                body(2 * i + 1, 1, i)
            body(NW - 1, 0, NW // 2)

        def later(g):
            return not isinstance(g, int) or g >= 2

        def not_first(g):
            return not isinstance(g, int) or g >= 1

        def has_next(g, n=1):
            return not isinstance(g, int) or g + n < NG

        def at(g):
            return bass.ds(g * G, G)

        COLUMNS = {"l1a": D, "l1b": D, "l2": F}

        means_b = moving[:, 1, 0:NB * D].rearrange("p (b d) -> p b d", d=D)
        totals_b = sums_b[:, 0:NB, 0:D]

        def rel_ps(r):
            return misc[:, 0:NW * D] if r == R1 - 1 else acc[:, r * BANK:r * BANK + NW * D]

        def near(s):
            return moving[:, s, 0:G * 2 * F].rearrange("p (k b f) -> p k b f", b=2, f=F)

        def near0(s):
            return moving[:, s, 0:G * 2 * F0].rearrange("p (k b f) -> p k b f", b=2, f=F0)

        def wide0(s):
            return moving[:, s, 0:NB0 * F0].rearrange("p (b f) -> p b f", f=F0)

        def wide(s):
            return moving[:, s, 0:NB * F].rearrange("p (b f) -> p b f", f=F)

        @block.sync
        def _(sp):
            for to, frm in ((int_a, dst), (int_b, src), (int_c, rel8), (int_d, rel230),
                            (int_e, tile_first.partition_broadcast(P))):
                sp.dma_start(to, frm).then_inc(s_edges, 16)
            sp.dma_start(xin[:, :, :].rearrange("p w d -> p (w d)"), x).then_inc(s_edges, 16)
            sp.dma_start(big[:, :], attr16).then_inc(s_attr16, 16)
            sp.dma_start(flat_i, src_flat).then_inc(s_flat, 16)
            sp.wait_ge(s_consts, 1)
            for to, frm in ((w1_sb[:, :], w1), (root1_sb[0:D, :], root1), (root1_sb[D:D + 1, :], b1),
                            (w2_sb[0:H1, 0:R1 * D], w2), (w2_sb[0:H1, R1 * D:], root2),
                            (w2_sb[H1:H1 + 1, R1 * D:], b2),
                            (weights_big[0:D, 0:TAB], relw), (weights_big[D:D + 1, 0:TAB], relemb),
                            (weights_big[0:D, TAB:], loopw),
                            (wmsg_sb[:, :], wmsg), (wmlin_sb[:, :], wmlin),
                            (wupd_sb[:, 0, :], wupd[0:P, :]), (wupd_sb[:, 1, :], wupd[P:2 * P, :]),
                            (wulin_sb[:, :], wulin)):
                sp.dma_start(to, frm).then_inc(s_weights, 16)
            sp.wait_ge(s_lanes, 1)
            sp.dma_start(lane_rows, flat_b).then_inc(s_lstored, 16)
            sp.wait_ge(s_table, 1)
            sp.dma_start(x_table.rearrange("(p w) d -> p (w d)", p=P),
                         xc[:, :, :].rearrange("p w d -> p (w d)")).then_inc(s_written, 16)
            sp.wait_ge(s_inv, 1)
            sp.dma_start(inv_table.rearrange("(w p) r -> p w r", p=P), inv_rel[:, :, :]).then_inc(s_invst, 16)
            sp.wait_ge(s_invst, 16)
            sp.dma_start(inv_T[:, :, :], inv_table.rearrange("(j q n) r -> q j (n r)", j=2, n=BN)).then_inc(s_invld, 16)
            sp.wait_ge(s_wsplit, 3)
            for q in range(6):
                sp.dma_start(w_high_mid[q * K1:(q + 1) * K1, :], w_part[q // 3]).then_inc(s_wstack, 16)
            for q in range(3):
                sp.dma_start(w_low[q * K1:(q + 1) * K1, :], w_part[2]).then_inc(s_wstack, 16)
            sp.wait_ge(s_lstored, 16)

            def load_lanes(ph):
                n = ON_CHIP[ph]
                flat = lane_rows.rearrange("(o p) t -> o (p t)", o=1).rearrange("o (g e) -> o g e", g=NG)

                def load(g, s, i):
                    if later(g):
                        sp.wait_ge(s_hotT[ph], g - 1)
                    frm = flat[:, bass.ds(g, 1), (G - n) * P:].rearrange("o g e -> o (g e)")
                    sp.dma_start(lane_row[s][:, 0:n * P], frm.partition_broadcast(P)).then_inc(s_lrow[ph][s], 16)
                pairs(sp, load)
            load_lanes("l1a")
            sp.wait_ge(s_table, 2)
            sp.dma_start(y_table.rearrange("(p w) d -> p (w d)", p=P), moving[:, 0, 0:WIDE]).then_inc(s_written, 16)
            t_rows = t_table.rearrange("(p w r) d -> p w (r d)", p=P, w=NW)

            def store(w, s, i):
                sp.wait_ge(s_ev_a, 4 * (w + 1))
                sp.wait_ge(s_ev_v, 4 * (w + 1))
                sp.dma_start(t_rows[:, bass.ds(w, 1), :], stage[s][:, None, :]).then_inc(s_tabst[s], 16)
            windows(sp, store)
            sp.wait_ge(s_tabst[0], 16 * (NW // 2 + 1))
            sp.wait_ge(s_tabst[1], 16 * (NW // 2))
            sp.dma_start(big[:, 0:T * A8], attr8).then_inc(s_attr8, 16)
            sp.wait_ge(s_table, 3)
            sp.dma_start(z_table.rearrange("(p w) d -> p (w d)", p=P),
                         xc[:, :, :].rearrange("p w d -> p (w d)")).then_inc(s_written, 16)
            sp.wait_ge(s_out, 1)
            sp.dma_start(out, xc[:, :, :].rearrange("p w d -> p (w d)")).then_inc(s_done, 16)
            sp.wait_ge(s_done, 16)

        @block.gpsimd
        def _(pool):
            nc.gpsimd.iota(count[:, :], [[1, 2 * P]], base=0, channel_multiplier=0,
                           allow_small_or_imprecise_dtypes=True)
            nc.gpsimd.iota(lane[:, :], [[1, P]], base=0, channel_multiplier=0, allow_small_or_imprecise_dtypes=True)
            nc.gpsimd.iota(part[:, :], [[0, 1]], base=0, channel_multiplier=1,
                           allow_small_or_imprecise_dtypes=True).then_inc(s_iota, 1)
            pool.wait_ge(s_violation, 1)
            nc.gpsimd.partition_all_reduce(flag[:, 1:2], flag[:, 0:1], P, RMAX).then_inc(s_allviol, 1)

            def gather(n, ph, table):
                tiles = G - ON_CHIP.get(ph, 0)

                def group(g, s, i):
                    if later(g):
                        pool.wait_ge(s_ready[ph] if ph != "l3" else s_outer, g - 1)
                        pool.wait_ge(s_landed[ph][s], 16 * tiles * i)
                    nc.gpsimd.tensor_copy(row_index[:, s, :], gather_row[:, at(g)]).then_inc(s_staged, 1)
                    pool.wait_ge(s_staged, n * NG + g + 1)
                    pool.sem_inc(s_seen, 1)
                    for k in range(tiles):
                        nc.gpsimd.indirect_dma_start(
                            out=rows[:, s, k, :], out_offset=None, in_=table,
                            in_offset=bass.IndirectOffsetOnAxis(ap=row_index[:, s, k:k + 1], axis=0),
                        ).then_inc(s_landed[ph][s], 16)
                pairs(pool, group)
                pool.wait_ge(s_landed[ph][0], 16 * tiles * NG // 2)
                pool.wait_ge(s_landed[ph][1], 16 * tiles * NG // 2)

            pool.wait_ge(s_index, 1)
            pool.wait_ge(s_written, 16)
            gather(0, "l1a", x_table)
            pool.wait_ge(s_index, 2)
            pool.wait_ge(s_written, 32)
            gather(1, "l1b", y_table)

            pool.wait_ge(s_tangent, 1)

            def operand(w, s, i):
                if later(w):
                    pool.wait_ge(s_tabps, 8 * (w - 1))
                nc.gpsimd.tensor_copy(stat[:, s, :], tan_stack_T[:, bass.ds(w, 1), :].rearrange("p o e -> p (o e)")
                                      ).then_inc(s_stat, 1)
            windows(pool, operand)
            pool.wait_ge(s_index, 3)
            pool.wait_ge(s_tabst[0], 16 * (NW // 2 + 1))
            pool.wait_ge(s_tabst[1], 16 * (NW // 2))
            gather(2, "l2", t_table)
            pool.wait_ge(s_index, 4)
            pool.wait_ge(s_written, 48)
            gather(3, "l3", z_table)

        @block.scalar
        def _(act):
            served = [0]

            def function(out_, in_, func, scale=1.0):
                served[0] += 1
                act.wait_ge(s_toact, served[0])
                nc.scalar.activation(out_, in_, func, scale=scale).then_inc(s_fromact, 1)

            function(s_["g"][:, :], s_["f"][:, :], ACT.Sqrt)
            function(s_["d"][:, :], s_["c"][:, :], ACT.Sqrt)
            function(s_["d"][:, :], s_["c"][:, :], ACT.Sqrt)
            function(s_["c"][:, :], s_["b"][:, :], ACT.Sqrt, scale=C)
            function(s_["g"][:, :], s_["f"][:, :], ACT.Ln)

            def evacuate(w, s, i):
                if later(w):
                    act.wait_ge(s_tabst[s], 16 * i)
                for c in (0, 2, 4, 6):
                    act.wait_ge(s_tabps, 8 * w + c + 1)
                    nc.scalar.copy(stage[s][:, c * CH:(c + 1) * CH], acc[:, c * BANK:c * BANK + CH]).then_inc(s_ev_a, 1)
            windows(act, evacuate)

            function(s_["c"][:, :], s_["b"][:, :], ACT.Sqrt, scale=C)
            function(s_["d"][:, :], s_["c"][:, :], ACT.Tanh)

            def hyperbolic(g, s, i):
                act.wait_ge(s_norm, g + 1)
                nc.scalar.activation(col["z"][:, :], col["ssc"][:, :], ACT.Sqrt, scale=C).then_inc(s_tanh, 1)
                act.wait_ge(s_tanh, 2 * g + 1)
                nc.scalar.activation(col["t"][:, :], col["z"][:, :], ACT.Tanh).then_inc(s_tanh, 1)
            pairs(act, hyperbolic)
            function(s_["c"][:, :], s_["b"][:, :], ACT.Sqrt)
            function(s_["d"][:, :], s_["c"][:, :], ACT.Sqrt)

            def last_layer(g, s, i):
                if later(g):
                    act.wait_ge(s_mps, g - 1)
                act.wait_ge(s_trans, g + 1)
                for c in range(0, G, 4):
                    n = min(4, G - c)
                    last = nc.scalar.copy(outer_T[s][:, c:c + n, :].rearrange("p k e -> p (k e)"),
                                          zt_ps[:, c * P:(c + n) * P])
                last.then_inc(s_outT, 1)
                act.wait_ge(s_mps, g + 1)
                if later(g):
                    act.wait_ge(s_ready["l3"], 2 * (g - 1))
                nc.scalar.activation(msg[:, s, :, 0:D], m_ps[s].rearrange("p (k d) -> p k d", d=D), ACT.Silu,
                                     scale=float((D * A8) ** -0.5)).then_inc(s_silu, 1)
            pairs(act, last_layer)
            function(nodeT[0:D, :, :].rearrange("p w e -> p (w e)"), acc[0:D, 0:NW * P], ACT.Silu,
                     scale=float((D * D) ** -0.5))
            function(s_["d"][:, :], s_["c"][:, :], ACT.Sqrt)

        @block.vector
        def _(dve):
            V = nc.vector
            steps = [0]
            asked = [0]

            def link(ins):
                steps[0] += 1
                ins.then_inc(s_dve, 1)
                dve.wait_ge(s_dve, steps[0])

            def to_act(ins):
                asked[0] += 1
                ins.then_inc(s_toact, 1)
                dve.wait_ge(s_fromact, asked[0])

            def bc(ap, n):
                return ap[:, :, None].to_broadcast([P, ap.shape[1], n])

            def layer_norm(v):
                link(V.reduce_sum(s_["a"][:, :], v, AX_X))
                link(V.tensor_scalar(s_["a"][:, :], s_["a"][:, :], 1.0 / D, None, ALU.mult))
                link(V.tensor_tensor(na[:, :, :], v, bc(s_["a"], D), ALU.subtract))
                link(V.tensor_tensor(ncx[:, :, :], na[:, :, :], na[:, :, :], ALU.mult))
                link(V.reduce_sum(s_["b"][:, :], ncx[:, :, :], AX_X))
                to_act(V.tensor_scalar(s_["c"][:, :], s_["b"][:, :], 1.0 / D, LN_EPS, ALU.mult, ALU.add))
                link(V.reciprocal(s_["e"][:, :], s_["d"][:, :]))
                link(V.tensor_tensor(xc[:, :, :], na[:, :, :], bc(s_["e"], D), ALU.mult))

            link(V.memset(zeros[:, :], 0.0))
            link(V.memset(w2_sb[:, :], 0.0))
            link(V.memset(x_one[:, :, :], 1.0))
            link(V.memset(nodeT[H1:H1 + 1, :, :], 1.0))
            V.memset(weights_big[:, TAB:], 0.0).then_inc(s_consts, 1)
            dve.wait_ge(s_iota, 1)
            V.tensor_scalar(ident[:, :], lane[:, :], part[:, 0:1], None, ALU.is_equal).then_inc(s_topose, 1)
            dve.wait_ge(s_edges, 6 * 16)

            def bits(to, ids, op, n):
                link(V.tensor_scalar(int_t, ids, n, None, op))
                link(V.tensor_copy(to, int_t))
            SHR = ALU.arith_shift_right
            bits(dst_key[:, :], int_a, ALU.bitwise_and, BN - 1)
            bits(dst_blk[:, :], int_a, SHR, BN.bit_length() - 1)
            bits(flt_w, int_e, SHR, BN.bit_length() - 1)
            bits(dst_key0[:, :], int_a, ALU.bitwise_and, BN0 - 1)
            bits(dst_blk0[:, :], int_a, SHR, BN0.bit_length() - 1)
            bits(src_row[:, :], int_a, ALU.bitwise_and, P - 1)
            bits(flt_t, int_a, SHR, P.bit_length() - 1)
            link(V.scalar_tensor_tensor(dst_row[:, :], src_row[:, :], float(NW), flt_t, ALU.mult, ALU.add))
            bits(src_lane[:, :], int_b, ALU.bitwise_and, P - 1)
            bits(src_win[:, :], int_b, SHR, P.bit_length() - 1)
            link(V.tensor_copy(rel_f[:, :], int_c))
            link(V.tensor_copy(rel230_f[:, :], int_d))
            link(V.scalar_tensor_tensor(src_row[:, :], src_lane[:, :], float(NW), src_win[:, :], ALU.mult, ALU.add))
            V.tensor_copy(gather_row[:, :], src_row[:, :]).then_inc(s_index, 1)
            link(V.scalar_tensor_tensor(dst_key[:, :], dst_key[:, :], float(R1), rel_f[:, :], ALU.mult, ALU.add))
            dve.wait_ge(s_flat, 16)
            link(V.tensor_scalar(int_t, flat_i, P - 1, None, ALU.bitwise_and))
            V.tensor_copy(flat_b, int_t).then_inc(s_lanes, 1)
            dve.wait_ge(s_lanes, 1)
            link(V.tensor_tensor(flt_t, dst_blk[:, :], flt_w, ALU.subtract))
            link(V.scalar_tensor_tensor(flt_u, flt_t, -1.0, flt_t, ALU.add, ALU.mult))
            V.reduce_max(flag[:, 0:1], flt_u, AX_X).then_inc(s_violation, 1)
            dve.wait_ge(s_allviol, 1)
            link(V.tensor_scalar(flag[:, 2:3], flag[:, 1:2], 0.0, None, ALU.is_equal))
            link(V.tensor_copy(flag_i[:, :], flag[:, 2:3]))
            link(V.tensor_scalar(flt_w, flt_w, flag[:, 2:3], None, ALU.mult))
            link(V.tensor_tensor(dst_blk[:, :], dst_blk[:, :], flt_w, ALU.subtract))

            def first_columns(to, bank_b, banks, f):
                link(V.tensor_scalar(flt_t, flt_w, float(bank_b), None, ALU.is_ge))
                for b in range(2, banks):
                    link(V.scalar_tensor_tensor(flt_t, flt_w, float(b * bank_b), flt_t, ALU.is_ge, ALU.add))
                link(V.tensor_scalar(flt_t, flt_t, float(BANK - bank_b * f), None, ALU.mult))
                link(V.scalar_tensor_tensor(flt_t, flt_w, float(f), flt_t, ALU.mult, ALU.add))
                link(V.tensor_copy(to, flt_t.rearrange("p (g k) -> p g k", k=G)[:, :, 0:G:RUN]))
            first_columns(first_off[:, :, :], BANK_B, BANKS_B, F)
            bits(flt_w, int_e, SHR, BN0.bit_length() - 1)
            link(V.tensor_scalar(flt_w, flt_w, flag[:, 2:3], None, ALU.mult))
            link(V.tensor_tensor(dst_blk0[:, :], dst_blk0[:, :], flt_w, ALU.subtract))
            first_columns(first_off0[:, :, :], BANK_B0, BANKS_B0, F0)
            link(V.tensor_scalar(select0[:, :], count[0:BN0, 0:P + SHIFT0], part[0:BN0, 0:1], float(SHIFT0),
                                 ALU.subtract, ALU.is_equal))
            V.memset(tick[:, :], 0.0).then_inc(s_flag, 1)
            link(V.tensor_copy(part_i[:, 0:1], part[:, 0:1]))
            link(V.tensor_scalar(part_i[:, 1:2], part_i[:, 0:1], R1 - 1, None, ALU.bitwise_and))
            link(V.tensor_scalar(part_i[:, 2:3], part_i[:, 0:1], R1.bit_length() - 1, None, SHR))
            link(V.tensor_copy(part_f[:, 0:3], part_i[:, :]))
            link(V.tensor_scalar(part_f[:, 2:3], part_f[:, 2:3], float(SHIFT), None, ALU.add))
            link(V.tensor_scalar(part_f[:, 3:3 + R1], count[:, 0:R1], part_f[:, 1:2], None, ALU.is_equal))
            link(V.tensor_scalar(select[:, R1, :], count[:, 0:P + SHIFT], part_f[:, 2:3], None, ALU.is_equal))
            link(V.tensor_tensor(select[:, 0:R1, :], select[:, R1:R1 + 1, :].to_broadcast([P, R1, P + SHIFT]),
                                 part_f[:, 3:3 + R1][:, :, None].to_broadcast([P, R1, P + SHIFT]), ALU.mult))
            dve.wait_ge(s_flag, 1)
            narrow = dve.value_load(flag_i[0:1, 0:1], min_val=0, max_val=1)

            def hot_of(to, n, keys):
                return V.tensor_tensor(to, count[:, None, 0:n].to_broadcast([P, G, n]),
                                       keys[:, :, None].to_broadcast([P, G, n]), ALU.is_equal)

            NORM_STEPS = 11

            def norms(s, g, base):
                v = rows[:, s, :, :]
                n = [0]

                def step(ins):
                    n[0] += 1
                    ins.then_inc(s_step["l2"], 1)
                    dve.wait_ge(s_step["l2"], base + n[0])
                step(V.tensor_tensor(sq_e[:, :, :], v, v, ALU.mult))
                step(V.reduce_sum(col["ss"][:, :], sq_e[:, :, :], AX_X))
                V.tensor_scalar(col["ssc"][:, :], col["ss"][:, :], MIN_NORM, None, ALU.max).then_inc(s_norm, 1)
                dve.wait_ge(s_tanh, 2 * g + 2)
                step(V.reciprocal(col["rz"][:, :], col["z"][:, :]))
                step(V.tensor_tensor(col["u"][:, :], col["t"][:, :], col["rz"][:, :], ALU.mult))
                step(V.tensor_tensor(col["a"][:, :], col["u"][:, :], col["u"][:, :], ALU.mult))
                step(V.tensor_tensor(col["a"][:, :], col["a"][:, :], col["ss"][:, :], ALU.mult))
                step(V.tensor_scalar(col["q"][:, :], col["a"][:, :], -C, 1.0 + EPS, ALU.mult, ALU.add))
                step(V.reciprocal(col["q"][:, :], col["q"][:, :]))
                step(V.tensor_scalar(msg[:, s, :, D], col["q"][:, :], 2.0, None, ALU.mult))
                step(V.tensor_tensor(col["f"][:, :], msg[:, s, :, D], col["u"][:, :], ALU.mult))
                step(V.tensor_tensor(msg[:, s, :, 0:D], v, bc(col["f"], D), ALU.mult))
                assert n[0] == NORM_STEPS

            def lanes_hot(ph, g, s, i):
                n = ON_CHIP[ph]
                dve.wait_ge(s_lrow[ph][s], 16 * (i + 1))
                if later(g):
                    dve.wait_ge(s_allw[ph], n * (g - 1))
                V.tensor_scalar(hot_T[s][:, 0:n * P], lane_row[s][:, 0:n * P], part[:, 0:1], None, ALU.is_equal
                                ).then_inc(s_hotT[ph], 1)
                if not_first(g):
                    dve.wait_ge(s_kept[ph], n * g)
                V.tensor_tensor(hot_window[:, 0:n, :], count[:, None, 0:NW].to_broadcast([P, n, NW]),
                                src_win[:, bass.ds(g * G + G - n, n)][:, :, None].to_broadcast([P, n, NW]), ALU.is_equal
                                ).then_inc(s_hotw[ph], 1)

            def keep(ph, g, s, k):
                n = ON_CHIP[ph]
                if k == 0:
                    dve.wait_ge(s_hotw[ph], g + 1)
                dve.wait_ge(s_allw[ph], n * g + k + 1)
                if not isinstance(g, int) or n * g + k >= 2:
                    dve.wait_ge(s_row[ph], n * g + k - 1)
                V.tensor_tensor(all_windows[(n * s + k) % 2].rearrange("p (w d) -> p w d", d=D),
                                misc[:, 0:NW * D].rearrange("p (w d) -> p w d", d=D),
                                hot_window[:, k, :][:, :, None].to_broadcast([P, NW, D]), ALU.mult
                                ).then_inc(s_kept[ph], 1)

            def own_row(ph, g, s, k):
                n = ON_CHIP[ph]
                dve.wait_ge(s_kept[ph], n * g + k + 1)
                V.reduce_sum(rows[:, s, G - n + k, :], all_windows[(n * s + k) % 2].rearrange("p (w d) -> p d w", d=D),
                             AX_X).then_inc(s_row[ph], 1)

            def own_rows(ph, g, s):
                n = ON_CHIP[ph]
                for k in range(n):
                    keep(ph, g, s, k)
                    if k:
                        own_row(ph, g, s, k - 1)
                own_row(ph, g, s, n - 1)

            rel_hot = hot_small[:, G * 2:G * (2 + R1)].rearrange("p (k r) -> p k r", k=G)

            def near_first():
                blocks = hot_small[:, 0:G * 2].rearrange("p (k b) -> p k b", k=G)

                def group(g, s, i):
                    if not_first(g):
                        dve.wait_ge(s_ready["l0"], g)
                    if later(g):
                        dve.wait_ge(s_used["l0"], g - 1)
                    hot_of(blocks, 2, dst_blk0[:, at(g)])
                    hot_of(rel_hot, R1, rel_f[:, at(g)]).then_inc(s_step["l0"], 1)
                    hot_of(hot_lane[:, s, :, 0:BN0], BN0, dst_key0[:, at(g)])
                    dve.wait_ge(s_step["l0"], g + 1)
                    for c0, c1, val in ((0, D, attr16_sb[:, at(g), :]), (D, F0, rel_hot)):
                        last = V.tensor_tensor(near0(s)[:, :, :, c0:c1],
                                               blocks[:, :, :, None].to_broadcast([P, G, 2, c1 - c0]),
                                               val[:, :, None, :].to_broadcast([P, G, 2, c1 - c0]), ALU.mult)
                    last.then_inc(s_ready["l0"], 1)
                pairs(dve, group)

            def wide_first():
                hot = hot_wide[:, 0:NB0]

                def group(g, s, i):
                    if not_first(g):
                        dve.wait_ge(s_ready["l0"], g)
                    if later(g):
                        dve.wait_ge(s_wused["l0"], G * (g - 1))
                    hot_of(hot_lane[:, s, :, 0:BN0], BN0, dst_key0[:, at(g)])
                    hot_of(rel_hot, R1, rel_f[:, at(g)])
                    for k in range(G):
                        tile = G * g + k
                        one = bass.ds(tile, 1)
                        if k:
                            dve.wait_ge(s_wready["l0"], tile)
                        if not isinstance(g, int) or tile >= 2:
                            dve.wait_ge(s_wused["l0"], tile - 1)
                        mv = wide0((s * G + k) % 2)
                        V.tensor_tensor(hot, count[:, 0:NB0], dst_blk0[:, one].to_broadcast([P, NB0]),
                                        ALU.is_equal).then_inc(s_step["l0"], 1)
                        dve.wait_ge(s_step["l0"], G * g + k + 1)
                        for c0, c1, val in ((0, D, attr16_sb[:, one, :]), (D, F0, rel_hot[:, k:k + 1, :])):
                            last = V.tensor_tensor(mv[:, :, c0:c1], hot[:, :, None].to_broadcast([P, NB0, c1 - c0]),
                                                   val.to_broadcast([P, NB0, c1 - c0]), ALU.mult)
                        last.then_inc(s_wready["l0"], 1)
                    dve.wait_ge(s_wready["l0"], G * (g + 1))
                    V.memset(tick[:, :], 0.0).then_inc(s_ready["l0"], 1)
                pairs(dve, group)

            def near_messages(ph):
                before = NORM_STEPS if ph == "l2" else 0
                on = ON_CHIP.get(ph, 0)

                def group(g, s, i):
                    if not_first(g):
                        dve.wait_ge(s_ready[ph], g)
                    if on and has_next(g):
                        keep(ph, g + 1, 1 - s, 0)
                    if later(g):
                        dve.wait_ge(s_used[ph], g - 1)
                    dve.wait_ge(s_landed[ph][s], 16 * (G - on) * (i + 1))
                    if on:
                        dve.wait_ge(s_row[ph], on * (g + 1))
                    val = rows[:, s, :, :]
                    if ph == "l2":
                        norms(s, g, (before + 1) * g)
                        val = msg[:, s, :, :]
                    mv = near(s)
                    f = val.shape[2]
                    blocks = hot_small[:, 0:G * 2].rearrange("p (k b) -> p k b", k=G)
                    hot_of(blocks, 2, dst_blk[:, at(g)]).then_inc(s_step[ph], 1)
                    dve.wait_ge(s_step[ph], (before + 1) * (g + 1))
                    V.tensor_tensor(mv[:, :, :, 0:f], blocks[:, :, :, None].to_broadcast([P, G, 2, f]),
                                    val[:, :, None, :].to_broadcast([P, G, 2, f]), ALU.mult)
                    hot_of(hot_lane[:, s, :, :], P, dst_key[:, at(g)]).then_inc(s_ready[ph], 1)
                    if on and has_next(g):
                        for k in range(1, on):
                            keep(ph, g + 1, 1 - s, k)
                            own_row(ph, g + 1, 1 - s, k - 1)
                        own_row(ph, g + 1, 1 - s, on - 1)
                        if has_next(g, 2):
                            lanes_hot(ph, g + 2, s, i + 1)
                if on:
                    lanes_hot(ph, 0, 0, 0)
                    own_rows(ph, 0, 0)
                    lanes_hot(ph, 1, 1, 0)
                pairs(dve, group, tail=2 if on else 0)

            def wide_messages(ph):
                before = NORM_STEPS if ph == "l2" else 0
                hot = hot_wide[:, :]
                on = ON_CHIP.get(ph, 0)

                def group(g, s, i):
                    if not_first(g):
                        dve.wait_ge(s_ready[ph], g)
                    if later(g):
                        dve.wait_ge(s_wused[ph], G * (g - 1))
                    if on:
                        own_rows(ph, g, s)
                        if has_next(g):
                            lanes_hot(ph, g + 1, 1 - s, i + s)
                        dve.wait_ge(s_row[ph], on * (g + 1))
                    dve.wait_ge(s_landed[ph][s], 16 * (G - on) * (i + 1))
                    if ph == "l2":
                        norms(s, g, (before + G) * g)
                    hot_of(hot_lane[:, s, :, :], P, dst_key[:, at(g)])
                    for k in range(G):
                        tile = G * g + k
                        one = bass.ds(tile, 1)
                        val = msg[:, s, k:k + 1, :] if ph == "l2" else rows[:, s, k:k + 1, :]
                        f = val.shape[2]
                        if k:
                            dve.wait_ge(s_wready[ph], tile)
                        if not isinstance(g, int) or tile >= 2:
                            dve.wait_ge(s_wused[ph], tile - 1)
                        mv = wide((s * G + k) % 2)
                        V.tensor_tensor(hot, count[:, 0:NB], dst_blk[:, one].to_broadcast([P, NB]),
                                        ALU.is_equal).then_inc(s_step[ph], 1)
                        dve.wait_ge(s_step[ph], (before + G) * g + before + k + 1)
                        V.tensor_tensor(mv[:, :, 0:f], hot[:, :, None].to_broadcast([P, NB, f]),
                                        val.to_broadcast([P, NB, f]), ALU.mult).then_inc(s_wready[ph], 1)
                    dve.wait_ge(s_wready[ph], G * (g + 1))
                    V.memset(tick[:, :], 0.0).then_inc(s_ready[ph], 1)
                if on:
                    lanes_hot(ph, 0, 0, 0)
                pairs(dve, group, tail=2 if on else 0)

            def messages(ph):
                with dve.If(narrow):
                    near_messages(ph) if ph != "l0" else near_first()
                with dve.Else():
                    wide_messages(ph) if ph != "l0" else wide_first()

            def split_features():
                link(V.tensor_copy(nb[:, :, :], xc[:, :, :]))
                for i in range(3):
                    ins = V.tensor_copy(x_part[i], flat(nb[:, :, :]))
                    if i < 2:
                        link(ins)
                        link(V.tensor_tensor(flat(nb[:, :, :]), flat(nb[:, :, :]), x_part[i], ALU.subtract))
                ins.then_inc(s_xpart, 1)

            def to_tensor(ins):
                posed[0] += 1
                ins.then_inc(s_topose, 1)
                dve.wait_ge(s_posed, posed[0])
            posed = [0]

            def flat(ap):
                return ap.rearrange("p w d -> p (w d)")

            def sums_out(n):
                dve.wait_ge(s_summed, n)
                link(V.tensor_copy(sums_b.rearrange("p (k b) f -> p k (b f)", k=BANKS_B), acc_bank[:, :, 0:BANK_B * F]))
                firsts = sums_b.rearrange("p (k b) f -> p k b f", k=BANKS_B)[:, 1:, 0, :]
                return V.tensor_tensor(firsts, firsts, acc_bank[:, 0:BANKS_B - 1, BANK_B * F:(BANK_B + 1) * F], ALU.add)

            dve.wait_ge(s_attr16, 16)
            dve.wait_ge(s_lstored, 16)
            messages("l0")
            dve.wait_ge(s_summed, 1)
            link(V.tensor_copy(sums_0.rearrange("p (k b) f -> p k (b f)", k=BANKS_B0),
                               acc_bank[0:BN0, 0:BANKS_B0, 0:BANK_B0 * F0]))
            firsts_0 = sums_0.rearrange("p (k b) f -> p k b f", k=BANKS_B0)[:, 1:, 0, :]
            to_tensor(V.tensor_tensor(firsts_0, firsts_0,
                                      acc_bank[0:BN0, 0:BANKS_B0 - 1, BANK_B0 * F0:(BANK_B0 + 1) * F0], ALU.add))
            counts = counts_ps.rearrange("p (w r) -> p w r", r=R1)
            link(V.reduce_sum(deg[:, :], counts, AX_X))
            to_act(V.tensor_scalar(s_["f"][:, :], deg[:, :], 1.0, None, ALU.max))
            link(V.reciprocal(s_["h"][:, :], s_["f"][:, :]))
            link(V.tensor_tensor(na[:, :, :], misc[:, 0:NW * D].rearrange("p (w d) -> p w d", d=D), bc(s_["h"], D), ALU.mult))
            link(V.tensor_tensor(nb[:, :, :], na[:, :, :], xin[:, :, :], ALU.add))
            link(V.reciprocal(s_["g"][:, :], s_["g"][:, :]))
            link(V.tensor_tensor(s_["f"][:, :], s_["g"][:, :], deg[:, :], ALU.mult))
            link(V.tensor_scalar(s_["f"][:, :], s_["f"][:, :], EPS, None, ALU.add))
            link(V.reciprocal(s_["f"][:, :], s_["f"][:, :]))
            link(V.tensor_tensor(w_node[:, :], s_["g"][:, :], s_["f"][:, :], ALU.mult))
            layer_norm(nb[:, :, :])
            V.tensor_copy(x_one[:, :, 0:D], xc[:, :, :]).then_inc(s_table, 1)

            split_features()
            link(V.tensor_scalar(inv_rel[:, :, :], counts, 1.0, None, ALU.max))
            V.reciprocal(inv_rel[:, :, :], inv_rel[:, :, :]).then_inc(s_inv, 1)
            dve.wait_ge(s_inv, 1)
            V.memset(tick[:, :], 0.0).then_inc(s_sumread, 1)

            dve.wait_ge(s_weights, 14 * 16)
            for i in range(3):
                V.tensor_copy(w_part[i], w_rows).then_inc(s_wsplit, 1)
                if i < 2:
                    dve.wait_ge(s_wsplit, i + 1)
                    link(V.tensor_tensor(w_rows, w_rows, w_part[i], ALU.subtract))

            messages("l1a")
            V.scalar_tensor_tensor(gather_row[:, :], src_row[:, :], float(R1), rel_f[:, :], ALU.mult, ALU.add
                                   ).then_inc(s_index, 1)
            to_tensor(sums_out(2))
            means = moving[:, 0, 0:WIDE].rearrange("p (w r d) -> p w r d", r=R1, d=D)
            for r in range(R1):
                last = V.tensor_tensor(means[:, :, r, :], rel_ps(r).rearrange("p (w d) -> p w d", d=D),
                                       inv_rel[:, :, r][:, :, None].to_broadcast([P, NW, D]), ALU.mult)
            to_tensor(last)
            to_tensor(V.tensor_copy(moving[:, 1, 0:WIDE], acc[:, 0:NW * P]))
            to_tensor(V.tensor_copy(nodeT[0:D + 1, :, :].rearrange("p w e -> p (w e)"), acc[0:D + 1, 0:NW * P]))
            to_tensor(V.tensor_scalar(nodeT[0:H1, :, :].rearrange("p w e -> p (w e)"), acc[0:H1, 0:NW * P],
                                      0.0, None, ALU.max))
            V.tensor_copy(flat(base2[:, :, :]), misc[:, 0:NW * D])
            V.tensor_copy(moving[:, 0, 0:WIDE], acc[:, 0:WIDE]).then_inc(s_table, 1)
            dve.wait_ge(s_table, 2)

            to_tensor(V.memset(tick[:, :], 0.0))
            link(V.tensor_copy(inv_key[:, :], misc[:, 0:NB]))
            dve.wait_ge(s_written, 32)
            messages("l1b")
            V.scalar_tensor_tensor(gather_row[:, :], src_row[:, :], float(R2), rel230_f[:, :], ALU.mult, ALU.add
                                   ).then_inc(s_index, 1)
            link(sums_out(3))
            to_tensor(V.tensor_tensor(means_b, sums_b[:, 0:NB, 0:D], inv_key[:, :, None].to_broadcast([P, NB, D]), ALU.mult))
            link(V.tensor_tensor(flat(nb[:, :, :]), misc[:, 0:NW * D], flat(base2[:, :, :]), ALU.add))
            link(V.tensor_tensor(nb[:, :, :], nb[:, :, :], xc[:, :, :], ALU.add))
            layer_norm(nb[:, :, :])

            link(V.tensor_tensor(na[:, :, :], xc[:, :, :], xc[:, :, :], ALU.mult))
            link(V.reduce_sum(s_["a"][:, :], na[:, :, :], AX_X))
            to_act(V.tensor_scalar(s_["b"][:, :], s_["a"][:, :], MIN_NORM, None, ALU.max))
            link(V.tensor_scalar(s_["d"][:, :], s_["c"][:, :], 1.0 - BALL_EPS, -1.0 + BALL_EPS, ALU.min, ALU.max))
            link(V.tensor_scalar(s_["e"][:, :], s_["d"][:, :], 1.0, None, ALU.add))
            link(V.tensor_scalar(s_["a"][:, :], s_["d"][:, :], -1.0, 1.0, ALU.mult, ALU.add))
            link(V.reciprocal(s_["a"][:, :], s_["a"][:, :]))
            to_act(V.tensor_tensor(s_["f"][:, :], s_["e"][:, :], s_["a"][:, :], ALU.mult))
            link(V.reciprocal(s_["h"][:, :], s_["c"][:, :]))
            link(V.scalar_tensor_tensor(s_["e"][:, :], s_["g"][:, :], 0.5, s_["h"][:, :], ALU.mult, ALU.mult))
            link(V.tensor_tensor(s_["f"][:, :], s_["d"][:, :], s_["d"][:, :], ALU.mult))
            link(V.tensor_scalar(s_["a"][:, :], s_["f"][:, :], 1.0 / 13, 1.0 / 11, ALU.mult, ALU.add))
            for k in (9, 7, 5, 3, 1):
                link(V.tensor_tensor(s_["a"][:, :], s_["a"][:, :], s_["f"][:, :], ALU.mult))
                link(V.tensor_scalar(s_["a"][:, :], s_["a"][:, :], 1.0 / k, None, ALU.add))
            link(V.tensor_scalar(s_["b"][:, :], s_["c"][:, :], SMALL_ATANH, None, ALU.is_lt))
            link(V.tensor_tensor(s_["a"][:, :], s_["a"][:, :], s_["e"][:, :], ALU.subtract))
            link(V.tensor_tensor(s_["a"][:, :], s_["a"][:, :], s_["b"][:, :], ALU.mult))
            link(V.tensor_tensor(s_["e"][:, :], s_["e"][:, :], s_["a"][:, :], ALU.add))
            link(V.tensor_tensor(x_one[:, :, 0:D], xc[:, :, :], bc(s_["e"], D), ALU.mult))
            for i in range(3):
                link(V.tensor_copy(tan_part[:, i, :, :], x_one[:, :, :]))
                if i < 2:
                    link(V.tensor_tensor(x_one[:, :, :], x_one[:, :, :], tan_part[:, i, :, :], ALU.subtract))
            for q in range(6):
                last = V.tensor_copy(tan_stack[:, :, q * K1:(q + 1) * K1], tan_part[:, q % 3, :, :])
            to_tensor(last)
            V.tensor_copy(tan_stack_T.rearrange("p w e -> p (w e)"), acc[0:KS, 0:NW * P]).then_inc(s_tangent, 1)

            def evacuate(w, s, i):
                if later(w):
                    dve.wait_ge(s_tabst[s], 16 * i)
                for c in (1, 3, 5):
                    dve.wait_ge(s_tabps, 8 * w + c + 1)
                    V.tensor_copy(stage[s][:, c * CH:(c + 1) * CH], acc[:, c * BANK:c * BANK + CH]).then_inc(s_ev_v, 1)
                dve.wait_ge(s_tabps, 8 * w + 8)
                V.tensor_copy(loopv[:, bass.ds(w, 1), :].rearrange("p o d -> p (o d)"), misc[:, LAST_TAB:CH])
                V.tensor_copy(stage[s][:, 7 * CH:TAB], misc[:, 0:LAST_TAB]).then_inc(s_ev_v, 1)
            windows(dve, evacuate)
            dve.wait_ge(s_ev_v, 4 * NW)
            link(V.tensor_tensor(na[:, :, :], loopv[:, :, :], loopv[:, :, :], ALU.mult))
            link(V.reduce_sum(s_["a"][:, :], na[:, :, :], AX_X))
            to_act(V.tensor_scalar(s_["b"][:, :], s_["a"][:, :], MIN_NORM, None, ALU.max))
            to_act(V.memset(tick[:, :], 0.0))
            link(V.reciprocal(s_["c"][:, :], s_["c"][:, :]))
            link(V.tensor_tensor(s_["c"][:, :], s_["c"][:, :], s_["d"][:, :], ALU.mult))
            link(V.tensor_tensor(loopv[:, :, :], loopv[:, :, :], bc(s_["c"], D), ALU.mult))
            V.memset(tick[:, :], 0.0).then_inc(s_sumread, 1)

            messages("l2")
            V.tensor_copy(gather_row[:, :], dst_row[:, :]).then_inc(s_index, 1)
            to_tensor(sums_out(4))
            link(V.tensor_tensor(s_["a"][:, :], w_node[:, :], node_sums[:, :, D], ALU.mult))
            link(V.tensor_scalar(s_["a"][:, :], s_["a"][:, :], EPS, None, ALU.add))
            link(V.reciprocal(s_["a"][:, :], s_["a"][:, :]))
            link(V.tensor_tensor(s_["a"][:, :], s_["a"][:, :], w_node[:, :], ALU.mult))
            link(V.tensor_tensor(nb[:, :, :], node_sums[:, :, 0:D], bc(s_["a"], D), ALU.mult))
            link(V.tensor_tensor(na[:, :, :], nb[:, :, :], nb[:, :, :], ALU.mult))
            link(V.reduce_sum(s_["a"][:, :], na[:, :, :], AX_X))
            to_act(V.tensor_scalar(s_["b"][:, :], s_["a"][:, :], MIN_NORM, None, ALU.max))
            link(V.reciprocal(s_["d"][:, :], s_["c"][:, :]))
            link(V.tensor_scalar(s_["d"][:, :], s_["d"][:, :], MAXN, 1.0, ALU.mult, ALU.min))
            link(V.tensor_tensor(nb[:, :, :], nb[:, :, :], bc(s_["d"], D), ALU.mult))
            link(V.tensor_tensor(na[:, :, :], nb[:, :, :], nb[:, :, :], ALU.mult))
            link(V.reduce_sum(s_["a"][:, :], na[:, :, :], AX_X))
            link(V.tensor_tensor(na[:, :, :], loopv[:, :, :], loopv[:, :, :], ALU.mult))
            link(V.reduce_sum(s_["b"][:, :], na[:, :, :], AX_X))
            link(V.tensor_tensor(na[:, :, :], loopv[:, :, :], nb[:, :, :], ALU.mult))
            link(V.reduce_sum(s_["c"][:, :], na[:, :, :], AX_X))
            link(V.tensor_scalar(s_["c"][:, :], s_["c"][:, :], 2 * C, 1.0, ALU.mult, ALU.add))
            link(V.scalar_tensor_tensor(s_["e"][:, :], s_["b"][:, :], C, s_["c"][:, :], ALU.mult, ALU.add))
            link(V.tensor_tensor(s_["f"][:, :], s_["a"][:, :], s_["b"][:, :], ALU.mult))
            link(V.scalar_tensor_tensor(s_["f"][:, :], s_["f"][:, :], C * C, s_["c"][:, :], ALU.mult, ALU.add))
            link(V.tensor_scalar(s_["f"][:, :], s_["f"][:, :], MIN_NORM, None, ALU.max))
            link(V.reciprocal(s_["f"][:, :], s_["f"][:, :]))
            link(V.tensor_scalar(s_["a"][:, :], s_["a"][:, :], -C, 1.0, ALU.mult, ALU.add))
            link(V.tensor_tensor(nb[:, :, :], nb[:, :, :], bc(s_["e"], D), ALU.mult))
            link(V.tensor_tensor(na[:, :, :], loopv[:, :, :], bc(s_["a"], D), ALU.mult))
            link(V.tensor_tensor(nb[:, :, :], nb[:, :, :], na[:, :, :], ALU.add))
            link(V.tensor_tensor(nb[:, :, :], nb[:, :, :], bc(s_["f"], D), ALU.mult))
            link(V.tensor_tensor(nb[:, :, :], nb[:, :, :], xc[:, :, :], ALU.add))
            layer_norm(nb[:, :, :])
            V.memset(tick[:, :], 0.0).then_inc(s_table, 1)
            dve.wait_ge(s_table, 3)
            V.memset(tick[:, :], 0.0).then_inc(s_sumread, 1)

            dve.wait_ge(s_attr8, 16)
            hot_src = hot_small[:, :].rearrange("p (k w) -> p k w", k=G)

            def outer(g, s, i):
                dve.wait_ge(s_landed["l3"][s], 16 * G * (i + 1))
                if later(g):
                    dve.wait_ge(s_trans, g - 1)
                V.tensor_tensor(outer_e[s].rearrange("p (k i j) -> p k i j", i=D, j=A8),
                                rows[:, s, :, :][:, :, :, None].to_broadcast([P, G, D, A8]),
                                attr8_sb[:, at(g), :][:, :, None, :].to_broadcast([P, G, D, A8]), ALU.mult
                                ).then_inc(s_outer, 1)

            def by_src(g, s):
                if not_first(g):
                    dve.wait_ge(s_ready["l3"], 2 * g)
                if later(g):
                    dve.wait_ge(s_used["l3"], 2 * g - 2)
                hot_of(hot_src, NW, src_win[:, at(g)])
                hot_of(hot_lane[:, s, :, :], P, src_lane[:, at(g)]).then_inc(s_step["l3"], 1)
                dve.wait_ge(s_step["l3"], g + 1)
                dve.wait_ge(s_silu, g + 1)
                for q, (k0, k1) in enumerate(SUB):
                    if not_first(g):
                        dve.wait_ge(s_used["l3"], 2 * g - 1 + q)
                    n = k1 - k0
                    V.tensor_tensor(moving[:, q, 0:n * NW * D].rearrange("p (k w d) -> p k w d", w=NW, d=D),
                                    hot_src[:, k0:k1, :][:, :, :, None].to_broadcast([P, n, NW, D]),
                                    msg[:, s, k0:k1, 0:D][:, :, None, :].to_broadcast([P, n, NW, D]), ALU.mult
                                    ).then_inc(s_ready["l3"], 1)

            def last_layer(g, s, i):
                outer(g, s, i)
                if later(g):
                    by_src(g - 2, s)
            pairs(dve, last_layer, peel=4)
            by_src(NG - 2, 0)
            by_src(NG - 1, 1)
            dve.wait_ge(s_summed, 5)

            lin = float(D ** -0.5)
            to_tensor(V.tensor_copy(flat(nb[:, :, :]), acc_src))
            to_tensor(V.tensor_copy(nodeT[0:D, :, :].rearrange("p w e -> p (w e)"), acc[0:D, 0:NW * P]))
            link(V.tensor_scalar(flat(na[:, :, :]), misc[:, 0:NW * D], lin, None, ALU.mult))
            pair_of = moving[:, :, :].rearrange("p s m -> p (s m)")[:, 0:NW * D * D]
            to_tensor(V.tensor_tensor(pair_of.rearrange("p (w i h) -> p w i h", i=D, h=D),
                                      xc[:, :, :, None].to_broadcast([P, NW, D, D]),
                                      na[:, :, None, :].to_broadcast([P, NW, D, D]), ALU.mult))
            to_tensor(V.tensor_copy(big[:, 0:NW * P], acc[:, 0:NW * P]))
            to_tensor(V.tensor_copy(big[:, NW * P:2 * NW * P], acc[:, 0:NW * P]))
            to_act(V.memset(tick[:, :], 0.0))
            to_tensor(V.memset(tick[:, :], 0.0))
            link(V.tensor_scalar(flat(nb[:, :, :]), misc[:, 0:NW * D], lin, None, ALU.mult))
            link(V.scalar_tensor_tensor(nb[:, :, :], xc[:, :, :], 2.0, nb[:, :, :], ALU.mult, ALU.add))
            layer_norm(nb[:, :, :])
            V.memset(tick[:, :], 0.0).then_inc(s_out, 1)

        @block.tensor
        def _(pe):
            M = nc.tensor
            pe.wait_ge(s_topose, 1)
            pe.wait_ge(s_flag, 1)
            narrow = pe.value_load(flag_i[0:1, 0:1], min_val=0, max_val=1)
            turn = [1]
            loads = [0]

            def clear(banks):
                for b in range(banks):
                    M.matmul(acc[:, b * BANK:(b + 1) * BANK], zeros[:, 0:P], zeros[:, :], start=True, stop=True)

            def add(to, lanes, mv):
                return M.matmul(to, lanes, mv, start=False, stop=False, skip_group_check=True)

            def close():
                M.matmul(acc[:, 0:P], zeros[:, 0:P], zeros[:, 0:P], start=False, stop=True,
                         skip_group_check=True).then_inc(s_summed, 1)

            def on_chip(ph, g, s, k):
                n = ON_CHIP[ph]
                if k == 0:
                    pe.wait_ge(s_hotT[ph], g + 1)
                if not isinstance(g, int) or n * g + k >= 1:
                    pe.wait_ge(s_kept[ph], n * g + k)
                for i in range(3):
                    last = M.matmul(misc[:, 0:NW * D], hot_T[s][:, k * P:(k + 1) * P], x_part[i],
                                    start=(i == 0), stop=(i == 2))
                last.then_inc(s_allw[ph], 1)

            def scatter_first():
                def near_group(g, s, i):
                    loads[0] += 1
                    first = [pe.alloc_register(f"first_column_{loads[0]}_{k}") for k in range(RUNS)]
                    pe.load(first, first_off0[0:1, bass.ds(g, 1), :])
                    cols = [pe.snap(r, donate=True, min_val=0, max_val=BANKS_B0 * BANK - 2 * F0) for r in first]
                    pe.wait_ge(s_ready["l0"], g + 1)
                    for k in range(G):
                        last = add(acc[0:BN0, bass.ds(cols[k // RUN], 2 * F0)], hot_lane[:, s, k, 0:BN0],
                                   near0(s)[:, k, :, :].rearrange("p b f -> p (b f)"))
                    last.then_inc(s_used["l0"], 1)

                def wide_group(g, s, i):
                    for k in range(G):
                        pe.wait_ge(s_wready["l0"], G * g + k + 1)
                        mv = wide0((s * G + k) % 2)
                        for b in range(BANKS_B0):
                            last = add(acc_bank[0:BN0, b, 0:BANK_B0 * F0], hot_lane[:, s, k, 0:BN0],
                                       mv[:, b * BANK_B0:(b + 1) * BANK_B0, :].rearrange("p b f -> p (b f)"))
                        last.then_inc(s_wused["l0"], 1)
                clear(BANKS_B0)
                with pe.If(narrow):
                    pairs(pe, near_group)
                with pe.Else():
                    pairs(pe, wide_group)
                close()

            def scatter(ph):
                f = COLUMNS[ph]
                on = ON_CHIP.get(ph, 0)

                def near_group(g, s, rows_of=None):
                    loads[0] += 1
                    first = [pe.alloc_register(f"first_column_{loads[0]}_{k}") for k in range(RUNS)]
                    pe.load(first, first_off[0:1, bass.ds(g, 1), :])
                    cols = [pe.snap(r, donate=True, min_val=0, max_val=7 * BANK - 2 * F) for r in first]
                    pe.wait_ge(s_ready[ph], g + 1)
                    for k in range(G):
                        to = acc[:, bass.ds(cols[k // RUN], 2 * F)].rearrange("p (b f) -> p b f", f=F)
                        last = add(to[:, :, 0:f], hot_lane[:, s, k, :], near(s)[:, k, :, 0:f])
                        if rows_of is not None and k % FEED == FEED - 1 and k // FEED + 1 < on:
                            on_chip(ph, rows_of, s, k // FEED + 1)
                    last.then_inc(s_used[ph], 1)

                def near_step(g, s, i):
                    if not on:
                        near_group(g, s)
                    elif isinstance(g, int) and g == 0:
                        for k in range(on):
                            on_chip(ph, 1, 1, k)
                    elif has_next(g):
                        on_chip(ph, g + 1, 1 - s, 0)
                        near_group(g - 1, 1 - s, rows_of=g + 1)
                    else:
                        near_group(g - 1, 1 - s)
                        near_group(g, s)

                def wide_group(g, s, i):
                    for k in range(on):
                        on_chip(ph, g, s, k)
                    for k in range(G):
                        pe.wait_ge(s_wready[ph], G * g + k + 1)
                        mv = wide((s * G + k) % 2)
                        for b in range(BANKS_B):
                            n = min(BANK_B, NB - b * BANK_B)
                            to = acc_bank[:, b, 0:n * F].rearrange("p (b f) -> p b f", f=F)
                            last = add(to[:, :, 0:f], hot_lane[:, s, k, :], mv[:, b * BANK_B:b * BANK_B + n, 0:f])
                        last.then_inc(s_wused[ph], 1)
                clear(BANKS_B)
                with pe.If(narrow):
                    for k in range(on):
                        on_chip(ph, 0, 0, k)
                    pairs(pe, near_step, tail=2 if on else 0)
                with pe.Else():
                    pairs(pe, wide_group)
                close()

            def to_nodes(to, of, r):
                for b in range(BW):
                    last = M.matmul(to, select[:, r, SHIFT - BN * b:SHIFT - BN * b + P],
                                    of[:, b:NB:BW, :], start=(b == 0), stop=(b == BW - 1))
                return last

            def operand_ready():
                turn[0] += 1
                pe.wait_ge(s_topose, turn[0])

            def transposes(block_of, n):
                for w in range(NW):
                    last = M.transpose(acc[0:n, w * P:(w + 1) * P], block_of(w), ident[:, :])
                last.then_inc(s_posed, 1)

            scatter_first()
            operand_ready()
            for to, c0, c1 in ((misc[:, 0:NW * D], 0, D), (counts_ps, D, F0)):
                for b in range(BW0):
                    last = M.matmul(to, select0[:, SHIFT0 - BN0 * b:SHIFT0 - BN0 * b + P],
                                    sums_0[:, b:NB0:BW0, c0:c1], start=(b == 0), stop=(b == BW0 - 1))
            last.then_inc(s_posed, 1)
            pe.wait_ge(s_sumread, 1)
            pe.wait_ge(s_xpart, 1)
            scatter("l1a")
            pe.wait_ge(s_weights, 14 * 16)
            operand_ready()
            for r in range(R1):
                last = to_nodes(rel_ps(r), totals_b, r)
            last.then_inc(s_posed, 1)
            operand_ready()
            transposes(lambda w: moving[:, 0, w * P:(w + 1) * P], P)
            operand_ready()
            transposes(lambda w: x_one[:, w, :], D + 1)
            operand_ready()
            for w in range(0, NW, 4):
                n = min(4, NW - w)
                h_w = acc[0:H1, w * P:(w + n) * P]
                M.matmul(h_w, w1_sb[:, :], moving[:, 1, w * P:(w + n) * P], start=True, stop=False)
                last = M.matmul(h_w, root1_sb[:, :], nodeT[0:D + 1, w:w + n, :].rearrange("p w e -> p (w e)"),
                                start=False, stop=True)
            last.then_inc(s_posed, 1)
            operand_ready()
            for w in range(NW):
                M.matmul(acc[:, w * P:(w + 1) * P], nodeT[0:H1 + 1, w, :], w2_sb[:, 0:R1 * D], start=True, stop=True)
                last = M.matmul(misc[:, w * D:(w + 1) * D], nodeT[0:H1 + 1, w, :], w2_sb[:, R1 * D:], start=True, stop=True)
            last.then_inc(s_posed, 1)
            operand_ready()
            pe.wait_ge(s_invld, 16)
            for j in range(2):
                last = M.transpose(misc[:, j * NB_HALF:(j + 1) * NB_HALF], inv_T[:, j, :], ident[0:NB_HALF, 0:NB_HALF])
            last.then_inc(s_posed, 1)
            scatter("l1b")
            operand_ready()
            to_nodes(misc[:, 0:NW * D], means_b, R1).then_inc(s_posed, 1)
            operand_ready()
            transposes(lambda w: tan_stack[:, w, :], KS)
            pe.wait_ge(s_wstack, 16 * 9)

            def table(w, s, i):
                pe.wait_ge(s_stat, w + 1)
                for c in range(8):
                    if not_first(w):
                        if c % 2:
                            pe.wait_ge(s_ev_v, 4 * (w - 1) + c // 2 + 1)
                        else:
                            pe.wait_ge(s_ev_a, 4 * (w - 1) + c // 2 + 1)
                    to = misc[:, 0:CH] if c == 7 else acc[:, c * BANK:c * BANK + CH]
                    M.matmul(to, stat[:, s, :], w_high_mid[:, c * CH:(c + 1) * CH], start=True, stop=False)
                    M.matmul(to, stat[0:KX, s, :], w_low[:, c * CH:(c + 1) * CH], start=False, stop=True
                             ).then_inc(s_tabps, 1)
            windows(pe, table)
            pe.wait_ge(s_sumread, 2)
            scatter("l2")
            operand_ready()
            to_nodes(misc[:, 0:NW * F], sums_b, R1).then_inc(s_posed, 1)
            clear(1)

            def transpose_outer(g, s):
                pe.wait_ge(s_outer, g + 1)
                if not_first(g):
                    pe.wait_ge(s_outT, g)
                for k in range(G):
                    last = M.transpose(zt_ps[:, k * P:(k + 1) * P], outer_e[s][:, k * P:(k + 1) * P], ident[:, :])
                last.then_inc(s_trans, 1)

            def message(g, s):
                pe.wait_ge(s_outT, g + 1)
                if later(g):
                    pe.wait_ge(s_silu, g - 1)
                for k in range(G):
                    last = M.matmul(m_ps[s][:, k * D:(k + 1) * D], outer_T[s][:, k, :], wmsg_sb[:, :],
                                    start=True, stop=True)
                last.then_inc(s_mps, 1)

            def add_by_src(g, s):
                for q, (k0, k1) in enumerate(SUB):
                    pe.wait_ge(s_ready["l3"], 2 * g + q + 1)
                    for k in range(k0, k1):
                        last = add(acc_src, hot_lane[:, s, k, :],
                                   moving[:, q, (k - k0) * NW * D:(k - k0 + 1) * NW * D])
                    last.then_inc(s_used["l3"], 1)

            def last_layer(g, s, i):
                transpose_outer(g, s)
                if later(g):
                    add_by_src(g - 2, s)
                message(g, s)
            pairs(pe, last_layer, peel=4)
            add_by_src(NG - 2, 0)
            add_by_src(NG - 1, 1)
            close()

            operand_ready()
            transposes(lambda w: nb[:, w, :], D)
            operand_ready()
            for w in range(NW):
                last = M.matmul(misc[:, w * D:(w + 1) * D], nodeT[0:D, w, :], wmlin_sb[:, :], start=True, stop=True)
            last.then_inc(s_posed, 1)
            operand_ready()
            pairs_flat = moving[:, :, :].rearrange("p s m -> p (s m)")
            transposes(lambda w: pairs_flat[:, w * P:(w + 1) * P], P)
            operand_ready()
            transposes(lambda w: pairs_flat[:, (NW + w) * P:(NW + w + 1) * P], P)
            operand_ready()
            halves = big[:, 0:2 * NW * P].rearrange("p (w h e) -> p w h e", h=2, e=P)
            for w in range(0, NW, 4):
                n = min(4, NW - w)
                for half in range(2):
                    last = M.matmul(acc[0:D, w * P:(w + n) * P].rearrange("p (w e) -> p w e", e=P),
                                    wupd_sb[:, half, :], halves[:, w:w + n, half, :], start=(half == 0), stop=(half == 1))
            last.then_inc(s_posed, 1)
            operand_ready()
            for w in range(NW):
                last = M.matmul(misc[:, w * D:(w + 1) * D], nodeT[0:D, w, :], wulin_sb[:, :], start=True, stop=True)
            last.then_inc(s_posed, 1)


def kernel(x, src, dst, edge_attr_16, edge_attr_8, edge_type_230, edge_type_8, node_vec1, L1_gnn_W1, L1_gnn_root1,
           L1_gnn_b1, L1_gnn_W2, L1_gnn_root2, L1_gnn_b2, L2_gnn_rel_weight, L2_gnn_loop_weight, L2_gnn_rel_emb,
           L3_gnn_W_msg_tp, L3_gnn_W_msg_lin, L3_gnn_W_upd_tp, L3_gnn_W_upd_lin):
    import numpy as np
    import concourse.bacc as bacc
    from concourse.bass_utils import run_bass_kernel_spmd

    def edges(a, fill):
        a = np.asarray(a)
        pad = np.full((P * T - N_EDGES,) + a.shape[1:], fill, a.dtype)
        a = np.concatenate([a, pad]).reshape(T, P, -1)
        return np.ascontiguousarray(a.transpose(1, 0, 2).reshape(P, -1))

    def nodes(a):
        a = np.asarray(a)
        a = np.concatenate([a, np.zeros((P * NW - N_NODES, a.shape[1]), a.dtype)]).reshape(NW, P, -1)
        return np.ascontiguousarray(a.transpose(1, 0, 2).reshape(P, -1))

    past = (N_NODES - 1) | (BN - 1)
    assert past >= N_NODES
    dst_e = edges(dst, past)
    run_first = np.repeat(dst_e[0].reshape(NG, G)[:, ::RUN], RUN, axis=1)[:, :G].reshape(1, T)

    def flat(a):
        a = np.asarray(a)
        return np.concatenate([a, np.full(P * T - N_EDGES, past, a.dtype)]).reshape(P, T)

    relw = np.asarray(L2_gnn_rel_weight)
    arrays = {
        "x": nodes(x), "src_flat": flat(src), "dst": dst_e, "src": edges(src, past), "tile_first": run_first,
        "attr16": edges(edge_attr_16, 0), "attr8": edges(edge_attr_8, 0),
        "rel230": edges(edge_type_230, 0), "rel8": edges(edge_type_8, 0),
        "w1": np.asarray(L1_gnn_W1).reshape(R1 * D, H1), "root1": np.asarray(L1_gnn_root1),
        "b1": np.asarray(L1_gnn_b1).reshape(1, H1),
        "w2": np.ascontiguousarray(np.asarray(L1_gnn_W2).transpose(1, 0, 2).reshape(H1, R1 * D)),
        "root2": np.asarray(L1_gnn_root2), "b2": np.asarray(L1_gnn_b2).reshape(1, D),
        "relw": np.ascontiguousarray(relw.transpose(1, 0, 2).reshape(D, TAB)),
        "loopw": np.asarray(L2_gnn_loop_weight), "relemb": np.asarray(L2_gnn_rel_emb).reshape(1, TAB),
        "wmsg": np.asarray(L3_gnn_W_msg_tp).reshape(P, D), "wmlin": np.asarray(L3_gnn_W_msg_lin),
        "wupd": np.asarray(L3_gnn_W_upd_tp).reshape(2 * P, D), "wulin": np.asarray(L3_gnn_W_upd_lin),
    }
    nc = bacc.Bacc("TRN2", target_bir_lowering=False, num_devices=1)
    args = {k: nc.dram_tensor("in_" + k, a.shape, mybir.dt.from_np(a.dtype), kind="ExternalInput").ap()
            for k, a in arrays.items()}
    out = nc.dram_tensor("out", [P, NW * D], F32, kind="ExternalOutput").ap()
    build(nc, out=out, **args)
    r = run_bass_kernel_spmd(nc, [{"in_" + k: a for k, a in arrays.items()}], core_ids=[0])
    got = np.asarray(r.results[0]["out"]).reshape(P, NW, D).transpose(1, 0, 2).reshape(P * NW, D)
    return np.ascontiguousarray(got[:N_NODES])
```
